# Optimizing a Trainium2 kernel written in Bass

```python
import numpy as np
import jax
import jax.numpy as jnp

def _softmax(x, axis=-1):
    return jax.nn.softmax(x, axis=axis)

def _gelu(x):
    return jax.nn.gelu(x, approximate=True)

def _silu(x):
    return jax.nn.silu(x)

def _sigmoid(x):
    return jax.nn.sigmoid(x)

def _layernorm(x, axis=-1, eps=1e-05):
    m = jnp.mean(x, axis=axis, keepdims=True)
    v = jnp.var(x, axis=axis, keepdims=True)
    return (x - m) / jnp.sqrt(v + eps)

def _scatter_add(tgt, idx, src, axis=0):
    return tgt.at[idx].add(src)

def _segment_sum(src, seg, n):
    return jax.ops.segment_sum(src, seg, n)
kernel_name = 'mk_vit_tower_cls_d1_tok_img1024_r4_7c8c5a'

def setup_inputs(seed: int=0):
    np.random.seed(seed)
    _w = jnp.asarray

    def _rec_inputs():
        import jax
        import jax.numpy as jnp
        _rk = jax.random.key(seed)
        x = 7.22013e-05 + 1.00017 * jax.random.normal(jax.random.fold_in(_rk, 1), (8, 64, 256, 4), jnp.float32)
        cls_tok = 0.02 * jax.random.normal(jax.random.fold_in(_rk, 5), (1, 1, 256), jnp.float32)
        return (x, cls_tok)
    x, cls_tok = _rec_inputs()

    def _L0_tok_setup():
        import jax, jax.numpy as jnp
        import numpy as np
        B, F, L, H, D = (8, 64, 256, 4, 64)
        MODEL = H * F
        WIN = 128

        def _local_mask():
            m = np.ones((L, L), dtype=bool)
            m = np.tril(m, WIN - 1)
            m = np.triu(m, -(WIN - 1))
            return jnp.asarray(m)

        def _flatten(y):
            n = y.shape[0]
            return y.transpose(0, 2, 3, 1).reshape(n, L, -1)
        key = jax.random.key(seed)
        ks = jax.random.split(key, 12)
        s = lambda n: 1.0 / np.sqrt(n)
        xav = np.sqrt(6.0 / (L + L))
        return {'x': jax.random.normal(ks[0], (B, F, L, H), jnp.float32), 'Wq_w': jax.random.normal(ks[1], (D, F), jnp.float32) * s(F), 'Wq_b': jnp.zeros((D,), jnp.float32), 'Wk_w': jax.random.normal(ks[2], (D, F), jnp.float32) * s(F), 'Wk_b': jnp.zeros((D,), jnp.float32), 'Wv_w': jax.random.normal(ks[3], (D, F), jnp.float32) * s(F), 'Wv_b': jnp.zeros((D,), jnp.float32), 'w_bias': jax.random.uniform(ks[4], (L, L), jnp.float32, -xav, xav), 'out_w': jax.random.normal(ks[5], (H * D, MODEL), jnp.float32) * s(H * D), 'out_b': jnp.zeros((MODEL,), jnp.float32), 'ln_g': jnp.ones((MODEL,), jnp.float32), 'ln_b': jnp.zeros((MODEL,), jnp.float32), 'local_mask': _local_mask()}
    _L0_tok_all = _L0_tok_setup()
    _L0_tok_in = {k: v for k, v in _L0_tok_all.items() if k in ('Wq_w', 'Wq_b', 'Wk_w', 'Wk_b', 'Wv_w', 'Wv_b', 'w_bias', 'out_w', 'out_b', 'ln_g', 'ln_b', 'local_mask')}
    del _L0_tok_all

    def _L0_attn_setup():
        import jax, jax.numpy as jnp
        import numpy as np
        HIDDEN = 256
        NHEADS = 16
        HEAD_DIM = HIDDEN // NHEADS
        CONV_K = 4
        EPS = 1e-06

        def _short_conv(x, w):
            K = w.shape[-1]
            L = x.shape[1]
            xp = jnp.pad(x, ((0, 0), (K - 1, 0), (0, 0)))
            y = jnp.zeros_like(x)
            for k in range(K):
                y = y + xp[:, k:k + L, :] * w[:, k]
            return y

        def _l2norm(x):
            n = jnp.sqrt(jnp.sum(x * x, axis=-1, keepdims=True))
            return x / jnp.maximum(n, EPS)

        def _delta_rule(q, k, v, beta):
            b, h, l, dk = q.shape
            dv = v.shape[-1]
            q = q * dk ** (-0.5)
            S0 = jnp.zeros((b, h, dk, dv), dtype=v.dtype)

            def step(S, inp):
                q_t, k_t, v_t, b_t = inp
                v_new = (v_t - jnp.einsum('bhd,bhdm->bhm', k_t, S)) * b_t[..., None]
                S = S + jnp.einsum('bhd,bhm->bhdm', k_t, v_new)
                o_t = jnp.einsum('bhd,bhdm->bhm', q_t, S)
                return (S, o_t)
            ql, kl, vl = (t.transpose(2, 0, 1, 3) for t in (q, k, v))
            bl = beta.transpose(2, 0, 1)
            S, o = jax.lax.scan(step, S0, (ql, kl, vl, bl))
            return (o.transpose(1, 2, 0, 3), S)

        def _reference_tuple_inner(x, Wq, Wk, Wv, Wb, Wo, conv_q, conv_k, conv_v, o_norm_w):
            b, l, _ = x.shape
            q = x @ Wq.T
            k = x @ Wk.T
            v = x @ Wv.T
            beta = jax.nn.sigmoid(x @ Wb.T)
            q = jax.nn.silu(_short_conv(q, conv_q))
            k = jax.nn.silu(_short_conv(k, conv_k))
            v = jax.nn.silu(_short_conv(v, conv_v))

            def to_heads(t):
                return t.reshape(b, l, NHEADS, HEAD_DIM).transpose(0, 2, 1, 3)
            q, k, v = (to_heads(q), to_heads(k), to_heads(v))
            beta = beta.transpose(0, 2, 1)
            q = _l2norm(q)
            k = _l2norm(k)
            o, S = _delta_rule(q, k, v, beta)
            o = o * jax.lax.rsqrt(jnp.mean(o * o, axis=-1, keepdims=True) + EPS) * o_norm_w
            out = o.transpose(0, 2, 1, 3).reshape(b, l, HIDDEN) @ Wo.T
            return (out, S)
        key = jax.random.key(seed)
        ks = jax.random.split(key, 10)
        b, l = (4, 256)
        init = 0.02
        return {'x': jax.random.normal(ks[0], (b, l, HIDDEN), dtype=jnp.float32), 'Wq': jax.random.normal(ks[1], (HIDDEN, HIDDEN), dtype=jnp.float32) * init, 'Wk': jax.random.normal(ks[2], (HIDDEN, HIDDEN), dtype=jnp.float32) * init, 'Wv': jax.random.normal(ks[3], (HIDDEN, HIDDEN), dtype=jnp.float32) * init, 'Wb': jax.random.normal(ks[4], (NHEADS, HIDDEN), dtype=jnp.float32) * init, 'Wo': jax.random.normal(ks[5], (HIDDEN, HIDDEN), dtype=jnp.float32) * init, 'conv_q': jax.random.normal(ks[6], (HIDDEN, CONV_K), dtype=jnp.float32) * 0.3, 'conv_k': jax.random.normal(ks[7], (HIDDEN, CONV_K), dtype=jnp.float32) * 0.3, 'conv_v': jax.random.normal(ks[8], (HIDDEN, CONV_K), dtype=jnp.float32) * 0.3, 'o_norm_w': jnp.ones((HEAD_DIM,), dtype=jnp.float32)}
    _L0_attn_all = _L0_attn_setup()
    _L0_attn_in = {k: v for k, v in _L0_attn_all.items() if k in ('Wq', 'Wk', 'Wv', 'Wb', 'Wo', 'conv_q', 'conv_k', 'conv_v', 'o_norm_w')}
    del _L0_attn_all

    def _L0_ffn_setup():
        import jax, jax.numpy as jnp
        import numpy as np
        B, S, D, F, E, K = (2, 512, 256, 512, 8, 2)
        key = jax.random.key(seed)
        ks = jax.random.split(key, 5)
        scale = 0.02
        return {'x': jax.random.normal(ks[0], (B, S, D), dtype=jnp.float32), 'Wg': jax.random.normal(ks[1], (E, D), dtype=jnp.float32) * scale, 'W1': jax.random.normal(ks[2], (E, F, D), dtype=jnp.float32) * scale, 'W2': jax.random.normal(ks[3], (E, F, D), dtype=jnp.float32) * scale, 'W3': jax.random.normal(ks[4], (E, D, F), dtype=jnp.float32) * scale}
    _L0_ffn_all = _L0_ffn_setup()
    _L0_ffn_in = {k: v for k, v in _L0_ffn_all.items() if k in ('Wg', 'W1', 'W2', 'W3')}
    del _L0_ffn_all
    return {'x': x, 'cls_tok': cls_tok, 'L0_tok_Wq_w': _L0_tok_in['Wq_w'], 'L0_tok_Wq_b': _L0_tok_in['Wq_b'], 'L0_tok_Wk_w': _L0_tok_in['Wk_w'], 'L0_tok_Wk_b': _L0_tok_in['Wk_b'], 'L0_tok_Wv_w': _L0_tok_in['Wv_w'], 'L0_tok_Wv_b': _L0_tok_in['Wv_b'], 'L0_tok_w_bias': _L0_tok_in['w_bias'], 'L0_tok_out_w': _L0_tok_in['out_w'], 'L0_tok_out_b': _L0_tok_in['out_b'], 'L0_tok_ln_g': _L0_tok_in['ln_g'], 'L0_tok_ln_b': _L0_tok_in['ln_b'], 'L0_tok_local_mask': _L0_tok_in['local_mask'], 'L0_attn_Wq': _L0_attn_in['Wq'], 'L0_attn_Wk': _L0_attn_in['Wk'], 'L0_attn_Wv': _L0_attn_in['Wv'], 'L0_attn_Wb': _L0_attn_in['Wb'], 'L0_attn_Wo': _L0_attn_in['Wo'], 'L0_attn_conv_q': _L0_attn_in['conv_q'], 'L0_attn_conv_k': _L0_attn_in['conv_k'], 'L0_attn_conv_v': _L0_attn_in['conv_v'], 'L0_attn_o_norm_w': _L0_attn_in['o_norm_w'], 'L0_ffn_Wg': _L0_ffn_in['Wg'], 'L0_ffn_W1': _L0_ffn_in['W1'], 'L0_ffn_W2': _L0_ffn_in['W2'], 'L0_ffn_W3': _L0_ffn_in['W3']}

def reference(x, cls_tok, L0_tok_Wq_w, L0_tok_Wq_b, L0_tok_Wk_w, L0_tok_Wk_b, L0_tok_Wv_w, L0_tok_Wv_b, L0_tok_w_bias, L0_tok_out_w, L0_tok_out_b, L0_tok_ln_g, L0_tok_ln_b, L0_tok_local_mask, L0_attn_Wq, L0_attn_Wk, L0_attn_Wv, L0_attn_Wb, L0_attn_Wo, L0_attn_conv_q, L0_attn_conv_k, L0_attn_conv_v, L0_attn_o_norm_w, L0_ffn_Wg, L0_ffn_W1, L0_ffn_W2, L0_ffn_W3):
    import jax
    import jax.numpy as jnp

    def _L0_tok_ref(x, Wq_w, Wq_b, Wk_w, Wk_b, Wv_w, Wv_b, w_bias, out_w, out_b, ln_g, ln_b, local_mask):
        import jax, jax.numpy as jnp
        import numpy as np
        B, F, L, H, D = (8, 64, 256, 4, 64)
        MODEL = H * F
        WIN = 128

        def _local_mask():
            m = np.ones((L, L), dtype=bool)
            m = np.tril(m, WIN - 1)
            m = np.triu(m, -(WIN - 1))
            return jnp.asarray(m)

        def _flatten(y):
            n = y.shape[0]
            return y.transpose(0, 2, 3, 1).reshape(n, L, -1)

        def proj(w, b):
            y = jnp.einsum('nclh,dc->ndlh', x, w) + b[None, :, None, None]
            return _flatten(y)
        q = proj(Wq_w, Wq_b)
        k = proj(Wk_w, Wk_b)
        v = proj(Wv_w, Wv_b)
        wb = w_bias * local_mask.astype(w_bias.dtype)
        ew = jnp.exp(wb)
        ek = jnp.exp(k)
        num = jnp.einsum('ts,nsd->ntd', ew, ek * v)
        den = jnp.einsum('ts,nsd->ntd', ew, ek)
        y = jax.nn.sigmoid(q) * num / den
        h = y @ out_w + out_b + _flatten(x)
        mu = jnp.mean(h, axis=-1, keepdims=True)
        var = jnp.mean(jnp.square(h - mu), axis=-1, keepdims=True)
        return (h - mu) * jax.lax.rsqrt(var + 1e-05) * ln_g + ln_b

    def _L0_attn_ref(x, Wq, Wk, Wv, Wb, Wo, conv_q, conv_k, conv_v, o_norm_w):
        import jax, jax.numpy as jnp
        import numpy as np
        HIDDEN = 256
        NHEADS = 16
        HEAD_DIM = HIDDEN // NHEADS
        CONV_K = 4
        EPS = 1e-06

        def _short_conv(x, w):
            K = w.shape[-1]
            L = x.shape[1]
            xp = jnp.pad(x, ((0, 0), (K - 1, 0), (0, 0)))
            y = jnp.zeros_like(x)
            for k in range(K):
                y = y + xp[:, k:k + L, :] * w[:, k]
            return y

        def _l2norm(x):
            n = jnp.sqrt(jnp.sum(x * x, axis=-1, keepdims=True))
            return x / jnp.maximum(n, EPS)

        def _delta_rule(q, k, v, beta):
            b, h, l, dk = q.shape
            dv = v.shape[-1]
            q = q * dk ** (-0.5)
            S0 = jnp.zeros((b, h, dk, dv), dtype=v.dtype)

            def step(S, inp):
                q_t, k_t, v_t, b_t = inp
                v_new = (v_t - jnp.einsum('bhd,bhdm->bhm', k_t, S)) * b_t[..., None]
                S = S + jnp.einsum('bhd,bhm->bhdm', k_t, v_new)
                o_t = jnp.einsum('bhd,bhdm->bhm', q_t, S)
                return (S, o_t)
            ql, kl, vl = (t.transpose(2, 0, 1, 3) for t in (q, k, v))
            bl = beta.transpose(2, 0, 1)
            S, o = jax.lax.scan(step, S0, (ql, kl, vl, bl))
            return (o.transpose(1, 2, 0, 3), S)

        def _reference_tuple_inner(x, Wq, Wk, Wv, Wb, Wo, conv_q, conv_k, conv_v, o_norm_w):
            b, l, _ = x.shape
            q = x @ Wq.T
            k = x @ Wk.T
            v = x @ Wv.T
            beta = jax.nn.sigmoid(x @ Wb.T)
            q = jax.nn.silu(_short_conv(q, conv_q))
            k = jax.nn.silu(_short_conv(k, conv_k))
            v = jax.nn.silu(_short_conv(v, conv_v))

            def to_heads(t):
                return t.reshape(b, l, NHEADS, HEAD_DIM).transpose(0, 2, 1, 3)
            q, k, v = (to_heads(q), to_heads(k), to_heads(v))
            beta = beta.transpose(0, 2, 1)
            q = _l2norm(q)
            k = _l2norm(k)
            o, S = _delta_rule(q, k, v, beta)
            o = o * jax.lax.rsqrt(jnp.mean(o * o, axis=-1, keepdims=True) + EPS) * o_norm_w
            out = o.transpose(0, 2, 1, 3).reshape(b, l, HIDDEN) @ Wo.T
            return (out, S)
        return _reference_tuple_inner(x, Wq, Wk, Wv, Wb, Wo, conv_q, conv_k, conv_v, o_norm_w)[0]

    def _L0_ffn_ref(x, Wg, W1, W2, W3):
        import jax, jax.numpy as jnp
        import numpy as np
        B, S, D, F, E, K = (2, 512, 256, 512, 8, 2)
        k = K
        scores = jnp.einsum('bsd,ed->bse', x, Wg)
        topk_scores, topk_idx = jax.lax.top_k(scores, k)
        topk_probs = jax.nn.softmax(topk_scores, axis=-1)
        h1 = jnp.einsum('bsd,efd->bsef', x, W1)
        h2 = jnp.einsum('bsd,efd->bsef', x, W2)
        hidden = jax.nn.silu(h1) * h2
        expert_out = jnp.einsum('bsef,edf->bsed', hidden, W3)
        onehot = jax.nn.one_hot(topk_idx, scores.shape[-1], dtype=x.dtype)
        gating = jnp.einsum('bsk,bske->bse', topk_probs, onehot)
        return jnp.einsum('bse,bsed->bsd', gating, expert_out)
    h = _L0_tok_ref(x, L0_tok_Wq_w, L0_tok_Wq_b, L0_tok_Wk_w, L0_tok_Wk_b, L0_tok_Wv_w, L0_tok_Wv_b, L0_tok_w_bias, L0_tok_out_w, L0_tok_out_b, L0_tok_ln_g, L0_tok_ln_b, L0_tok_local_mask)
    h = jnp.concatenate([jnp.broadcast_to(cls_tok, (h.shape[0], 1, h.shape[2])), h], axis=1)
    h = h + _L0_attn_ref(_layernorm(h, axis=-1), L0_attn_Wq, L0_attn_Wk, L0_attn_Wv, L0_attn_Wb, L0_attn_Wo, L0_attn_conv_q, L0_attn_conv_k, L0_attn_conv_v, L0_attn_o_norm_w)
    h = h + _L0_ffn_ref(_layernorm(h, axis=-1), L0_ffn_Wg, L0_ffn_W1, L0_ffn_W2, L0_ffn_W3)
    return h

_drawn_inputs = setup_inputs


def setup_inputs(seed=0):
    import zlib

    import numpy as np

    out = dict(_drawn_inputs(seed))
    spreads = {'L0_tok_Wq_b': (0.0, 0.8),
     'L0_tok_Wk_b': (0.0, 0.8),
     'L0_tok_Wv_b': (0.0, 0.1),
     'L0_tok_out_b': (0.0, 0.1),
     'L0_tok_ln_g': (1.0, 0.2),
     'L0_tok_ln_b': (0.0, 0.1),
     'L0_attn_o_norm_w': (1.0, 0.2)}
    factors = {'L0_tok_w_bias': 8.0,
     'L0_ffn_Wg': 4.135,
     'L0_ffn_W1': 3.654,
     'L0_ffn_W2': 3.623,
     'L0_ffn_W3': 3.611}
    for name, (base, spread) in spreads.items():
        noise = np.random.default_rng([zlib.crc32(name.encode()), seed]).standard_normal(out[name].shape)
        drawn = base * np.exp(spread * noise) if base else spread * noise
        out[name] = jnp.asarray(drawn.astype(out[name].dtype))
    for name, factor in factors.items():
        out[name] = (out[name] * factor).astype(out[name].dtype)
    return out
```

```python
from contextlib import ExitStack

import concourse.bass as bass
from concourse import mybir

F32 = mybir.dt.float32
I32 = mybir.dt.int32
U32 = mybir.dt.uint32
U8 = mybir.dt.uint8
ALU = mybir.AluOpType
ACT = mybir.ActivationFunctionType
AX = mybir.AxisListType.X
ds = bass.ds

P = 128
B, F, L, H, D = 8, 64, 256, 4, 64
C = H * F
T = L + 1
NH, HD = 16, C // 16
TAPS = 4
RING = 16
PART = RING // 2
E, FF, TOPK = 8, 512, 2
CJ = C // P
FJ = FF // P
TT = L // P
NTILE = B * TT + 1
PAIRS = B * T * TOPK
NT = (PAIRS + E * (P - 1)) // P
WORK = 5360 + HD * T
ZC = 4
EPS_LN = 1e-5
EPS = 1e-6


class Steps:

    def __init__(self, eng, sem):
        self.eng, self.sem, self.base, self.n = eng, sem, 0, 0

    def mark(self, ins):
        ins.then_inc(self.sem, 1)
        self.n += 1
        return self.base + self.n

    def link(self, ins):
        self.eng.wait_ge(self.sem, self.mark(ins))

    def turn(self, base, i, per):
        self.base, self.n = base + i * per, 0


class Batch:

    def __init__(self, n, half, slot):
        self.n, self.half, self.slot = n, half, slot


def pair(i):
    return Batch(2 * i + 2, i + 1, 0), Batch(2 * i + 3, i + 1, 1), Batch(2 * i + 1, i, 1)


def six(i):
    return [Batch(4 * i + k, 2 * i + k // 2, k % 2) for k in range(3, 9)]


def fixed(n):
    return Batch(n, n // 2, n % 2)


def vit_block(nc, x_ch, x_tok, cls_tok, tWq, tWk, tWv, tbq, tbk, tbv, w_bias, mask, out_w, out_b, ln_g, ln_b,
              aWq, aWk, aWv, aWb, aWo, conv_q, conv_k, conv_v, o_norm, Wg, W1, W2, W3, out):
    with ExitStack() as ctx:
        def sb(name, shape, dt=F32):
            return ctx.enter_context(nc.sbuf_tensor(name, shape, dt))

        def sem(name):
            return ctx.enter_context(nc.semaphore(name))

        expert_in = nc.dram_tensor("expert_in", [NT * P, C], F32).ap()
        expert_out = nc.dram_tensor("expert_out", [NT * P, C], F32).ap()

        ident = sb("ident", [P, P])
        ones = sb("ones", [P, P])
        before = sb("before", [P, P])
        bdq = sb("bdq", [P, P])
        bdkv = sb("bdkv", [P, 2, P])
        neg_bq = sb("neg_bq", [P, 1])
        kv_bias = sb("kv_bias", [P, 2, 2, D])
        ew = sb("ew", [P, 2, L])
        wmask8 = sb("wmask8", [P, 2, L], U8)
        wmask = sb("wmask", [P, 2, L])
        outw = sb("outw", [P, CJ, C])
        outb = sb("outb", [P, C])
        lng = sb("lng", [P, C])
        lnb = sb("lnb", [P, C])
        wqkv = sb("wqkv", [P, 3, CJ, C])
        wb = sb("wb", [P, CJ, NH])
        wo = sb("wo", [P, CJ, C])
        taps = sb("taps", [P, 3, CJ, TAPS])
        onw = sb("onw", [P, 1])
        wg = sb("wg", [P, CJ, E])
        w1 = sb("w1", [P, E, CJ, FF])
        w2 = sb("w2", [P, E, CJ, FF])
        h = sb("h", [P, NTILE, C])
        big = sb("big", [P, NTILE * C])
        x1T = big[:, 0:CJ * B * T].rearrange("p (j b t) -> p j b t", j=CJ, b=B)
        squares = big[:, 0:HD * T].rearrange("p (d t) -> p d t", d=HD)
        nbk = squares
        x2 = big[:, :].rearrange("p (n c) -> p n c", c=C)
        kq = sb("kq", [P, 2, HD, T])
        zeros = kq[:, 1, :, :].rearrange("p d t -> p (d t)")[:, 0:ZC * C]
        w3 = kq[:, :, :, :].rearrange("p w d t -> p (w d t)")[:, 0:E * FJ * C].rearrange(
            "p (e j c) -> p e j c", e=E, j=FJ)
        betaL = sb("betaL", [P, T])
        nbeta = sb("nbeta", [P, T])
        rk = sb("rk", [P, T])
        rq = sb("rq", [P, T])
        sumsq = sb("sumsq", [P, T])
        root = sb("root", [P, T])
        roott = sb("roott", [P, T])
        work = sb("work", [P, WORK])

        def cut(at, shape):
            n = 1
            for s in shape:
                n *= s
            names = "abcd"[:len(shape)]
            v = work[:, at:at + n]
            if len(shape) == 1:
                return v
            return v.rearrange("p (%s) -> p %s" % (" ".join(names), " ".join(names)),
                               **{k: s for k, s in zip(names, shape)})

        xT = cut(0, [2, CJ, L])
        xtok = cut(1024, [2, TT, C])
        kvb = cut(2048, [2, CJ, L])
        ekv = cut(3072, [2, 2, 2 * C])
        ekv = cut(3072, [2, 2, 2, C])
        eq = cut(5120, [CJ, L])
        yT = cut(5632, [2, CJ, L])
        den1 = cut(6656, [CJ, L])
        hs = cut(7168, [TT, C])
        x1 = cut(7680, [2, TT, C])
        x1c = cut(8704, [C])
        pre = cut(0, [3, T + TAPS - 1])
        conv = cut(1024, [3, T])
        act_ = cut(2048, [3, T])
        bet = cut(3072, [2, T])
        vL = cut(WORK - HD * T, [HD, T])
        qS = cut(0, [RING, HD, HD])
        prod = cut(4096, [2, HD, HD + 1])
        outer = cut(4640, [HD, HD])
        S = cut(4896, [HD, HD])
        u = cut(5152, [HD])
        pairs = wqkv[:, 0:2, :, :].rearrange("p w j (m d) -> p (w j m d)", d=HD)[:, 0:PART * HD * 8].rearrange(
            "p (t m d) -> p t m d", t=PART, m=HD)
        fours = wqkv[:, 2, :, :].rearrange("p j c -> p (j c)").rearrange("p (t m d) -> p t m d", t=PART, m=HD)
        eights = outw[:, 0, :].rearrange("p (t m d) -> p t m d", t=PART, m=HD)
        oT = cut(0, [2, CJ, T])
        oTc = cut(1100, [CJ, B])
        x2T = cut(2048, [CJ, TT, P])
        xs = cut(4096, [2, C])
        xsT = cut(4608, [2, C])
        hid = cut(5120, [2, FF])
        sil = cut(6144, [FF])
        hidT = cut(6656, [2, FF])
        ys = cut(7680, [2, C])
        g0 = cut(8192, [2, C])
        g1 = cut(8704, [2, C])
        stats = sb("stats", [P, 2, 2, 6])
        mv = sb("mv", [P, TT, 2])
        rstd = sb("rstd", [P, TT])
        newv = sb("newv", [P, TT])
        newt = sb("newt", [P, TT])
        eps_ln = sb("eps_ln", [P, 1])
        cst = sb("cst", [P, 10])
        scores = sb("scores", [P, NTILE, E])
        top = sb("top", [P, NTILE, 8])
        topi = sb("topi", [P, NTILE, 8], U32)
        topf = sb("topf", [P, NTILE, TOPK])
        valid = sb("valid", [P, NTILE])
        iota_e = sb("iota_e", [P, E])
        iota_t = sb("iota_t", [P, NT])
        hot = sb("hot", [P, TOPK, NTILE, E])
        hots = sb("hots", [P, NTILE, E])
        tot = sb("tot", [P, NTILE + 1, E])
        ntile_f = sb("ntile_f", [P, E])
        ntile_i = sb("ntile_i", [P, E], I32)
        start = sb("start", [P, E + 1])
        place = sb("place", [P, NTILE, E])
        pick = sb("pick", [P, NTILE, E])
        slotf = sb("slotf", [P, TOPK, NTILE])
        slot = sb("slot", [P, TOPK, NTILE], U32)
        gate = sb("gate", [P, TOPK, NTILE])
        gexp = sb("gexp", [P, NTILE])
        cmp = sb("cmp", [P, NT, E])
        etab_f = sb("etab_f", [P, NT])
        etab = sb("etab", [P, NT], I32)

        ps = ctx.enter_context(nc.psum_tensor("ps", [P, 8, 512], F32))
        kvp = [ps[:, n, :].rearrange("p (j c) -> p j c", j=CJ) for n in range(2)]
        qp = ps[:, 2, :].rearrange("p (j l) -> p j l", j=CJ)
        ndp = [ps[:, 3 + n, :].rearrange("p (w l) -> p w l", w=2) for n in range(2)]
        outp = ps[:, 5, :].rearrange("p (t c) -> p t c", t=TT)
        trp = ps[:, 6, :].rearrange("p (j t) -> p j t", j=CJ)
        clp = ps[:, 7, 0:CJ * B].rearrange("p (j b) -> p j b", j=CJ)

        ld_small = sem("ld_small")
        ld_attn = sem("ld_attn")
        ld_ffn = sem("ld_ffn")
        ld_down = sem("ld_down")
        zeroed = sem("zeroed")
        x_loaded = [sem(f"x_loaded{s}") for s in range(2)]
        pool_const = sem("pool_const")
        blocks0 = sem("blocks0")
        ew_ready = sem("ew_ready")
        wm_ready = sem("wm_ready")
        xb_ready = sem("xb_ready")
        kv_ready = sem("kv_ready")
        q_ready = sem("q_ready")
        kvb_ready = sem("kvb_ready")
        ek_ready = sem("ek_ready")
        ekv_ready = sem("ekv_ready")
        eq_ready = sem("eq_ready")
        nd_ready = sem("nd_ready")
        y_ready = sem("y_ready")
        h_ready = sem("h_ready")
        h_taken = sem("h_taken")
        x1_ready = sem("x1_ready")
        tr_ready = sem("tr_ready")
        x1T_ready = sem("x1T_ready")
        c_ready = sem("c_ready")
        qkv_ready = sem("qkv_ready")
        pre_ready = sem("pre_ready")
        pad_ready = sem("pad_ready")
        conv_ready = sem("conv_ready")
        act_ready = sem("act_ready")
        bet_ready = sem("bet_ready")
        bet_copied = sem("bet_copied")
        relay = [sem(f"relay{s}") for s in range(3)]
        brelay = [sem(f"brelay{s}") for s in range(2)]
        sq_ready = sem("sq_ready")
        norm_step = sem("norm_step")
        sum_ready = sem("sum_ready")
        root_near = sem("root_near")
        root_ready = sem("root_ready")
        near_step = sem("near_step")
        near_ready = sem("near_ready")
        var_ready = sem("var_ready")
        rstd_ready = sem("rstd_ready")
        beta_exp = sem("beta_exp")
        beta_ready = sem("beta_ready")
        v_ready = sem("v_ready")
        scan_ready = sem("scan_ready")
        scan_step = sem("scan_step")
        bv_put = sem("bv_put")
        q_read = sem("q_read")
        summed = sem("summed")
        o_sq = sem("o_sq")
        o_done = sem("o_done")
        o_ready = sem("o_ready")
        wo_ready = sem("wo_ready")
        oT_loaded = [sem(f"oT_loaded{s}") for s in range(2)]
        oc_ready = sem("oc_ready")
        p_ready = sem("p_ready")
        x2_ready = sem("x2_ready")
        t2_ready = sem("t2_ready")
        x2T_ready = sem("x2T_ready")
        sc_ready = sem("sc_ready")
        sc_taken = sem("sc_taken")
        hot_ready = sem("hot_ready")
        rank_ready = sem("rank_ready")
        gd_ready = sem("gd_ready")
        ge_ready = sem("ge_ready")
        slot_ready = sem("slot_ready")
        etab_ready = sem("etab_ready")
        scattered = sem("scattered")
        xs_loaded = [sem(f"xs_loaded{s}") for s in range(2)]
        xst_ready = sem("xst_ready")
        xsT_ready = sem("xsT_ready")
        up_ready = sem("up_ready")
        gt_ready = sem("gt_ready")
        sil_ready = sem("sil_ready")
        hid_ready = sem("hid_ready")
        ht_ready = sem("ht_ready")
        hidT_ready = sem("hidT_ready")
        y2_ready = sem("y2_ready")
        ys_ready = sem("ys_ready")
        ys_stored = [sem(f"ys_stored{s}") for s in range(2)]
        gathered = [sem(f"gathered{s}") for s in range(2)]
        fin_ready = sem("fin_ready")
        stored = sem("stored")
        dve_step = sem("dve_step")
        act_step = sem("act_step")
        pool_step = sem("pool_step")

        N_SMALL, N_ATTN, N_FFN = 0, 0, 0
        small_loads = [
            (bdq[0:F, 0:D], tWq), (bdq[F:P, D:P], tWq),
            (bdkv[0:F, 0, 0:D], tWk), (bdkv[F:P, 0, D:P], tWk),
            (bdkv[0:F, 1, 0:D], tWv), (bdkv[F:P, 1, D:P], tWv)]
        plain_loads = [
            (neg_bq[0:D, :], tbq), (neg_bq[D:P, :], tbq),
            (ew[:, :, :], w_bias.rearrange("(a p) t -> p a t", p=P)),
            (wmask8[:, :, :], mask.rearrange("(a p) t -> p a t", p=P)),
            (outw[:, :, :], out_w.rearrange("(a p) t -> p a t", p=P)),
            (outb[:, :], out_b.partition_broadcast(P)), (lng[:, :], ln_g.partition_broadcast(P)),
            (lnb[:, :], ln_b.partition_broadcast(P)),
            (h[0:B, NTILE - 1, :], cls_tok.partition_broadcast(B))]
        for r in range(2):
            plain_loads += [(kv_bias[:, 0, r, :], tbk.partition_broadcast(P)),
                            (kv_bias[:, 1, r, :], tbv.partition_broadcast(P))]
        attn_loads = [(wb[:, :, :], aWb.rearrange("(a p) t -> p a t", p=P)),
                      (wo[:, :, :], aWo.rearrange("(a p) t -> p a t", p=P)),
                      (wg[:, :, :], Wg.rearrange("(a p) t -> p a t", p=P))]
        for n, (w, c) in enumerate(((aWq, conv_q), (aWk, conv_k), (aWv, conv_v))):
            attn_loads += [(wqkv[:, n, :, :], w.rearrange("(a p) t -> p a t", p=P)),
                           (taps[:, n, :, :], c.rearrange("(a p) t -> p a t", p=P))]
        for r in range(P // HD):
            attn_loads.append((onw[r * HD:(r + 1) * HD, :], o_norm))
        N_SMALL, N_ATTN = 16 * (len(small_loads) + len(plain_loads)), 16 * len(attn_loads)
        ffn_loads = []
        for e in range(E):
            ffn_loads += [(w1[:, e, :, :], W1[e].rearrange("(a p) f -> p a f", p=P)),
                          (w2[:, e, :, :], W2[e].rearrange("(a p) f -> p a f", p=P))]
        N_FFN = 16 * len(ffn_loads)

        def ge(eng, s, v):
            if not (isinstance(v, int) and v <= 0):
                eng.wait_ge(s, v)

        def apart(eng, s, v):
            if not isinstance(v, int):
                v = eng.to_reg(v)
                eng.wait_ge(ld_small, N_SMALL)
            eng.wait_ge(s, v)

        block = ctx.enter_context(nc.Block())

        @block.sync
        def _(sp):
            def load_x(b):
                sp.dma_start(xT[:, b.slot, :, :], x_ch[ds(b.n, 1), :, :].rearrange("o (a p) l -> p (o a) l", p=P)
                             ).then_inc(x_loaded[b.slot], 16)
                sp.dma_start(xtok[:, b.slot, :, :], x_tok[ds(b.n, 1), :, :].rearrange("o (a p) c -> p (o a) c", p=P)
                             ).then_inc(x_loaded[b.slot], 16)

            load_x(fixed(0))
            for dst, src in plain_loads:
                sp.dma_start(dst, src).then_inc(ld_small, 16)
            sp.wait_ge(blocks0, 2)
            for dst, src in small_loads:
                sp.dma_start(dst, src).then_inc(ld_small, 16)
            load_x(fixed(1))
            for dst, src in attn_loads:
                sp.dma_start(dst, src).then_inc(ld_attn, 16)

            def reload_x(b):
                sp.wait_ge(q_ready, b.n - 1)
                sp.wait_ge(h_taken, b.n - 1)
                load_x(b)

            with sp.Fori(0, (B - 2) // 2) as i:
                for b in pair(i)[:2]:
                    reload_x(b)
            sp.wait_ge(zeroed, 16 * (NT // ZC))
            for b in range(B):
                for n in range(6):
                    w, m = n // 2, n % 2
                    at = b * NH + m * (P // HD)
                    dst = vL[at:at + P // HD, :, :] if w == 2 else kq[at:at + P // HD, 1 - w, :, :]
                    sp.wait_ge(act_ready, 6 * b + n + 1)
                    sp.dma_start(dst, act_[:, n % 3, :]).then_inc(relay[n % 3], 16)
                sp.wait_ge(bet_copied, b + 1)
                sp.dma_start(betaL[b * NH:(b + 1) * NH, :], bet[0:NH, b % 2, :]).then_inc(brelay[b % 2], 16)
            for b in range(B):
                if b == 0:
                    sp.wait_ge(o_ready, 1)
                if b >= 2:
                    sp.wait_ge(p_ready, b - 1)
                    sp.wait_ge(oc_ready, b - 1)
                for m in range(CJ):
                    at = b * NH + m * (P // HD)
                    sp.dma_start(oT[:, b % 2, m, :], kq[at:at + P // HD, 1, :, :]).then_inc(oT_loaded[b % 2], 16)
            for s in range(2):
                sp.wait_ge(oT_loaded[s], 32 * (B // 2))
            for e in range(E):
                sp.dma_start(w3[:, e, :, :], W3[e].rearrange("(a p) c -> p a c", p=P)).then_inc(ld_down, 16)
            sp.wait_ge(scattered, 16 * 2 * NTILE)

            def load_tile(j):
                sp.dma_start(xs[:, j.slot, :], expert_in[ds(P * j.n, P), :]).then_inc(xs_loaded[j.slot], 16)

            load_tile(fixed(0))
            load_tile(fixed(1))

            def turn(j):
                sp.wait_ge(xst_ready, j.n - 1)
                load_tile(j)
                store_tile(j, 2)

            def store_tile(j, back):
                n = j.n - back
                sp.wait_ge(ys_ready, n + 1)
                sp.dma_start(expert_out[ds(P * n, P), :], ys[:, j.slot, :]).then_inc(ys_stored[j.slot], 16)

            with sp.Fori(0, (NT - 2) // 2) as i:
                for j in pair(i)[:2]:
                    turn(j)
            store_tile(fixed(NT - 2), 0)
            store_tile(fixed(NT - 1), 0)
            for n in range(NTILE):
                sp.wait_ge(fin_ready, n + 1)
                if n < NTILE - 1:
                    b, t = n // TT, n % TT
                    sp.dma_start(out[b, 1 + t * P:1 + (t + 1) * P, :], h[:, n, :]).then_inc(stored, 16)
                else:
                    sp.dma_start(out[:, 0, :], h[0:B, n, :]).then_inc(stored, 16)
            sp.wait_ge(stored, 16 * NTILE)

        @block.gpsimd
        def _(pool):
            st = Steps(pool, pool_step)
            nc.gpsimd.memset(bdq[:, :], 0.0).then_inc(blocks0, 1)
            nc.gpsimd.memset(bdkv[:, :, :], 0.0).then_inc(blocks0, 1)
            nc.gpsimd.memset(eps_ln[:, :], EPS_LN).then_inc(pool_const, 1)
            nc.gpsimd.memset(ones[:, :], 1.0).then_inc(pool_const, 1)
            nc.gpsimd.memset(zeros, 0.0).then_inc(pool_const, 1)
            st.link(nc.gpsimd.memset(ident[:, :], 0.0))
            nc.gpsimd.affine_select(out=ident[:, :], in_=ident[:, :], compare_op=ALU.not_equal, fill=1.0,
                                    base=0, pattern=[[-1, P]], channel_multiplier=1).then_inc(pool_const, 1)
            st.link(nc.gpsimd.memset(before[:, :], 1.0))
            nc.gpsimd.affine_select(out=before[:, :], in_=before[:, :], compare_op=ALU.is_gt, fill=0.0,
                                    base=0, pattern=[[1, P]], channel_multiplier=-1).then_inc(pool_const, 1)
            st.link(nc.gpsimd.memset(valid[:, :], 1.0))
            nc.gpsimd.affine_select(out=valid[:, :], in_=valid[:, :], compare_op=ALU.is_gt, fill=0.0,
                                    base=B + P * (NTILE - 1), pattern=[[-P, NTILE]], channel_multiplier=-1
                                    ).then_inc(pool_const, 1)
            nc.gpsimd.iota(iota_e[:, :], pattern=[[1, E]], base=0, channel_multiplier=0,
                           allow_small_or_imprecise_dtypes=True).then_inc(pool_const, 1)
            nc.gpsimd.iota(iota_t[:, :], pattern=[[1, NT]], base=0, channel_multiplier=0,
                           allow_small_or_imprecise_dtypes=True).then_inc(pool_const, 1)
            pool.wait_ge(pool_const, 3)
            for n in range(NT // ZC):
                pool.dma_start(expert_in[n * ZC * P:(n + 1) * ZC * P, :].rearrange("(p r) c -> p (r c)", p=P),
                               zeros).then_inc(zeroed, 16)
            for dst, src in ffn_loads:
                pool.dma_start(dst, src).then_inc(ld_ffn, 16)

            def newton(y, v, t, ready):
                st.link(nc.gpsimd.tensor_tensor(t, y, y, ALU.mult))
                step = st.mark(nc.gpsimd.tensor_tensor(t, v, t, ALU.mult))
                apart(pool, pool_step, step)
                st.link(nc.gpsimd.tensor_scalar(t, t, -0.5, 1.5, ALU.mult, ALU.add))
                nc.gpsimd.tensor_tensor(y, y, t, ALU.mult).then_inc(ready, 1)

            def rsqrt(number, n=TT, rows=P):
                apart(pool, var_ready, number + 1)
                ve = newv[0:rows, 0:n]
                st.link(nc.gpsimd.tensor_scalar(ve, mv[0:rows, 0:n, 1], EPS_LN, None, ALU.add))
                pool.wait_ge(near_ready, number + 1)
                newton(rstd[0:rows, 0:n], ve, newt[0:rows, 0:n], rstd_ready)

            def mix(b):
                pool.wait_ge(x_loaded[b.slot], 32 * b.half + 32)
                nc.gpsimd.tensor_tensor(xtok[:, b.slot, :, :], xtok[:, b.slot, :, :],
                                        outb[:, :].unsqueeze(1).to_broadcast([P, TT, C]),
                                        ALU.add).then_inc(xb_ready, 1)
                for lt in range(2):
                    pool.wait_ge(ek_ready, 2 * b.n + (lt + 1))
                    nc.gpsimd.tensor_tensor(
                        ekv[:, b.slot, lt, 0, :].rearrange("p (j c) -> p j c", j=CJ),
                        ekv[:, b.slot, lt, 1, :].rearrange("p (j c) -> p j c", j=CJ),
                        kvb[:, lt, :, P:2 * P], ALU.mult).then_inc(ekv_ready, 1)

            def turn(b):
                mix(b)
                for k in (-1, 0):
                    rsqrt(2 * b.n + k)

            pool.wait_ge(ld_small, N_SMALL)
            rsqrt(0, 1, B)
            mix(fixed(0))
            turn(fixed(1))
            base = st.n
            with pool.Fori(0, (B - 2) // 2) as i:
                st.turn(base, i, 16)
                for b in pair(i)[:2]:
                    turn(b)
                assert st.n == 16
            st.base, st.n = base + 8 * (B - 2), 0
            rsqrt(2 * B - 1)
            rsqrt(2 * B)
            pool.wait_ge(beta_ready, 1)
            for s in range(3):
                pool.wait_ge(relay[s], 16 * 2 * B)
            nc.gpsimd.tensor_tensor(vL, vL, betaL[:, :].unsqueeze(1).to_broadcast([P, HD, T]),
                                    ALU.mult).then_inc(v_ready, 1)
            for n in range(2):
                pool.wait_ge(root_near, n + 1)
                newton(root[:, :], sumsq[:, :], roott[:, :], root_ready)

            G = nc.gpsimd.tensor_tensor

            def read_S(t, n):
                apart(pool, scan_step, 8 * t + 8)
                q_t = kq[:, 1, :, ds(t, 1)].rearrange("p d o -> p (o d)")
                G(qS[:, n % RING, :, :], S, q_t.unsqueeze(1).to_broadcast([P, HD, HD]), ALU.mult).then_inc(q_read, 1)

            def sum_piece(t, n):
                at = (n + PART) % RING // PART * PART
                k = n % PART
                if k == 0:
                    pool.wait_ge(q_read, t)
                elif k < PART - 1:
                    pool.wait_ge(summed, t - PART)
                else:
                    apart(pool, summed, t - PART)
                if k < 4:
                    x, y = slice(at + 2 * k, at + 2 * k + 2), slice(2 * k, 2 * k + 2)
                    last = G(pairs[:, y], qS[:, x, :, 0:8], qS[:, x, :, 8:16], ALU.add)
                elif k < 6:
                    y = slice(4 * k - 16, 4 * k - 12)
                    last = G(fours[:, y], pairs[:, y, :, 0:4], pairs[:, y, :, 4:8], ALU.add)
                elif k == 6:
                    last = G(eights, fours[:, :, :, 0:2], fours[:, :, :, 2:4], ALU.add)
                else:
                    o = kq[:, 1, :, ds(t - (2 * PART - 1), PART)].rearrange("p m t -> p t m")
                    last = G(o, eights[:, :, :, 0], eights[:, :, :, 1], ALU.add)
                last.then_inc(summed, 1)

            for t in range(RING):
                read_S(t, t)
                if t >= PART:
                    sum_piece(t, t)
            with pool.Fori(0, T // RING - 1) as i:
                for n in range(RING):
                    read_S(i * RING + (n + RING), n)
                    sum_piece(i * RING + (n + RING), n)
            read_S(T - 1, 0)
            for k in range(PART):
                sum_piece(T - 1 + k, k)
            pool.wait_ge(q_read, T)
            pool.wait_ge(summed, T - 1)
            st.link(G(pairs[:, 0], qS[:, 0, :, 0:8], qS[:, 0, :, 8:16], ALU.add))
            st.link(G(fours[:, 0], pairs[:, 0, :, 0:4], pairs[:, 0, :, 4:8], ALU.add))
            st.link(G(eights[:, 0], fours[:, 0, :, 0:2], fours[:, 0, :, 2:4], ALU.add))
            G(kq[:, 1, :, T - 1], eights[:, 0, :, 0], eights[:, 0, :, 1], ALU.add).then_inc(o_done, 1)
            pool.wait_ge(root_near, 3)
            newton(root[:, :], sumsq[:, :], roott[:, :], root_ready)
            for b in range(B + 1):
                if b < B:
                    pool.wait_ge(oT_loaded[b % 2], 32 * (b // 2 + 1))
                    nc.gpsimd.tensor_copy(oTc[:, :, b], oT[:, b % 2, :, 0]).then_inc(oc_ready, 1)
                if b:
                    rsqrt(2 * B + b)
            rsqrt(3 * B + 1, 1, B)
            pool.wait_ge(zeroed, 16 * (NT // ZC))
            pool.wait_ge(slot_ready, 1)
            for n in range(NTILE):
                rows = P if n < NTILE - 1 else B
                for k in range(TOPK):
                    nc.gpsimd.indirect_dma_start(
                        out=expert_in, out_offset=bass.IndirectOffsetOnAxis(ap=slot[0:rows, k, n:n + 1], axis=0),
                        in_=x2[0:rows, n, :], in_offset=None).then_inc(scattered, 16)
            for s in range(2):
                pool.wait_ge(ys_stored[s], 16 * (NT // 2))
            for n in range(NTILE):
                rows = P if n < NTILE - 1 else B
                if n >= 2:
                    pool.wait_ge(fin_ready, n - 1)
                for k, g in ((0, g0), (1, g1)):
                    nc.gpsimd.indirect_dma_start(
                        out=g[0:rows, n % 2, :], out_offset=None, in_=expert_out,
                        in_offset=bass.IndirectOffsetOnAxis(ap=slot[0:rows, k, n:n + 1], axis=0)
                    ).then_inc(gathered[n % 2], 16)

        @block.scalar
        def _(act):
            def near_rsqrt(number, n=TT, rows=P):
                act.wait_ge(var_ready, number + 1)
                nc.scalar.activation(rstd[0:rows, 0:n], mv[0:rows, 0:n, 1], ACT.Ln, bias=eps_ln[0:rows, 0:1]
                                     ).then_inc(near_step, 1)
                act.wait_ge(near_step, number + 1)
                nc.scalar.activation(rstd[0:rows, 0:n], rstd[0:rows, 0:n], ACT.Exp, scale=-0.5
                                     ).then_inc(near_ready, 1)

            def near_root(n):
                act.wait_ge(norm_step, n + 1)
                nc.scalar.activation(root[:, :], sumsq[:, :], ACT.Ln).then_inc(act_step, 1)
                act.wait_ge(act_step, n + 2)
                nc.scalar.activation(root[:, :], root[:, :], ACT.Exp, scale=-0.5).then_inc(root_near, 1)

            act.wait_ge(ld_small, N_SMALL)
            act.wait_ge(wm_ready, 1)
            nc.scalar.activation(ew[:, :, :], ew[:, :, :], ACT.Exp).then_inc(ew_ready, 1)
            nc.scalar.mul(neg_bq[:, :], neg_bq[:, :], -1.0).then_inc(act_step, 1)
            act.wait_ge(act_step, 1)
            act.wait_ge(pool_const, 1)
            near_rsqrt(0, 1, B)
            act.wait_ge(c_ready, 2)
            nc.scalar.copy(x1T[:, :, :, 0], clp).then_inc(x1T_ready, 1)

            def mix_front(b):
                for lt in range(2):
                    act.wait_ge(kvb_ready, 2 * b.n + (lt + 1))
                    ge(act, nd_ready, 2 * b.n - 2)
                    nc.scalar.activation(ekv[:, b.slot, lt, 1, :].rearrange("p (j c) -> p j c", j=CJ),
                                         kvb[:, lt, :, 0:P], ACT.Exp).then_inc(ek_ready, 1)
                act.wait_ge(q_ready, b.n + 1)
                ge(act, y_ready, b.n)
                nc.scalar.activation(eq[:, :, :], qp, ACT.Exp, bias=neg_bq[:, 0:1], scale=-1.0).then_inc(eq_ready, 1)

            def mix_back(b):
                act.wait_ge(tr_ready, b.n + 1)
                nc.scalar.copy(x1T[:, :, ds(b.n, 1), 1:T].rearrange("p j o t -> p j (o t)"), trp
                               ).then_inc(x1T_ready, 1)

            def norms(b):
                near_rsqrt(2 * b.n + 1)
                near_rsqrt(2 * b.n + 2)

            def turn(b, prev):
                mix_front(b)
                norms(prev)
                mix_back(prev)

            mix_front(fixed(0))
            turn(fixed(1), fixed(0))
            with act.Fori(0, (B - 2) // 2) as i:
                one, two, prev = pair(i)
                turn(one, prev)
                turn(two, one)
            norms(fixed(7))
            mix_back(fixed(7))

            def proj(b, first):
                for n in range(7):
                    if n < 6:
                        act.wait_ge(qkv_ready, 6 * b.n + (n + 1))
                        if not (first and n < 3):
                            act.wait_ge(conv_ready, 6 * b.n + (n - 2))
                        nc.scalar.copy(pre[:, n % 3, TAPS - 1:], ps[:, n, 0:T]).then_inc(pre_ready, 1)
                    if n >= 1:
                        m = n - 1
                        act.wait_ge(conv_ready, 6 * b.n + (m + 1))
                        if not (first and m < 3):
                            act.wait_ge(relay[m % 3], 32 * b.n + 16 * (m // 3))
                        nc.scalar.activation(act_[:, m % 3, :], conv[:, m % 3, :], ACT.Silu).then_inc(act_ready, 1)
                act.wait_ge(bet_ready, b.n + 1)
                if not first:
                    ge(act, brelay[b.slot], 16 * b.half)
                nc.scalar.copy(bet[0:NH, b.slot, :], ps[0:NH, 7, 0:T]).then_inc(bet_copied, 1)

            act.wait_ge(pad_ready, 1)
            proj(fixed(0), True)
            proj(fixed(1), False)
            with act.Fori(0, (B - 2) // 2) as i:
                for b in pair(i)[:2]:
                    proj(b, False)
            for s in range(2):
                act.wait_ge(brelay[s], 16 * (B // 2))
            nc.scalar.activation(betaL[:, :], betaL[:, :], ACT.Exp, scale=-1.0).then_inc(beta_exp, 1)
            for s in range(3):
                act.wait_ge(relay[s], 16 * 2 * B)
            nc.scalar.activation(squares, kq[:, 0, :, :], ACT.Square).then_inc(sq_ready, 1)
            near_root(0)
            nc.scalar.activation(squares, kq[:, 1, :, :], ACT.Square).then_inc(sq_ready, 1)
            near_root(1)
            act.wait_ge(v_ready, 1)

            def put_v(t, n):
                ge(act, scan_step, 8 * t - 12 if n >= 2 else 0)
                nc.scalar.copy(prod[:, n % 2, :, HD:HD + 1], vL[:, :, ds(t, 1)]).then_inc(bv_put, 1)

            put_v(0, 0)
            put_v(1, 1)
            with act.Fori(0, (T - 2) // 2) as i:
                for n in (2, 3):
                    put_v(i * 2 + n, n)
            put_v(T - 1, 2)
            act.wait_ge(o_done, 1)
            nc.scalar.activation(squares, kq[:, 1, :, :], ACT.Square).then_inc(o_sq, 1)
            near_root(2)
            near_rsqrt(2 * B + 1)
            for n in range(B + 1):
                if n < B:
                    near_rsqrt(2 * B + 2 + n, *((TT, P) if n < B - 1 else (1, B)))
                act.wait_ge(t2_ready, n + 1)
                ge(act, sc_ready, n)
                rows = P if n < B else B
                w = TT if n < B else 1
                nc.scalar.copy(x2T[:, :, 0:w, 0:rows],
                               ps[:, 2 + n % 2, :].rearrange("p (j t r) -> p j t r", j=CJ, t=TT)[:, :, 0:w, 0:rows]
                               ).then_inc(x2T_ready, 1)
            act.wait_ge(gd_ready, 1)
            nc.scalar.activation(gexp[:, :], gexp[:, :], ACT.Exp).then_inc(ge_ready, 1)

            def transposed_in(j):
                act.wait_ge(xst_ready, j.n + 1)
                ge(act, gt_ready, j.n - 1)
                nc.scalar.copy(xsT[:, j.slot, :], ps[:, 4, 0:C]).then_inc(xsT_ready, 1)

            def silu(j):
                act.wait_ge(up_ready, j.n + 1)
                ge(act, hid_ready, j.n)
                nc.scalar.activation(sil, ps[:, j.slot, :], ACT.Silu).then_inc(sil_ready, 1)

            def transposed_hidden(j):
                act.wait_ge(ht_ready, j.n + 1)
                ge(act, y2_ready, j.n - 1)
                nc.scalar.copy(hidT[:, j.slot, :], ps[:, 5, :]).then_inc(hidT_ready, 1)

            def result(j):
                act.wait_ge(y2_ready, j.n + 1)
                ge(act, ys_stored[j.slot], 16 * j.half)
                nc.scalar.copy(ys[:, j.slot, :], ps[:, 6, 0:C]).then_inc(ys_ready, 1)

            def turn(j, last, coming):
                silu(j)
                if last is not None:
                    transposed_hidden(last)
                if coming is not None:
                    transposed_in(coming)
                if last is not None:
                    result(last)

            transposed_in(fixed(0))
            turn(fixed(0), None, fixed(1))
            for n in range(1, 4):
                turn(fixed(n), fixed(n - 1), fixed(n + 1))
            with act.Fori(0, (NT - 8) // 4) as i:
                tiles = six(i)
                for k in range(1, 5):
                    turn(tiles[k], tiles[k - 1], tiles[k + 1])
            for n in range(NT - 4, NT):
                turn(fixed(n), fixed(n - 1), fixed(n + 1) if n < NT - 1 else None)
            transposed_hidden(fixed(NT - 1))
            result(fixed(NT - 1))

        @block.vector
        def _(dve):
            st = Steps(dve, dve_step)
            V = nc.vector

            def layer_norm(number, dst, src, n, rows=P):
                for t in range(n):
                    last = st.mark(V.bn_stats(stats[0:rows, 0, t, :], src(t)))
                apart(dve, dve_step, last)
                for t in range(n):
                    last = V.bn_aggr(mv[0:rows, t, :], stats[0:rows, 0, t, :])
                    if t < n - 1:
                        st.mark(last)
                last.then_inc(var_ready, 1)
                dve.wait_ge(rstd_ready, number + 1)
                for t in range(n):
                    last = V.tensor_scalar(dst(t), src(t), mv[0:rows, t, 0:1], rstd[0:rows, t:t + 1],
                                           ALU.subtract, ALU.mult)
                return last

            dve.wait_ge(ld_small, N_SMALL)
            st.link(V.tensor_copy(wmask[:, :, :], wmask8[:, :, :]))
            V.tensor_tensor(ew[:, :, :], ew[:, :, :], wmask[:, :, :], ALU.mult).then_inc(wm_ready, 1)
            layer_norm(0, lambda t: x1c[0:B, :], lambda t: h[0:B, NTILE - 1, :], 1, B).then_inc(c_ready, 1)

            def keys_values(b):
                for lt in range(2):
                    dve.wait_ge(kv_ready, 2 * b.n + (lt + 1))
                    ge(dve, ekv_ready, 2 * b.n + (lt - 1))
                    V.tensor_tensor(kvb[:, lt, :, :], kvp[lt],
                                    kv_bias[:, :, :, :].rearrange("p w r d -> p (w r d)").unsqueeze(1)
                                    .to_broadcast([P, CJ, 2 * P]), ALU.add).then_inc(kvb_ready, 1)

            def mixed(b):
                dve.wait_ge(eq_ready, b.n + 1)
                ge(dve, h_ready, b.n - 1)
                for j in range(CJ):
                    dve.wait_ge(nd_ready, 2 * b.n + (j + 1))
                    last = st.mark(V.scalar_tensor_tensor(out=den1[:, j, :], in0=eq[:, j, :], scalar=1.0,
                                                          in1=ndp[j][:, 1, :], op0=ALU.add, op1=ALU.mult))
                dve.wait_ge(dve_step, last)
                st.link(V.reciprocal(den1[:, :, :], den1[:, :, :]))
                for j in range(CJ):
                    last = V.tensor_tensor(yT[:, b.slot, j, :], ndp[j][:, 0, :], den1[:, j, :], ALU.mult)
                    if j == 0:
                        st.mark(last)
                last.then_inc(y_ready, 1)

            def tokens(b):
                dve.wait_ge(h_ready, b.n + 1)
                dve.wait_ge(xb_ready, b.n + 1)
                V.tensor_tensor(hs[:, :, :], outp, xtok[:, b.slot, :, :], ALU.add).then_inc(h_taken, 1)
                dve.wait_ge(h_taken, b.n + 1)
                st.link(layer_norm(2 * b.n + 1, lambda t: hs[:, t, :], lambda t: hs[:, t, :], TT))
                st.link(V.tensor_tensor(hs[:, :, :], hs[:, :, :], lng[:, :].unsqueeze(1).to_broadcast([P, TT, C]),
                                        ALU.mult))
                ht = h[:, ds(2 * b.n, TT), :]
                step = st.mark(V.tensor_tensor(ht, hs[:, :, :], lnb[:, :].unsqueeze(1).to_broadcast([P, TT, C]),
                                               ALU.add))
                hh = [h[:, ds(2 * b.n + t, 1), :].rearrange("p o c -> p (o c)") for t in range(TT)]
                apart(dve, dve_step, step)
                ge(dve, tr_ready, b.n - 1)
                layer_norm(2 * b.n + 2, lambda t: x1[:, b.slot, t, :], lambda t: hh[t], TT).then_inc(x1_ready, 1)

            keys_values(fixed(0))

            def turn(b, prev):
                mixed(prev)
                keys_values(b)
                tokens(prev)

            turn(fixed(1), fixed(0))
            before_loop = st.n
            with dve.Fori(0, (B - 2) // 2) as i:
                st.turn(before_loop, i, 2 * MIX)
                one, two, prev = pair(i)
                turn(one, prev)
                turn(two, one)
                assert st.n == 2 * MIX
            st.base, st.n = before_loop + (B - 2) * MIX, 0
            mixed(fixed(7))
            tokens(fixed(7))

            V.memset(pre[:, :, 0:TAPS - 1], 0.0).then_inc(pad_ready, 1)

            def convolve(b, first):
                for n in range(6):
                    dve.wait_ge(pre_ready, 6 * b.n + (n + 1))
                    if not (first and n < 3):
                        dve.wait_ge(act_ready, 6 * b.n + (n - 2))
                    w, m = n // 2, n % 2
                    c = conv[:, n % 3, :]
                    st.link(V.tensor_scalar(c, pre[:, n % 3, 3:T + 3], taps[:, w, m, 3:4], None, ALU.mult))
                    for k in (2, 1, 0):
                        last = V.scalar_tensor_tensor(out=c, in0=pre[:, n % 3, k:T + k], scalar=taps[:, w, m, k:k + 1],
                                                      in1=c, op0=ALU.mult, op1=ALU.add)
                        if k:
                            st.link(last)
                    last.then_inc(conv_ready, 1)

            dve.wait_ge(ld_attn, N_ATTN)
            base = st.base + st.n
            st.base, st.n = base, 0
            convolve(fixed(0), True)
            convolve(fixed(1), False)
            base += st.n
            with dve.Fori(0, (B - 2) // 2) as i:
                st.turn(base, i, 36)
                for b in pair(i)[:2]:
                    convolve(b, False)
                assert st.n == 36
            st.base, st.n = base + 18 * (B - 2), 0

            dve.wait_ge(beta_exp, 1)
            st.link(V.tensor_scalar(betaL[:, :], betaL[:, :], 1.0, None, ALU.add))
            V.reciprocal(betaL[:, :], betaL[:, :]).then_inc(beta_ready, 1)
            dve.wait_ge(beta_ready, 1)
            st.link(V.tensor_scalar(nbeta[:, :], betaL[:, :], -1.0, None, ALU.mult))
            for n, (r, scale) in enumerate(((rk, 1.0), (rq, HD ** -0.5))):
                dve.wait_ge(sq_ready, n + 1)
                ge(dve, root_ready, n)
                V.tensor_reduce(sumsq[:, :], squares.rearrange("p d t -> p t d"), AX, ALU.add).then_inc(sum_ready, 1)
                dve.wait_ge(sum_ready, n + 1)
                V.tensor_scalar(sumsq[:, :], sumsq[:, :], EPS * EPS, None, ALU.max).then_inc(norm_step, 1)
                if n == 1:
                    last = V.tensor_tensor(kq[:, 0, :, :], kq[:, 0, :, :],
                                           rk[:, :].unsqueeze(1).to_broadcast([P, HD, T]), ALU.mult)
                    st.link(last)
                    st.link(V.tensor_tensor(nbk, kq[:, 0, :, :], nbeta[:, :].unsqueeze(1).to_broadcast([P, HD, T]),
                                            ALU.mult))
                dve.wait_ge(root_ready, n + 1)
                st.link(V.tensor_scalar(r[:, :], root[:, :], scale, None, ALU.mult))
            dve.wait_ge(sq_ready, 2)
            V.memset(S, 0.0).then_inc(scan_ready, 1)
            dve.wait_ge(scan_ready, 1)

            halves = [slice(0, HD // 2), slice(HD // 2, HD)]
            wide = [P, HD // 2, HD]

            def step(t, n, first=False):
                bk_t = nbk[:, :, ds(t, 1)].rearrange("p d o -> p (o d)")
                k_t = kq[:, 0, :, ds(t, 1)].rearrange("p d o -> p (o d)")
                for i, m in enumerate(halves):
                    if not first:
                        dve.wait_ge(scan_step, 8 * t + (i - 1))
                    V.tensor_tensor(prod[:, n, m, 0:HD], S[:, m, :], bk_t.unsqueeze(1).to_broadcast(wide),
                                    ALU.mult).then_inc(scan_step, 1)
                dve.wait_ge(bv_put, t + 1)
                for i, m in enumerate(halves):
                    dve.wait_ge(scan_step, 8 * t + (i + 1))
                    V.tensor_reduce(u[:, m], prod[:, n, m, :], AX, ALU.add).then_inc(scan_step, 1)
                for i, m in enumerate(halves):
                    dve.wait_ge(scan_step, 8 * t + (i + 3))
                    V.tensor_tensor(outer[:, m, :], u[:, m].unsqueeze(2).to_broadcast(wide),
                                    k_t.unsqueeze(1).to_broadcast(wide), ALU.mult).then_inc(scan_step, 1)
                if not first:
                    dve.wait_ge(q_read, t)
                for i, m in enumerate(halves):
                    dve.wait_ge(scan_step, 8 * t + (i + 5))
                    V.tensor_tensor(S[:, m, :], S[:, m, :], outer[:, m, :], ALU.add).then_inc(scan_step, 1)

            step(0, 0, True)
            with dve.Fori(0, (T - 1) // RING) as i:
                for k in range(RING):
                    step(i * RING + (k + 1), (k + 1) % 2)

            dve.wait_ge(o_sq, 1)
            st.link(V.tensor_reduce(sumsq[:, :], squares.rearrange("p d t -> p t d"), AX, ALU.add))
            st.link(V.tensor_tensor(sumsq[:, :], sumsq[:, :], rq[:, :], ALU.mult))
            st.link(V.tensor_tensor(sumsq[:, :], sumsq[:, :], rq[:, :], ALU.mult))
            V.tensor_scalar(sumsq[:, :], sumsq[:, :], 1.0 / HD, EPS, ALU.mult, ALU.add).then_inc(norm_step, 1)
            dve.wait_ge(root_ready, 3)
            st.link(V.tensor_tensor(root[:, :], root[:, :], rq[:, :], ALU.mult))
            V.tensor_tensor(kq[:, 1, :, :], kq[:, 1, :, :], root[:, :].unsqueeze(1).to_broadcast([P, HD, T]),
                            ALU.mult).then_inc(o_ready, 1)
            V.tensor_scalar(wo[:, :, :], wo[:, :, :], onw[:, 0:1], None, ALU.mult).then_inc(wo_ready, 1)

            for b in range(B + 1):
                rows, w = (P, TT) if b < B else (B, 1)
                dve.wait_ge(p_ready, b + 1)
                acc = ps[:, b % 2, :].rearrange("p (t c) -> p t c", t=TT)
                st.link(V.tensor_tensor(h[0:rows, 2 * b:2 * b + w, :], h[0:rows, 2 * b:2 * b + w, :],
                                        acc[0:rows, 0:w, :], ALU.add))
                if b == 0:
                    dve.wait_ge(o_ready, 1)
                layer_norm(2 * B + 1 + b, lambda t: x2[0:rows, 2 * b + t, :], lambda t: h[0:rows, 2 * b + t, :], w, rows
                           ).then_inc(x2_ready, 1)
                if b == 0:
                    st.link(V.memset(scores[:, NTILE - 1, :], 0.0))
                if b:
                    dve.wait_ge(sc_ready, b)
                    V.tensor_copy(scores[:, 2 * b - 2:2 * b, :],
                                  ps[:, 4 + (b - 1) % 2, 0:TT * E].rearrange("p (t e) -> p t e", t=TT)
                                  ).then_inc(sc_taken, 1)
            dve.wait_ge(sc_ready, B + 1)
            V.tensor_copy(scores[0:B, NTILE - 1, :], ps[0:B, 4, 0:E]).then_inc(sc_taken, 1)
            dve.wait_ge(sc_taken, B + 1)

            for n in range(NTILE):
                last = st.mark(V.max(top[:, n, :], scores[:, n, :]))
            dve.wait_ge(dve_step, last)
            for n in range(NTILE):
                last = st.mark(V.max_index(topi[:, n, :], top[:, n, :], scores[:, n, :]))
            V.tensor_tensor(gexp[:, :], top[:, :, 1], top[:, :, 0], ALU.subtract).then_inc(gd_ready, 1)
            dve.wait_ge(dve_step, last)
            st.link(V.tensor_copy(topf[:, :, :], topi[:, :, 0:TOPK]))
            for k in range(TOPK):
                last = st.mark(V.tensor_tensor(hot[:, k, :, :], topf[:, :, k:k + 1].to_broadcast([P, NTILE, E]),
                                               iota_e[:, :].unsqueeze(1).to_broadcast([P, NTILE, E]), ALU.is_equal))
            dve.wait_ge(dve_step, last)
            st.link(V.tensor_tensor(hots[:, :, :], hot[:, 0, :, :], hot[:, 1, :, :], ALU.add))
            V.tensor_tensor(hots[:, :, :], hots[:, :, :], valid[:, :].unsqueeze(2).to_broadcast([P, NTILE, E]),
                            ALU.mult).then_inc(hot_ready, 1)
            dve.wait_ge(ge_ready, 1)
            st.link(V.tensor_scalar(gate[:, 0, :], gexp[:, :], 1.0, None, ALU.add))
            st.link(V.reciprocal(gate[:, 0, :], gate[:, 0, :]))
            st.link(V.tensor_tensor(gate[:, 1, :], gexp[:, :], gate[:, 0, :], ALU.mult))
            dve.wait_ge(rank_ready, 1)
            counts = ps[:, 1, 0:NTILE * E].rearrange("p (n e) -> p n e", e=E)
            rank = ps[:, 0, 0:NTILE * E].rearrange("p (n e) -> p n e", e=E)
            st.link(V.memset(tot[:, 0, :], 0.0))
            for n in range(NTILE):
                st.link(V.tensor_tensor(tot[:, n + 1, :], tot[:, n, :], counts[:, n, :], ALU.add))
            st.link(V.tensor_scalar(ntile_f[:, :], tot[:, NTILE, :], float(P - 1), None, ALU.add))
            st.link(V.tensor_copy(ntile_i[:, :], ntile_f[:, :]))
            st.link(V.tensor_scalar(ntile_i[:, :], ntile_i[:, :], P.bit_length() - 1, None, ALU.arith_shift_right))
            st.link(V.tensor_copy(ntile_f[:, :], ntile_i[:, :]))
            st.link(V.memset(start[:, 0:1], 0.0))
            for e in range(E):
                st.link(V.tensor_tensor(start[:, e + 1:e + 2], start[:, e:e + 1], ntile_f[:, e:e + 1], ALU.add))
            st.link(V.tensor_tensor(place[:, :, :], rank, tot[:, 0:NTILE, :], ALU.add))
            st.link(V.scalar_tensor_tensor(out=place[:, :, :], in0=start[:, 0:E].unsqueeze(1).to_broadcast([P, NTILE, E]),
                                           scalar=float(P), in1=place[:, :, :], op0=ALU.mult, op1=ALU.add))
            for k in range(TOPK):
                st.link(V.tensor_tensor(pick[:, :, :], place[:, :, :], hot[:, k, :, :], ALU.mult))
                st.link(V.tensor_reduce(slotf[:, k, :], pick[:, :, :], AX, ALU.add))
            V.tensor_copy(slot[:, :, :], slotf[:, :, :]).then_inc(slot_ready, 1)
            st.link(V.tensor_tensor(cmp[:, :, :], iota_t[:, :].unsqueeze(2).to_broadcast([P, NT, E]),
                                    start[:, 0:E].unsqueeze(1).to_broadcast([P, NT, E]), ALU.is_ge))
            st.link(V.tensor_reduce(etab_f[:, :], cmp[:, :, :], AX, ALU.add))
            st.link(V.tensor_scalar(etab_f[:, :], etab_f[:, :], -1.0, None, ALU.add))
            V.tensor_copy(etab[:, :], etab_f[:, :]).then_inc(etab_ready, 1)

            def gated(j):
                dve.wait_ge(sil_ready, j.n + 1)
                dve.wait_ge(gt_ready, j.n + 1)
                ge(dve, ht_ready, j.n - 1)
                V.tensor_tensor(hid[:, j.slot, :], sil, ps[:, 2 + j.slot, :], ALU.mult).then_inc(hid_ready, 1)

            gated(fixed(0))
            gated(fixed(1))
            with dve.Fori(0, (NT - 2) // 2) as i:
                for j in pair(i)[:2]:
                    gated(j)
            for n in range(NTILE):
                rows = P if n < NTILE - 1 else B
                dve.wait_ge(gathered[n % 2], 32 * (n // 2 + 1))
                st.link(V.scalar_tensor_tensor(out=h[0:rows, n, :], in0=g0[0:rows, n % 2, :],
                                               scalar=gate[0:rows, 0, n:n + 1], in1=h[0:rows, n, :],
                                               op0=ALU.mult, op1=ALU.add))
                V.scalar_tensor_tensor(out=h[0:rows, n, :], in0=g1[0:rows, n % 2, :],
                                       scalar=gate[0:rows, 1, n:n + 1], in1=h[0:rows, n, :],
                                       op0=ALU.mult, op1=ALU.add).then_inc(fin_ready, 1)

        @block.tensor
        def _(pe):
            mm = nc.tensor.matmul
            pe.wait_ge(pool_const, 5)
            pe.wait_ge(c_ready, 1)
            for j in range(CJ):
                last = nc.tensor.transpose(clp[:, j, :], x1c[0:B, j * P:(j + 1) * P], ident[0:B, 0:B])
            last.then_inc(c_ready, 1)
            pe.wait_ge(ld_small, N_SMALL)

            def front(b):
                pe.wait_ge(x_loaded[b.slot], 32 * b.half + 32)
                for lt in range(2):
                    ge(pe, kvb_ready, 2 * b.n + (lt - 1))
                    for j in range(CJ):
                        last = mm(kvp[lt][:, j, :], xT[:, b.slot, j, lt * P:(lt + 1) * P],
                                  bdkv[:, :, :].rearrange("p w c -> p (w c)"), start=True, stop=True)
                    last.then_inc(kv_ready, 1)
                ge(pe, eq_ready, b.n)
                for j in range(CJ):
                    last = mm(qp[:, j, :], bdq[:, :], xT[:, b.slot, j, :], start=True, stop=True)
                last.then_inc(q_ready, 1)

            def sums(b):
                pe.wait_ge(ekv_ready, 2 * b.n + 2)
                ge(pe, y_ready, b.n)
                for j in range(CJ):
                    for w in range(2):
                        for s in range(2):
                            last = mm(ndp[j][:, w, :], ekv[:, b.slot, s, w, j * P:(j + 1) * P], ew[:, s, :],
                                      start=(s == 0), stop=(s == 1))
                    last.then_inc(nd_ready, 1)

            def project(b):
                pe.wait_ge(y_ready, b.n + 1)
                ge(pe, h_taken, b.n)
                for t in range(TT):
                    for j in range(CJ):
                        last = mm(outp[:, t, :], yT[:, b.slot, j, t * P:(t + 1) * P], outw[:, j, :],
                                  start=(j == 0), stop=(j == CJ - 1))
                last.then_inc(h_ready, 1)

            def turn_x1(b):
                pe.wait_ge(x1_ready, b.n + 1)
                pe.wait_ge(x1T_ready, b.n + 1)
                for t in range(TT):
                    for j in range(CJ):
                        last = nc.tensor.transpose(trp[:, j, t * P:(t + 1) * P], x1[:, b.slot, t, j * P:(j + 1) * P],
                                                   ident[:, :])
                last.then_inc(tr_ready, 1)

            def turn(b, prev):
                front(b)
                project(prev)
                sums(b)
                turn_x1(prev)

            front(fixed(0))
            pe.wait_ge(ew_ready, 1)
            sums(fixed(0))
            turn(fixed(1), fixed(0))
            with pe.Fori(0, (B - 2) // 2) as i:
                one, two, prev = pair(i)
                turn(one, prev)
                turn(two, one)
            project(fixed(7))
            turn_x1(fixed(7))

            def proj(b, first):
                rhs = [x1T[:, j, ds(b.n, 1), :].rearrange("p o t -> p (o t)") for j in range(CJ)]
                for n in range(6):
                    w, m = n // 2, n % 2
                    if not first:
                        pe.wait_ge(pre_ready, 6 * b.n + (n - 5))
                    for j in range(CJ):
                        last = mm(ps[:, n, 0:T], wqkv[:, w, j, m * P:(m + 1) * P], rhs[j],
                                  start=(j == 0), stop=(j == CJ - 1))
                    last.then_inc(qkv_ready, 1)
                if not first:
                    pe.wait_ge(ld_attn, N_ATTN)
                    pe.wait_ge(bet_copied, b.n)
                for j in range(CJ):
                    last = mm(ps[0:NH, 7, 0:T], wb[:, j, :], rhs[j], start=(j == 0), stop=(j == CJ - 1))
                last.then_inc(bet_ready, 1)

            pe.wait_ge(ld_attn, N_ATTN)
            pe.wait_ge(x1T_ready, B + 1)
            proj(fixed(0), True)
            proj(fixed(1), False)
            with pe.Fori(0, (B - 2) // 2) as i:
                for b in pair(i)[:2]:
                    proj(b, False)

            def attn_out(b):
                if b < B:
                    pe.wait_ge(oT_loaded[b % 2], 32 * (b // 2 + 1))
                else:
                    pe.wait_ge(oc_ready, B)
                ge(pe, x2_ready, b - 1)
                rows, w = (P, TT) if b < B else (B, 1)
                for t in range(w):
                    for m in range(CJ):
                        lhsT = oT[:, b % 2, m, 1 + t * P:1 + (t + 1) * P] if b < B else oTc[:, m, :]
                        last = mm(ps[0:rows, b % 2, t * C:(t + 1) * C], lhsT, wo[:, m, :],
                                  start=(m == 0), stop=(m == CJ - 1))
                last.then_inc(p_ready, 1)

            def score(b):
                rows, w = (P, TT) if b < B else (B, 1)
                pe.wait_ge(x2_ready, b + 1)
                ge(pe, x2T_ready, b - 1)
                for t in range(w):
                    for j in range(CJ):
                        last = nc.tensor.transpose(
                            ps[:, 2 + b % 2, :].rearrange("p (j t r) -> p j t r", j=CJ, t=TT)[:, j, t, 0:rows],
                            x2[0:rows, 2 * b + t, j * P:(j + 1) * P], ident[0:rows, 0:rows])
                last.then_inc(t2_ready, 1)
                pe.wait_ge(x2T_ready, b + 1)
                ge(pe, sc_taken, b - 1)
                for t in range(w):
                    for j in range(CJ):
                        last = mm(ps[0:rows, 4 + b % 2, t * E:(t + 1) * E], x2T[:, j, t, 0:rows], wg[:, j, :],
                                  start=(j == 0), stop=(j == CJ - 1))
                last.then_inc(sc_ready, 1)

            pe.wait_ge(wo_ready, 1)
            attn_out(0)
            for b in range(1, B + 1):
                attn_out(b)
                score(b - 1)
            score(B)
            pe.wait_ge(hot_ready, 1)
            flat = hots[:, :, :].rearrange("p n e -> p (n e)")
            mm(ps[:, 0, 0:NTILE * E], before[:, :], flat, start=True, stop=True)
            mm(ps[:, 1, 0:NTILE * E], ones[:, :], flat, start=True, stop=True).then_inc(rank_ready, 1)

            pe.wait_ge(etab_ready, 1)
            pe.wait_ge(ld_ffn, N_FFN)
            pe.wait_ge(ld_down, 16 * E)

            def expert(n):
                return pe.value_load(etab[0:1, ds(n, 1)], min_val=0, max_val=E - 1)

            def rows_in(j):
                pe.wait_ge(xs_loaded[j.slot], 16 * j.half + 16)
                ge(pe, xsT_ready, j.n)
                for c in range(CJ):
                    last = nc.tensor.transpose(ps[:, 4, c * P:(c + 1) * P], xs[:, j.slot, c * P:(c + 1) * P], ident[:, :])
                last.then_inc(xst_ready, 1)

            def up(j, e, w, bank, s, taken):
                ge(pe, taken, j.n - 1)
                for c in range(CJ):
                    last = mm(ps[:, bank + j.slot, :], xsT[:, j.slot, c * P:(c + 1) * P],
                              w[:, ds(e, 1), c, :].rearrange("p o f -> p (o f)"), start=(c == 0), stop=(c == CJ - 1))
                last.then_inc(s, 1)

            def turn_hidden(j):
                pe.wait_ge(hid_ready, j.n + 1)
                ge(pe, hidT_ready, j.n)
                for f in range(FJ):
                    last = nc.tensor.transpose(ps[:, 5, f * P:(f + 1) * P], hid[:, j.slot, f * P:(f + 1) * P], ident[:, :])
                last.then_inc(ht_ready, 1)

            def down(j, e):
                pe.wait_ge(hidT_ready, j.n + 1)
                ge(pe, ys_ready, j.n)
                for f in range(FJ):
                    last = mm(ps[:, 6, 0:C], hidT[:, j.slot, f * P:(f + 1) * P],
                              w3[:, ds(e, 1), f, :].rearrange("p o c -> p (o c)"), start=(f == 0), stop=(f == FJ - 1))
                last.then_inc(y2_ready, 1)

            def ffn(j, e, prev, e_prev, coming):
                pe.wait_ge(xsT_ready, j.n + 1)
                up(j, e, w1, 0, up_ready, sil_ready)
                if prev is not None:
                    turn_hidden(prev)
                up(j, e, w2, 2, gt_ready, hid_ready)
                if coming is not None:
                    rows_in(coming)
                if prev is not None:
                    down(prev, e_prev)

            rows_in(fixed(0))
            ffn(fixed(0), expert(0), None, None, fixed(1))
            for n in range(1, 4):
                ffn(fixed(n), expert(n), fixed(n - 1), expert(n - 1), fixed(n + 1))
            with pe.Fori(0, (NT - 8) // 4) as i:
                tiles = six(i)
                e = [expert(j.n) for j in tiles[:5]]
                for k in range(1, 5):
                    ffn(tiles[k], e[k], tiles[k - 1], e[k - 1], tiles[k + 1])
            e = [expert(n) for n in range(NT - 5, NT)]
            for k in range(1, 5):
                n = NT - 5 + k
                ffn(fixed(n), e[k], fixed(n - 1), e[k - 1], fixed(n + 1) if n < NT - 1 else None)
            turn_hidden(fixed(NT - 1))
            down(fixed(NT - 1), e[4])


MIX = 13


def kernel(**inputs):
    import numpy as np
    import concourse.bacc as bacc
    from concourse.bass_utils import run_bass_kernel_spmd

    g = {k: np.asarray(v) for k, v in inputs.items()}
    x = g["x"]
    arrays = [
        ("x_ch", x.transpose(0, 3, 1, 2).reshape(B, C, L)),
        ("x_tok", x.transpose(0, 2, 3, 1).reshape(B, L, C)),
        ("cls_tok", g["cls_tok"].reshape(C)),
        ("tWq", g["L0_tok_Wq_w"].T), ("tWk", g["L0_tok_Wk_w"].T), ("tWv", g["L0_tok_Wv_w"].T),
        ("tbq", g["L0_tok_Wq_b"].reshape(D, 1)), ("tbk", g["L0_tok_Wk_b"]), ("tbv", g["L0_tok_Wv_b"]),
        ("w_bias", g["L0_tok_w_bias"].T), ("mask", g["L0_tok_local_mask"].T),
        ("out_w", g["L0_tok_out_w"]), ("out_b", g["L0_tok_out_b"]),
        ("ln_g", g["L0_tok_ln_g"]), ("ln_b", g["L0_tok_ln_b"]),
        ("aWq", g["L0_attn_Wq"].T), ("aWk", g["L0_attn_Wk"].T), ("aWv", g["L0_attn_Wv"].T),
        ("aWb", g["L0_attn_Wb"].T), ("aWo", g["L0_attn_Wo"].T),
        ("conv_q", g["L0_attn_conv_q"]), ("conv_k", g["L0_attn_conv_k"]), ("conv_v", g["L0_attn_conv_v"]),
        ("o_norm", g["L0_attn_o_norm_w"].reshape(HD, 1)), ("Wg", g["L0_ffn_Wg"].T),
        ("W1", g["L0_ffn_W1"].transpose(0, 2, 1)), ("W2", g["L0_ffn_W2"].transpose(0, 2, 1)),
        ("W3", g["L0_ffn_W3"].transpose(0, 2, 1)),
    ]
    nc = bacc.Bacc("TRN2", target_bir_lowering=False, num_devices=1)
    feed, args = {}, []
    for name, a in arrays:
        a = np.ascontiguousarray(a)
        feed["in_" + name] = a
        args.append(nc.dram_tensor("in_" + name, a.shape, mybir.dt.from_np(a.dtype), kind="ExternalInput").ap())
    out = nc.dram_tensor("out", [B, T, C], F32, kind="ExternalOutput").ap()
    vit_block(nc, *args, out)
    return run_bass_kernel_spmd(nc, [feed], core_ids=[0]).results[0]["out"]
```

```python
from contextlib import ExitStack

import concourse.bass as bass
from concourse import mybir

F32 = mybir.dt.float32
I32 = mybir.dt.int32
U32 = mybir.dt.uint32
BF16 = mybir.dt.bfloat16
U8 = mybir.dt.uint8
ALU = mybir.AluOpType
ACT = mybir.ActivationFunctionType
AX = mybir.AxisListType.X
ds = bass.ds

P = 128
B, F, L, H, D = 8, 64, 256, 4, 64
C = H * F
T = L + 1
NH, HD = 16, C // 16
TAPS = 4
RING = 16
PART = RING // 2
E, FF, TOPK = 8, 512, 2
CJ = C // P
FJ = FF // P
TT = L // P
NTILE = B * TT + 1
PAIRS = B * T * TOPK
NT = (PAIRS + E * (P - 1)) // P
WORK = 5360 + HD * T
ROW = C + 2
REGION = B * T + P
EPS_LN = 1e-5
EPS = 1e-6
SEED = 0x5F3759DF
PEEL = 4


class Steps:

    def __init__(self, eng, sem):
        self.eng, self.sem, self.base, self.n = eng, sem, 0, 0

    def mark(self, ins):
        ins.then_inc(self.sem, 1)
        self.n += 1
        return self.base + self.n

    def link(self, ins):
        self.eng.wait_ge(self.sem, self.mark(ins))

    def turn(self, base, i, per):
        self.base, self.n = base + i * per, 0


class Batch:

    def __init__(self, n, half, slot):
        self.n, self.half, self.slot = n, half, slot


def pair(i):
    return Batch(2 * i + 2, i + 1, 0), Batch(2 * i + 3, i + 1, 1), Batch(2 * i + 1, i, 1)


def around(i):
    return [Batch(2 * i + k, i + k // 2, k % 2) for k in range(2, 6)]


def six(i):
    return [Batch(4 * i + k, 2 * i + k // 2, k % 2) for k in range(3, 9)]


def fixed(n):
    return Batch(n, n // 2, n % 2)


def vit_block(nc, x_ch, x_tok, cls_tok, tWq, tWk, tWv, tbq, tbk, tbv, w_bias, mask, out_w, out_b, ln_g, ln_b,
              aWq, aWk, aWv, aWb, aWo, conv_q, conv_k, conv_v, o_norm, Wg, W1, W2, W3, out):
    with ExitStack() as ctx:
        def sb(name, shape, dt=F32):
            return ctx.enter_context(nc.sbuf_tensor(name, shape, dt))

        def sem(name):
            return ctx.enter_context(nc.semaphore(name))

        expert_in = nc.dram_tensor("expert_in", [E * REGION, ROW], F32).ap()
        pair_out = nc.dram_tensor("pair_out", [TOPK * (NTILE * P + 1), C], F32).ap()

        ident = sb("ident", [P, P])
        ones = sb("ones", [P, P])
        before = sb("before", [P, P])
        bdq = sb("bdq", [P, P])
        bdkv = sb("bdkv", [P, 2, P])
        neg_bq = sb("neg_bq", [P, 1])
        kv_bias = sb("kv_bias", [P, 2, 2, D])
        ew = sb("ew", [P, 2, L])
        wmask8 = sb("wmask8", [P, 2, L], U8)
        wmask = sb("wmask", [P, 2, L])
        outw = sb("outw", [P, CJ, C])
        outb = sb("outb", [P, C])
        lng = sb("lng", [P, C])
        lnb = sb("lnb", [P, C])
        wqkv = sb("wqkv", [P, 3, CJ, C])
        wb = sb("wb", [P, CJ, NH])
        wo = sb("wo", [P, CJ, C])
        taps = sb("taps", [P, 3, CJ, TAPS])
        onw = sb("onw", [P, 1])
        wg = sb("wg", [P, CJ, E])
        w1 = sb("w1", [P, E, CJ, FF])
        w2 = sb("w2", [P, E, CJ, FF])
        h = sb("h", [P, NTILE, C])
        big = sb("big", [P, NTILE * ROW])
        x1T = big[:, 0:CJ * B * T].rearrange("p (j b t) -> p j b t", j=CJ, b=B)
        squares = big[:, 0:HD * T].rearrange("p (d t) -> p d t", d=HD)
        nbk = squares
        x2 = big[:, :].rearrange("p (n c) -> p n c", c=ROW)
        kq = sb("kq", [P, 2, HD, T])
        w3 = kq[:, :, :, :].rearrange("p w d t -> p (w d t)")[:, 0:E * FJ * C].rearrange(
            "p (e j c) -> p e j c", e=E, j=FJ)
        betaL = sb("betaL", [P, T])
        nbeta = sb("nbeta", [P, T])
        eps_q = sb("eps_q", [P, T])
        sumsq = sb("sumsq", [P, T])
        root = sb("root", [P, T])
        roott = sb("roott", [P, T])
        work = sb("work", [P, WORK])

        def cut(at, shape):
            n = 1
            for s in shape:
                n *= s
            names = "abcd"[:len(shape)]
            v = work[:, at:at + n]
            if len(shape) == 1:
                return v
            return v.rearrange("p (%s) -> p %s" % (" ".join(names), " ".join(names)),
                               **{k: s for k, s in zip(names, shape)})

        spare = w2[:, :, :, :].rearrange("p e c f -> p (e c f)")

        def lent(at, shape):
            n = 1
            for s in shape:
                n *= s
            names = "abcd"[:len(shape)]
            return spare[:, at:at + n].rearrange("p (%s) -> p %s" % (" ".join(names), " ".join(names)),
                                                 **{k: s for k, s in zip(names, shape)})

        xtok = lent(0, [2, TT, C])
        kvb = lent(1024, [2, CJ, L])
        ekv = lent(2048, [2, 2, 2, C])
        eq = lent(4096, [CJ, L])
        yT = lent(4608, [2, CJ, L])
        den1 = lent(5632, [CJ, L])
        hs = lent(6144, [TT, C])
        x1 = lent(6656, [2, TT, C])
        x1c = lent(7680, [C])
        pre = cut(0, [3, T + TAPS - 1])
        conv = cut(1024, [3, T])
        act_ = cut(2048, [3, T])
        bet = cut(3072, [2, T])
        xT = cut(4096, [2, CJ, L])
        squares_q = cut(0, [HD, T])
        vL = cut(WORK - HD * T, [HD, T])
        qS = cut(0, [RING, HD, HD])
        prod = cut(4096, [2, HD, HD + 1])
        outer = cut(4640, [HD, HD])
        S = cut(4896, [HD, HD])
        u = cut(5152, [HD])
        pairs = wqkv[:, 0:2, :, :].rearrange("p w j (m d) -> p (w j m d)", d=HD)[:, 0:PART * HD * 8].rearrange(
            "p (t m d) -> p t m d", t=PART, m=HD)
        fours = wqkv[:, 2, :, :].rearrange("p j c -> p (j c)").rearrange("p (t m d) -> p t m d", t=PART, m=HD)
        eights = outw[:, 0, :].rearrange("p (t m d) -> p t m d", t=PART, m=HD)
        oT = cut(0, [2, CJ, T])
        oTc = cut(1100, [CJ, B])
        x2T = cut(2048, [CJ, TT, P])
        zero_rows = outw[:, :, :].rearrange("p j c -> p (j c)")[:, 0:ROW]
        xs = cut(4096, [2, ROW])
        xsT = cut(4612, [2, C])
        hid = cut(5124, [2, FF])
        sil = cut(6148, [FF])
        hidT = cut(6660, [2, FF])
        ys = cut(7684, [2, C])
        got = cut(0, [NTILE, TOPK, C])
        stats = sb("stats", [P, 2, 2, 6])
        mv = sb("mv", [P, 2, TT, 2])
        rstd = sb("rstd", [P, 2, TT])
        newv = sb("newv", [P, TT])
        newt = sb("newt", [P, TT])
        eps_ln = sb("eps_ln", [P, 1])
        cst = sb("cst", [P, 10])
        scores = sb("scores", [P, NTILE, E])
        top = sb("top", [P, NTILE, 8])
        topi = sb("topi", [P, NTILE, 8], U32)
        topf = sb("topf", [P, NTILE, TOPK])
        iota_e = sb("iota_e", [P, E])
        iota_t = sb("iota_t", [P, NT])
        hot = sb("hot", [P, TOPK, NTILE, E])
        hots = sb("hots", [P, 2, TT, E], BF16)
        before16 = sb("before16", [P, P], BF16)
        ones16 = sb("ones16", [P, P], BF16)
        region = sb("region", [P, E])
        token2 = sb("token2", [P, NTILE])
        tot = sb("tot", [P, B + 2, E])
        count = sb("count", [P, E])
        ntile_f = sb("ntile_f", [P, E])
        start = sb("start", [P, E + 1])
        place = sb("place", [P, TT, E])
        pick = sb("pick", [P, TOPK, TT, E])
        slotf = sb("slotf", [P, TOPK, TT])
        slot = sb("slot", [P, TOPK, NTILE], U32)
        zslot = sb("zslot", [P, E], I32)
        gate = sb("gate", [P, TOPK, NTILE])
        gexp = sb("gexp", [P, NTILE])
        cmp = sb("cmp", [P, NT, E])
        full = sb("full", [P, E, NT])
        tile_row = sb("tile_row", [P, NT, E])
        sel = sb("sel", [P, NT, E])
        row_f = sb("row_f", [P, NT])
        row_i = sb("row_i", [P, NT], I32)
        other = sb("other", [P, 2])
        pair_id = sb("pair_id", [P, 2], U32)
        etab_f = sb("etab_f", [P, NT])
        etab = sb("etab", [P, NT], I32)

        ps = ctx.enter_context(nc.psum_tensor("ps", [P, 8, 512], F32))
        kvp = [ps[:, n, :].rearrange("p (j c) -> p j c", j=CJ) for n in range(2)]
        qp = ps[:, 2, :].rearrange("p (j l) -> p j l", j=CJ)
        ndp = [ps[:, 3 + n, :].rearrange("p (w l) -> p w l", w=2) for n in range(2)]
        outp = ps[:, 5, :].rearrange("p (t c) -> p t c", t=TT)
        trp = ps[:, 5, :].rearrange("p (j t) -> p j t", j=CJ)
        clp = ps[:, 7, 0:CJ * B].rearrange("p (j b) -> p j b", j=CJ)

        ld_small = sem("ld_small")
        ld_attn = sem("ld_attn")
        ld_ffn = sem("ld_ffn")
        ld_down = sem("ld_down")
        zslot_ready = sem("zslot_ready")
        zeroed = sem("zeroed")
        near_step = sem("near_step")
        near_ready = sem("near_ready")
        place_ready = sem("place_ready")
        other_ready = sem("other_ready")
        pair_ready = sem("pair_ready")
        x_loaded = [sem(f"x_loaded{s}") for s in range(2)]
        pool_const = sem("pool_const")
        blocks0 = sem("blocks0")
        ew_ready = sem("ew_ready")
        wm_ready = sem("wm_ready")
        xb_ready = sem("xb_ready")
        kv_ready = sem("kv_ready")
        q_ready = sem("q_ready")
        kvb_ready = sem("kvb_ready")
        ek_ready = sem("ek_ready")
        ekv_ready = sem("ekv_ready")
        eq_ready = sem("eq_ready")
        nd_ready = sem("nd_ready")
        y_ready = sem("y_ready")
        h_ready = sem("h_ready")
        h_taken = sem("h_taken")
        x1_ready = sem("x1_ready")
        tr_ready = sem("tr_ready")
        x1T_ready = sem("x1T_ready")
        c_ready = sem("c_ready")
        qkv_ready = sem("qkv_ready")
        taken = sem("taken")
        pad_ready = sem("pad_ready")
        conv_ready = sem("conv_ready")
        act_ready = sem("act_ready")
        relay = [sem(f"relay{s}") for s in range(3)]
        brelay = [sem(f"brelay{s}") for s in range(2)]
        sq_ready = sem("sq_ready")
        norm_step = sem("norm_step")
        sum_ready = sem("sum_ready")
        root_near = sem("root_near")
        root_ready = sem("root_ready")
        var_ready = sem("var_ready")
        rstd_ready = sem("rstd_ready")
        beta_exp = sem("beta_exp")
        beta_ready = sem("beta_ready")
        scan_ready = sem("scan_ready")
        scan_step = sem("scan_step")
        bv_put = sem("bv_put")
        q_read = sem("q_read")
        summed = sem("summed")
        o_sq = sem("o_sq")
        o_done = sem("o_done")
        o_ready = sem("o_ready")
        wo_ready = sem("wo_ready")
        oT_loaded = [sem(f"oT_loaded{s}") for s in range(2)]
        oc_ready = sem("oc_ready")
        p_ready = sem("p_ready")
        x2_ready = sem("x2_ready")
        t2_ready = sem("t2_ready")
        x2T_ready = sem("x2T_ready")
        sc_ready = sem("sc_ready")
        sc_taken = sem("sc_taken")
        hot_ready = sem("hot_ready")
        rank_ready = sem("rank_ready")
        gd_ready = sem("gd_ready")
        ge_ready = sem("ge_ready")
        slot_ready = sem("slot_ready")
        etab_ready = sem("etab_ready")
        scattered = sem("scattered")
        xs_loaded = [sem(f"xs_loaded{s}") for s in range(2)]
        xst_ready = sem("xst_ready")
        xsT_ready = sem("xsT_ready")
        up_ready = sem("up_ready")
        gt_ready = sem("gt_ready")
        sil_ready = sem("sil_ready")
        hid_ready = sem("hid_ready")
        ht_ready = sem("ht_ready")
        hidT_ready = sem("hidT_ready")
        y2_ready = sem("y2_ready")
        ys_ready = sem("ys_ready")
        ys_stored = [sem(f"ys_stored{s}") for s in range(2)]
        got_loaded = [sem(f"got_loaded{n}") for n in range(B + 1)]
        fin_ready = sem("fin_ready")
        stored = sem("stored")
        dve_step = sem("dve_step")
        act_step = sem("act_step")
        pool_step = sem("pool_step")

        N_SMALL, N_ATTN, N_FFN = 0, 0, 0
        small_loads = [
            (bdq[0:F, 0:D], tWq), (bdq[F:P, D:P], tWq),
            (bdkv[0:F, 0, 0:D], tWk), (bdkv[F:P, 0, D:P], tWk),
            (bdkv[0:F, 1, 0:D], tWv), (bdkv[F:P, 1, D:P], tWv)]
        plain_loads = [
            (neg_bq[0:D, :], tbq), (neg_bq[D:P, :], tbq),
            (ew[:, :, :], w_bias.rearrange("(a p) t -> p a t", p=P)),
            (wmask8[:, :, :], mask.rearrange("(a p) t -> p a t", p=P)),
            (outw[:, :, :], out_w.rearrange("(a p) t -> p a t", p=P)),
            (outb[:, :], out_b.partition_broadcast(P)), (lng[:, :], ln_g.partition_broadcast(P)),
            (lnb[:, :], ln_b.partition_broadcast(P)),
            (h[0:B, NTILE - 1, :], cls_tok.partition_broadcast(B))]
        for r in range(2):
            plain_loads += [(kv_bias[:, 0, r, :], tbk.partition_broadcast(P)),
                            (kv_bias[:, 1, r, :], tbv.partition_broadcast(P))]
        attn_loads = [(wb[:, :, :], aWb.rearrange("(a p) t -> p a t", p=P)),
                      (wo[:, :, :], aWo.rearrange("(a p) t -> p a t", p=P)),
                      (wg[:, :, :], Wg.rearrange("(a p) t -> p a t", p=P))]
        for n, (w, c) in enumerate(((aWk, conv_k), (aWq, conv_q), (aWv, conv_v))):
            attn_loads += [(wqkv[:, n, :, :], w.rearrange("(a p) t -> p a t", p=P)),
                           (taps[:, n, :, :], c.rearrange("(a p) t -> p a t", p=P))]
        for r in range(P // HD):
            attn_loads.append((onw[r * HD:(r + 1) * HD, :], o_norm))
        N_SMALL, N_ATTN = 16 * (len(small_loads) + len(plain_loads)), 16 * len(attn_loads)
        ffn_loads = []
        for e in range(E):
            ffn_loads += [(w1[:, e, :, :], W1[e].rearrange("(a p) f -> p a f", p=P)),
                          (w2[:, e, :, :], W2[e].rearrange("(a p) f -> p a f", p=P))]
        N_FFN = 16 * len(ffn_loads)

        def ge(eng, s, v):
            if not (isinstance(v, int) and v <= 0):
                eng.wait_ge(s, v)

        def apart(eng, s, v):
            if not isinstance(v, int):
                v = eng.to_reg(v)
                eng.wait_ge(ld_small, N_SMALL)
            eng.wait_ge(s, v)

        block = ctx.enter_context(nc.Block())

        @block.sync
        def _(sp):
            def load_x(b):
                sp.dma_start(xT[:, b.slot, :, :], x_ch[ds(b.n, 1), :, :].rearrange("o (a p) l -> p (o a) l", p=P)
                             ).then_inc(x_loaded[b.slot], 16)
                sp.dma_start(xtok[:, b.slot, :, :], x_tok[ds(b.n, 1), :, :].rearrange("o (a p) c -> p (o a) c", p=P)
                             ).then_inc(x_loaded[b.slot], 16)

            load_x(fixed(0))
            for dst, src in plain_loads:
                sp.dma_start(dst, src).then_inc(ld_small, 16)
            sp.wait_ge(blocks0, 2)
            for dst, src in small_loads:
                sp.dma_start(dst, src).then_inc(ld_small, 16)
            load_x(fixed(1))
            for dst, src in attn_loads:
                sp.dma_start(dst, src).then_inc(ld_attn, 16)
            def reload_x(b):
                ge(sp, q_ready, b.n - 1)
                ge(sp, h_taken, b.n - 1)
                load_x(b)

            reload_x(fixed(2))
            for b in range(B):
                if b + 3 < B:
                    reload_x(fixed(b + 3))
                for n in range(6):
                    if n == 3:
                        sp.wait_ge(taken, 7 * b + 7)
                        sp.dma_start(betaL[b * NH:(b + 1) * NH, :], bet[0:NH, b % 2, :]).then_inc(brelay[b % 2], 16)
                    w, m = n // 2, n % 2
                    at = b * NH + m * (P // HD)
                    dst = vL[at:at + P // HD, :, :] if w == 2 else kq[at:at + P // HD, w, :, :]
                    sp.wait_ge(act_ready, 6 * b + n + 1)
                    sp.dma_start(dst, act_[:, n % 3, :]).then_inc(relay[n % 3], 16)
            for dst, src in ffn_loads:
                sp.dma_start(dst, src).then_inc(ld_ffn, 16)
            for b in range(B):
                if b == 0:
                    sp.wait_ge(o_ready, 1)
                if b >= 2:
                    sp.wait_ge(p_ready, b - 1)
                    sp.wait_ge(oc_ready, b - 1)
                for m in range(CJ):
                    at = b * NH + m * (P // HD)
                    sp.dma_start(oT[:, b % 2, m, :], kq[at:at + P // HD, 1, :, :]).then_inc(oT_loaded[b % 2], 16)
            for s in range(2):
                sp.wait_ge(oT_loaded[s], 32 * (B // 2))
            for e in range(E):
                sp.dma_start(w3[:, e, :, :], W3[e].rearrange("(a p) c -> p a c", p=P)).then_inc(ld_down, 16)
            sp.wait_ge(pool_const, 10)
            sp.wait_ge(zslot_ready, 1)
            for e in range(E):
                row = sp.value_load(zslot[0:1, e:e + 1], min_val=0, max_val=E * REGION - P)
                sp.dma_start(expert_in[ds(row, P), :], zero_rows).then_inc(zeroed, 16)
            sp.wait_ge(etab_ready, 1)
            sp.wait_ge(zeroed, 16 * E)
            sp.wait_ge(scattered, 16 * TOPK * NTILE)

            def load_tile(j):
                row = sp.value_load(row_i[0:1, ds(j.n, 1)], min_val=0, max_val=E * REGION - P)
                sp.dma_start(xs[:, j.slot, :], expert_in[ds(row, P), :]).then_inc(xs_loaded[j.slot], 16)

            load_tile(fixed(0))
            load_tile(fixed(1))
            with sp.Fori(0, (NT - 2) // 2) as i:
                for j in pair(i)[:2]:
                    sp.wait_ge(xst_ready, j.n - 1)
                    sp.wait_ge(pair_ready, j.n - 1)
                    load_tile(j)
            for s in range(2):
                sp.wait_ge(ys_stored[s], 16 * (NT // 2))
            flat = pair_out[:, :].rearrange("(t k) c -> t (k c)", k=TOPK)
            for b in range(B):
                at = 1 + TT * P * b
                sp.dma_start(got[:, TT * b:TT * (b + 1), :, :].rearrange("p n k c -> p n (k c)"),
                             flat[at:at + TT * P, :].rearrange("(n p) c -> p n c", p=P)).then_inc(got_loaded[b], 16)
            sp.dma_start(got[0:B, NTILE - 1, :, :].rearrange("p k c -> p (k c)"),
                         flat[1 + TT * P * B:1 + TT * P * B + B, :]).then_inc(got_loaded[B], 16)
            for b in range(B + 1):
                sp.wait_ge(fin_ready, b + 1)
                if b < B:
                    sp.dma_start(out[b, 1:T, :].rearrange("(n p) c -> p n c", p=P),
                                 h[:, TT * b:TT * (b + 1), :]).then_inc(stored, 16)
                else:
                    sp.dma_start(out[:, 0, :], h[0:B, NTILE - 1, :]).then_inc(stored, 16)
            sp.wait_ge(stored, 16 * (B + 1))

        @block.gpsimd
        def _(pool):
            st = Steps(pool, pool_step)
            nc.gpsimd.memset(bdq[:, :], 0.0).then_inc(blocks0, 1)
            nc.gpsimd.memset(bdkv[:, :, :], 0.0).then_inc(blocks0, 1)
            nc.gpsimd.memset(eps_ln[:, :], EPS_LN).then_inc(pool_const, 1)
            nc.gpsimd.memset(ones[:, :], 1.0).then_inc(pool_const, 1)
            st.link(nc.gpsimd.memset(ident[:, :], 0.0))
            nc.gpsimd.affine_select(out=ident[:, :], in_=ident[:, :], compare_op=ALU.not_equal, fill=1.0,
                                    base=0, pattern=[[-1, P]], channel_multiplier=1).then_inc(pool_const, 1)
            st.link(nc.gpsimd.memset(before[:, :], 1.0))
            nc.gpsimd.affine_select(out=before[:, :], in_=before[:, :], compare_op=ALU.is_gt, fill=0.0,
                                    base=0, pattern=[[1, P]], channel_multiplier=-1).then_inc(pool_const, 1)
            nc.gpsimd.iota(iota_e[:, :], pattern=[[1, E]], base=0, channel_multiplier=0,
                           allow_small_or_imprecise_dtypes=True).then_inc(pool_const, 1)
            nc.gpsimd.iota(iota_t[:, :], pattern=[[1, NT]], base=0, channel_multiplier=0,
                           allow_small_or_imprecise_dtypes=True).then_inc(pool_const, 1)
            nc.gpsimd.iota(region[:, :], pattern=[[REGION, E]], base=0, channel_multiplier=0,
                           allow_small_or_imprecise_dtypes=True).then_inc(pool_const, 1)
            st.link(nc.gpsimd.iota(token2[:, :], pattern=[[TOPK * P, NTILE]], base=TOPK, channel_multiplier=TOPK,
                                   allow_small_or_imprecise_dtypes=True))
            pool.wait_ge(pool_const, 4)
            nc.gpsimd.tensor_copy(before16[:, :], before[:, :]).then_inc(pool_const, 1)
            nc.gpsimd.tensor_copy(ones16[:, :], ones[:, :]).then_inc(pool_const, 1)
            def newton(y, v, t, ready):
                st.link(nc.gpsimd.tensor_tensor(t, y, y, ALU.mult))
                step = st.mark(nc.gpsimd.tensor_tensor(t, v, t, ALU.mult))
                apart(pool, pool_step, step)
                st.link(nc.gpsimd.tensor_scalar(t, t, -0.5, 1.5, ALU.mult, ALU.add))
                nc.gpsimd.tensor_tensor(y, y, t, ALU.mult).then_inc(ready, 1)

            def rsqrt(number, n=TT, rows=P):
                v, y, t = newv[0:rows, 0:n], rstd[0:rows, 0, 0:n], newt[0:rows, 0:n]
                apart(pool, var_ready, number + 1)
                step = st.mark(nc.gpsimd.tensor_scalar(v, mv[0:rows, 0, 0:n, 1], EPS_LN, None, ALU.add))
                apart(pool, pool_step, step)
                st.link(nc.gpsimd.tensor_scalar(y.bitcast(I32), v.bitcast(I32), -0.5, float(SEED), ALU.mult, ALU.add))
                for k in range(3):
                    st.link(nc.gpsimd.tensor_tensor(t, y, y, ALU.mult))
                    step = st.mark(nc.gpsimd.tensor_tensor(t, v, t, ALU.mult))
                    apart(pool, pool_step, step)
                    st.link(nc.gpsimd.tensor_scalar(t, t, -0.5, 1.5, ALU.mult, ALU.add))
                    last = nc.gpsimd.tensor_tensor(y, y, t, ALU.mult)
                    if k < 2:
                        st.link(last)
                last.then_inc(rstd_ready, 1)

            def mix(b):
                pool.wait_ge(x_loaded[b.slot], 32 * b.half + 32)
                nc.gpsimd.tensor_tensor(xtok[:, b.slot, :, :], xtok[:, b.slot, :, :],
                                        outb[:, :].unsqueeze(1).to_broadcast([P, TT, C]),
                                        ALU.add).then_inc(xb_ready, 1)
                for lt in range(2):
                    pool.wait_ge(ek_ready, 2 * b.n + (lt + 1))
                    nc.gpsimd.tensor_tensor(
                        ekv[:, b.slot, lt, 0, :].rearrange("p (j c) -> p j c", j=CJ),
                        ekv[:, b.slot, lt, 1, :].rearrange("p (j c) -> p j c", j=CJ),
                        kvb[:, lt, :, P:2 * P], ALU.mult).then_inc(ekv_ready, 1)

            def turn(b, prev):
                if b is not None:
                    mix(b)
                if prev is not None:
                    rsqrt(2 * prev.n + 1)
                    rsqrt(2 * prev.n + 2)

            pool.wait_ge(ld_small, N_SMALL)
            rsqrt(0, 1, B)
            turn(fixed(0), None)
            for n in range(1, PEEL):
                start_of = st.n
                turn(fixed(n), fixed(n - 1))
            base, per = st.n, st.n - start_of
            with pool.Fori(0, (B - PEEL) // 2) as i:
                st.turn(base, i, 2 * per)
                _, prev, one, two = around(i)
                turn(one, prev)
                turn(two, one)
            st.base, st.n = base + per * (B - PEEL), 0
            turn(None, fixed(B - 1))
            pool.wait_ge(root_near, 1)
            newton(root[:, :], sumsq[:, :], roott[:, :], root_ready)

            G = nc.gpsimd.tensor_tensor

            def read_S(t, n):
                apart(pool, scan_step, 8 * t + 8)
                q_t = kq[:, 1, :, ds(t, 1)].rearrange("p d o -> p (o d)")
                G(qS[:, n % RING, :, :], S, q_t.unsqueeze(1).to_broadcast([P, HD, HD]), ALU.mult).then_inc(q_read, 1)

            def sum_piece(t, n):
                at = (n + PART) % RING // PART * PART
                k = n % PART
                if k == 0:
                    pool.wait_ge(q_read, t)
                elif k < PART - 1:
                    pool.wait_ge(summed, t - PART)
                else:
                    apart(pool, summed, t - PART)
                if k < 4:
                    x, y = slice(at + 2 * k, at + 2 * k + 2), slice(2 * k, 2 * k + 2)
                    last = G(pairs[:, y], qS[:, x, :, 0:8], qS[:, x, :, 8:16], ALU.add)
                elif k < 6:
                    y = slice(4 * k - 16, 4 * k - 12)
                    last = G(fours[:, y], pairs[:, y, :, 0:4], pairs[:, y, :, 4:8], ALU.add)
                elif k == 6:
                    last = G(eights, fours[:, :, :, 0:2], fours[:, :, :, 2:4], ALU.add)
                else:
                    o = kq[:, 1, :, ds(t - (2 * PART - 1), PART)].rearrange("p m t -> p t m")
                    last = G(o, eights[:, :, :, 0], eights[:, :, :, 1], ALU.add)
                last.then_inc(summed, 1)

            assert T % RING == 1
            for t in range(RING):
                read_S(t, t)
                if t >= PART:
                    sum_piece(t, t)
            with pool.Fori(0, T // RING - 1) as i:
                for n in range(RING):
                    read_S(i * RING + (n + RING), n)
                    sum_piece(i * RING + (n + RING), n)
            read_S(T - 1, 0)
            pool.wait_ge(root_near, 2)
            newton(root[:, :], sumsq[:, :], roott[:, :], root_ready)
            st.link(nc.gpsimd.tensor_copy(x2[:, :, C], token2[:, :]))
            nc.gpsimd.memset(zero_rows, 0.0).then_inc(pool_const, 1)

            def refine(b):
                rows, w = (P, TT) if b < B else (B, 1)
                v = newv[0:rows, 0:w]
                pool.wait_ge(var_ready, 2 * B + 2 + b)
                st.link(nc.gpsimd.tensor_scalar(v, mv[0:rows, b % 2, 0:w, 1], EPS_LN, None, ALU.add))
                pool.wait_ge(near_ready, b + 1)
                newton(rstd[0:rows, b % 2, 0:w], v, newt[0:rows, 0:w], rstd_ready)

            for b in range(B + 4):
                if b < B:
                    pool.wait_ge(oT_loaded[b % 2], 32 * (b // 2 + 1))
                    nc.gpsimd.tensor_copy(oTc[:, :, b], oT[:, b % 2, :, 0]).then_inc(oc_ready, 1)
                if b <= B:
                    refine(b)
                if b >= 3:
                    pool.wait_ge(slot_ready, b - 2)
                    for n in range(TT * (b - 3), min(TT * (b - 2), NTILE)):
                        rows = P if n < NTILE - 1 else B
                        for k in range(TOPK):
                            nc.gpsimd.indirect_dma_start(
                                out=expert_in, out_offset=bass.IndirectOffsetOnAxis(ap=slot[0:rows, k, n:n + 1], axis=0),
                                in_=x2[0:rows, n, :], in_offset=None).then_inc(scattered, 16)
            def results_out(j):
                ge(pool, ys_stored[1 - j.slot], 16 * (j.half + j.slot))
                apart(pool, ys_ready, j.n + 1)
                nc.gpsimd.indirect_dma_start(
                    out=pair_out, out_offset=bass.IndirectOffsetOnAxis(ap=pair_id[:, j.slot:j.slot + 1], axis=0),
                    in_=ys[:, j.slot, :], in_offset=None).then_inc(ys_stored[j.slot], 16)

            results_out(fixed(0))
            results_out(fixed(1))
            with pool.Fori(0, (NT - 2) // 2) as i:
                for j in pair(i)[:2]:
                    results_out(j)

        @block.scalar
        def _(act):
            def near_root(n):
                act.wait_ge(norm_step, n + 1)
                nc.scalar.activation(root[:, :], sumsq[:, :], ACT.Ln).then_inc(act_step, 1)
                act.wait_ge(act_step, n + 2)
                nc.scalar.activation(root[:, :], root[:, :], ACT.Exp, scale=-0.5).then_inc(root_near, 1)

            act.wait_ge(ld_small, N_SMALL)
            act.wait_ge(wm_ready, 1)
            nc.scalar.activation(ew[:, :, :], ew[:, :, :], ACT.Exp).then_inc(ew_ready, 1)
            nc.scalar.mul(neg_bq[:, :], neg_bq[:, :], -1.0).then_inc(act_step, 1)
            act.wait_ge(act_step, 1)
            act.wait_ge(c_ready, 2)
            nc.scalar.copy(x1T[:, :, :, 0], clp).then_inc(x1T_ready, 1)

            def mix_front(b):
                for lt in range(2):
                    act.wait_ge(kvb_ready, 2 * b.n + (lt + 1))
                    ge(act, nd_ready, 2 * b.n - 2)
                    nc.scalar.activation(ekv[:, b.slot, lt, 1, :].rearrange("p (j c) -> p j c", j=CJ),
                                         kvb[:, lt, :, 0:P], ACT.Exp).then_inc(ek_ready, 1)
                act.wait_ge(q_ready, b.n + 1)
                ge(act, y_ready, b.n)
                nc.scalar.activation(eq[:, :, :], qp, ACT.Exp, bias=neg_bq[:, 0:1], scale=-1.0).then_inc(eq_ready, 1)

            def mix_back(b):
                act.wait_ge(tr_ready, b.n + 1)
                nc.scalar.copy(x1T[:, :, ds(b.n, 1), 1:T].rearrange("p j o t -> p j (o t)"), trp
                               ).then_inc(x1T_ready, 1)

            def unit_in(b, n):
                w, m = n // 2, n % 2
                act.wait_ge(qkv_ready, 7 * b.n + (n + 1))
                ge(act, conv_ready, 6 * b.n + (n - 2))
                bank = ps[:, 6 + (b.slot + n) % 2, 0:T]
                nc.scalar.copy(pre[:, n % 3, TAPS - 1:], bank)
                ge(act, act_ready, 6 * b.n + (n - 2))
                nc.scalar.mul(conv[:, n % 3, :], bank, taps[:, w, m, 3:4]).then_inc(taken, 1)

            def unit_out(b, n):
                act.wait_ge(conv_ready, 6 * b.n + (n + 1))
                ge(act, relay[n % 3], 32 * b.n + 16 * (n // 3))
                nc.scalar.activation(act_[:, n % 3, :], conv[:, n % 3, :], ACT.Silu).then_inc(act_ready, 1)

            def beta_out(b):
                act.wait_ge(qkv_ready, 7 * b.n + 7)
                ge(act, brelay[b.slot], 16 * b.half)
                nc.scalar.copy(bet[0:NH, b.slot, :], ps[0:NH, 6 + b.slot, 0:T]).then_inc(taken, 1)

            def turn(b, prev, old):
                if old is not None:
                    for n in range(3):
                        unit_in(old, n)
                if b is not None:
                    mix_front(b)
                if old is not None:
                    for n in range(3):
                        unit_out(old, n)
                    for n in range(3, 6):
                        unit_in(old, n)
                    beta_out(old)
                    for n in range(3, 6):
                        unit_out(old, n)
                if prev is not None:
                    mix_back(prev)

            act.wait_ge(pad_ready, 1)
            turn(fixed(0), None, None)
            turn(fixed(1), fixed(0), None)
            for n in range(2, PEEL):
                turn(fixed(n), fixed(n - 1), fixed(n - 2))
            with act.Fori(0, (B - PEEL) // 2) as i:
                older, prev, one, two = around(i)
                turn(one, prev, older)
                turn(two, one, prev)
            turn(None, fixed(B - 1), fixed(B - 2))
            turn(None, None, fixed(B - 1))
            for n in range(2):
                act.wait_ge(relay[n], 32 * (B - 1) + 16)
            nc.scalar.activation(squares, kq[:, 0, :, :], ACT.Square).then_inc(sq_ready, 1)
            for s in range(2):
                act.wait_ge(brelay[s], 16 * (B // 2))
            nc.scalar.activation(betaL[:, :], betaL[:, :], ACT.Exp, scale=-1.0).then_inc(beta_exp, 1)
            for s in range(3):
                act.wait_ge(relay[s], 16 * 2 * B)
            nc.scalar.activation(squares_q, kq[:, 1, :, :], ACT.Square).then_inc(sq_ready, 1)
            near_root(0)
            act.wait_ge(beta_ready, 1)

            def put_v(t, n):
                ge(act, scan_step, 8 * t - 12 if n >= 2 else 0)
                nc.scalar.activation(prod[:, n % 2, :, HD:HD + 1], vL[:, :, ds(t, 1)], ACT.Copy,
                                     scale=betaL[:, ds(t, 1)]).then_inc(bv_put, 1)

            put_v(0, 0)
            put_v(1, 1)
            with act.Fori(0, (T - 2) // 2) as i:
                for n in (2, 3):
                    put_v(i * 2 + n, n)
            put_v(T - 1, 2)
            early = T - 1 - 2 * PART
            act.wait_ge(summed, early)
            nc.scalar.activation(squares[:, :, 0:early], kq[:, 1, :, 0:early], ACT.Square).then_inc(o_sq, 1)
            act.wait_ge(o_done, 2)
            act.wait_ge(summed, T - 1 - PART)
            nc.scalar.activation(squares[:, :, early:], kq[:, 1, :, early:], ACT.Square).then_inc(o_sq, 1)
            near_root(1)
            def near_rsqrt(b):
                rows, w = (P, TT) if b < B else (B, 1)
                act.wait_ge(var_ready, 2 * B + 2 + b)
                y = rstd[0:rows, b % 2, 0:w]
                nc.scalar.activation(y, mv[0:rows, b % 2, 0:w, 1], ACT.Ln, bias=eps_ln[0:rows, 0:1]
                                     ).then_inc(near_step, 1)
                act.wait_ge(near_step, b + 1)
                nc.scalar.activation(y, y, ACT.Exp, scale=-0.5).then_inc(near_ready, 1)

            near_rsqrt(0)
            for n in range(B + 1):
                if n < B:
                    near_rsqrt(n + 1)
                act.wait_ge(t2_ready, n + 1)
                ge(act, sc_ready, n)
                rows = P if n < B else B
                w = TT if n < B else 1
                nc.scalar.copy(x2T[:, :, 0:w, 0:rows],
                               ps[:, 2 + n % 2, :].rearrange("p (j t r) -> p j t r", j=CJ, t=TT)[:, :, 0:w, 0:rows]
                               ).then_inc(x2T_ready, 1)
            act.wait_ge(gd_ready, 1)
            nc.scalar.activation(gexp[:, :], gexp[:, :], ACT.Exp).then_inc(ge_ready, 1)

            def transposed_in(j):
                act.wait_ge(xst_ready, j.n + 1)
                ge(act, gt_ready, j.n - 1)
                nc.scalar.copy(xsT[:, j.slot, :], ps[:, 4, 0:C]).then_inc(xsT_ready, 1)

            def silu(j):
                act.wait_ge(up_ready, j.n + 1)
                ge(act, hid_ready, j.n)
                nc.scalar.activation(sil, ps[:, j.slot, :], ACT.Silu).then_inc(sil_ready, 1)

            def transposed_hidden(j):
                act.wait_ge(ht_ready, j.n + 1)
                ge(act, y2_ready, j.n - 1)
                nc.scalar.copy(hidT[:, j.slot, :], ps[:, 5, :]).then_inc(hidT_ready, 1)

            def result(j):
                act.wait_ge(y2_ready, j.n + 1)
                ge(act, ys_stored[j.slot], 16 * j.half)
                nc.scalar.copy(ys[:, j.slot, :], ps[:, 6, 0:C]).then_inc(ys_ready, 1)

            def turn(j, last, coming):
                silu(j)
                if last is not None:
                    transposed_hidden(last)
                if coming is not None:
                    transposed_in(coming)
                if last is not None:
                    result(last)

            transposed_in(fixed(0))
            turn(fixed(0), None, fixed(1))
            for n in range(1, 4):
                turn(fixed(n), fixed(n - 1), fixed(n + 1))
            with act.Fori(0, (NT - 8) // 4) as i:
                tiles = six(i)
                for k in range(1, 5):
                    turn(tiles[k], tiles[k - 1], tiles[k + 1])
            for n in range(NT - 4, NT):
                turn(fixed(n), fixed(n - 1), fixed(n + 1) if n < NT - 1 else None)
            transposed_hidden(fixed(NT - 1))
            result(fixed(NT - 1))

        @block.vector
        def _(dve):
            st = Steps(dve, dve_step)
            V = nc.vector

            def variance(src, n, rows=P, s=0):
                for t in range(n):
                    last = st.mark(V.bn_stats(stats[0:rows, 0, t, :], src(t)))
                apart(dve, dve_step, last)
                for t in range(n):
                    last = V.bn_aggr(mv[0:rows, s, t, :], stats[0:rows, 0, t, :])
                    if t < n - 1:
                        st.mark(last)
                last.then_inc(var_ready, 1)

            def normed(number, dst, src, n, rows=P, s=0):
                dve.wait_ge(rstd_ready, number + 1)
                for t in range(n):
                    last = V.tensor_scalar(dst(t), src(t), mv[0:rows, s, t, 0:1], rstd[0:rows, s, t:t + 1],
                                           ALU.subtract, ALU.mult)
                return last

            def layer_norm(number, dst, src, n, rows=P):
                variance(src, n, rows)
                return normed(number, dst, src, n, rows)

            V.memset(pre[:, :, 0:TAPS - 1], 0.0).then_inc(pad_ready, 1)
            dve.wait_ge(ld_small, N_SMALL)
            st.link(V.tensor_copy(wmask[:, :, :], wmask8[:, :, :]))
            V.tensor_tensor(ew[:, :, :], ew[:, :, :], wmask[:, :, :], ALU.mult).then_inc(wm_ready, 1)
            layer_norm(0, lambda t: x1c[0:B, :], lambda t: h[0:B, NTILE - 1, :], 1, B).then_inc(c_ready, 1)

            def keys_values(b):
                for lt in range(2):
                    dve.wait_ge(kv_ready, 2 * b.n + (lt + 1))
                    ge(dve, ekv_ready, 2 * b.n + (lt - 1))
                    V.tensor_tensor(kvb[:, lt, :, :], kvp[lt],
                                    kv_bias[:, :, :, :].rearrange("p w r d -> p (w r d)").unsqueeze(1)
                                    .to_broadcast([P, CJ, 2 * P]), ALU.add).then_inc(kvb_ready, 1)

            def mixed(b):
                dve.wait_ge(eq_ready, b.n + 1)
                ge(dve, h_ready, b.n - 1)
                for j in range(CJ):
                    dve.wait_ge(nd_ready, 2 * b.n + (j + 1))
                    last = st.mark(V.scalar_tensor_tensor(out=den1[:, j, :], in0=eq[:, j, :], scalar=1.0,
                                                          in1=ndp[j][:, 1, :], op0=ALU.add, op1=ALU.mult))
                dve.wait_ge(dve_step, last)
                st.link(V.reciprocal(den1[:, :, :], den1[:, :, :]))
                for j in range(CJ):
                    last = V.tensor_tensor(yT[:, b.slot, j, :], ndp[j][:, 0, :], den1[:, j, :], ALU.mult)
                    if j == 0:
                        st.mark(last)
                last.then_inc(y_ready, 1)

            def first_variance(b):
                dve.wait_ge(h_ready, b.n + 1)
                dve.wait_ge(xb_ready, b.n + 1)
                V.tensor_tensor(hs[:, :, :], outp, xtok[:, b.slot, :, :], ALU.add).then_inc(h_taken, 1)
                dve.wait_ge(h_taken, b.n + 1)
                variance(lambda t: hs[:, t, :], TT)

            def h_tile(b, t):
                return h[:, ds(2 * b.n + t, 1), :].rearrange("p o c -> p (o c)")

            def first_norm(b):
                st.link(normed(2 * b.n + 1, lambda t: hs[:, t, :], lambda t: hs[:, t, :], TT))
                st.link(V.tensor_tensor(hs[:, :, :], hs[:, :, :], lng[:, :].unsqueeze(1).to_broadcast([P, TT, C]),
                                        ALU.mult))
                ht = h[:, ds(2 * b.n, TT), :]
                step = st.mark(V.tensor_tensor(ht, hs[:, :, :], lnb[:, :].unsqueeze(1).to_broadcast([P, TT, C]),
                                               ALU.add))
                apart(dve, dve_step, step)
                variance(lambda t: h_tile(b, t), TT)

            def second_norm(b):
                ge(dve, tr_ready, b.n - 1)
                normed(2 * b.n + 2, lambda t: x1[:, b.slot, t, :], lambda t: h_tile(b, t), TT).then_inc(x1_ready, 1)

            def convolve(b, half):
                units = range(3 * half, 3 * half + 3)
                steps = {}
                for k in (2, 1, 0):
                    for n in units:
                        if k == 2:
                            dve.wait_ge(taken, 7 * b.n + (n + 1))
                        else:
                            dve.wait_ge(dve_step, steps[n])
                        c = conv[:, n % 3, :]
                        last = V.scalar_tensor_tensor(out=c, in0=pre[:, n % 3, k:T + k],
                                                      scalar=taps[:, n // 2, n % 2, k:k + 1],
                                                      in1=c, op0=ALU.mult, op1=ALU.add)
                        if k:
                            steps[n] = st.mark(last)
                        else:
                            last.then_inc(conv_ready, 1)

            def turn(b, prev, old):
                if prev is not None:
                    mixed(prev)
                if b is not None:
                    keys_values(b)
                if prev is not None:
                    first_variance(prev)
                if old is not None:
                    convolve(old, 0)
                if prev is not None:
                    first_norm(prev)
                if old is not None:
                    convolve(old, 1)
                if prev is not None:
                    second_norm(prev)

            turn(fixed(0), None, None)
            turn(fixed(1), fixed(0), None)
            dve.wait_ge(ld_attn, N_ATTN)
            for n in range(2, PEEL):
                start_of = st.n
                turn(fixed(n), fixed(n - 1), fixed(n - 2))
            base, per = st.n, st.n - start_of
            with dve.Fori(0, (B - PEEL) // 2) as i:
                st.turn(base, i, 2 * per)
                older, prev, one, two = around(i)
                turn(one, prev, older)
                turn(two, one, prev)
            st.base, st.n = base + per * (B - PEEL), 0
            turn(None, fixed(B - 1), fixed(B - 2))
            turn(None, None, fixed(B - 1))

            dve.wait_ge(beta_exp, 1)
            st.link(V.tensor_scalar(betaL[:, :], betaL[:, :], 1.0, None, ALU.add))
            V.reciprocal(betaL[:, :], betaL[:, :]).then_inc(beta_ready, 1)
            dve.wait_ge(beta_ready, 1)
            st.link(V.tensor_scalar(nbeta[:, :], betaL[:, :], -1.0, None, ALU.mult))
            dve.wait_ge(sq_ready, 1)
            V.tensor_reduce(sumsq[:, :], squares.rearrange("p d t -> p t d"), AX, ALU.add).then_inc(sum_ready, 1)
            dve.wait_ge(sum_ready, 1)
            V.tensor_scalar(sumsq[:, :], sumsq[:, :], EPS * EPS, None, ALU.max).then_inc(norm_step, 1)
            dve.wait_ge(sq_ready, 2)
            st.link(V.tensor_reduce(eps_q[:, :], squares_q.rearrange("p d t -> p t d"), AX, ALU.add))
            st.link(V.tensor_scalar(eps_q[:, :], eps_q[:, :], EPS * EPS, EPS * HD, ALU.max, ALU.mult))
            dve.wait_ge(root_ready, 1)
            st.link(V.tensor_tensor(nbeta[:, :], nbeta[:, :], root[:, :], ALU.mult))
            step = st.mark(V.tensor_tensor(nbk, kq[:, 0, :, :], nbeta[:, :].unsqueeze(1).to_broadcast([P, HD, T]),
                                           ALU.mult))
            dve.wait_ge(dve_step, step)
            st.link(V.tensor_tensor(kq[:, 0, :, :], kq[:, 0, :, :], root[:, :].unsqueeze(1).to_broadcast([P, HD, T]),
                                    ALU.mult))
            V.memset(S, 0.0).then_inc(scan_ready, 1)
            dve.wait_ge(scan_ready, 1)

            halves = [slice(0, HD // 2), slice(HD // 2, HD)]
            wide = [P, HD // 2, HD]

            def step(t, n, first=False):
                bk_t = nbk[:, :, ds(t, 1)].rearrange("p d o -> p (o d)")
                k_t = kq[:, 0, :, ds(t, 1)].rearrange("p d o -> p (o d)")
                for i, m in enumerate(halves):
                    if not first:
                        dve.wait_ge(scan_step, 8 * t + (i - 1))
                    V.tensor_tensor(prod[:, n, m, 0:HD], S[:, m, :], bk_t.unsqueeze(1).to_broadcast(wide),
                                    ALU.mult).then_inc(scan_step, 1)
                dve.wait_ge(bv_put, t + 1)
                for i, m in enumerate(halves):
                    dve.wait_ge(scan_step, 8 * t + (i + 1))
                    V.tensor_reduce(u[:, m], prod[:, n, m, :], AX, ALU.add).then_inc(scan_step, 1)
                for i, m in enumerate(halves):
                    dve.wait_ge(scan_step, 8 * t + (i + 3))
                    V.tensor_tensor(outer[:, m, :], u[:, m].unsqueeze(2).to_broadcast(wide),
                                    k_t.unsqueeze(1).to_broadcast(wide), ALU.mult).then_inc(scan_step, 1)
                if not first:
                    dve.wait_ge(q_read, t)
                for i, m in enumerate(halves):
                    dve.wait_ge(scan_step, 8 * t + (i + 5))
                    V.tensor_tensor(S[:, m, :], S[:, m, :], outer[:, m, :], ALU.add).then_inc(scan_step, 1)

            step(0, 0, True)
            with dve.Fori(0, (T - 1) // RING) as i:
                for k in range(RING):
                    step(i * RING + (k + 1), (k + 1) % 2)

            for t, n in ((T - 1 - PART, PART), (T - 1, 1)):
                dve.wait_ge(q_read, t + n)
                last = V.tensor_reduce(kq[:, 1, :, t:t + n].rearrange("p m t -> p t m"),
                                       qS[:, t % RING:t % RING + n, :, :], AX, ALU.add).then_inc(o_done, 1)
            dve.wait_ge(o_sq, 2)
            st.link(V.tensor_reduce(sumsq[:, :], squares.rearrange("p d t -> p t d"), AX, ALU.add))
            V.scalar_tensor_tensor(out=sumsq[:, :], in0=sumsq[:, :], scalar=1.0 / HD, in1=eps_q[:, :],
                                   op0=ALU.mult, op1=ALU.add).then_inc(norm_step, 1)
            dve.wait_ge(root_ready, 2)
            V.tensor_tensor(kq[:, 1, :, :], kq[:, 1, :, :], root[:, :].unsqueeze(1).to_broadcast([P, HD, T]),
                            ALU.mult).then_inc(o_ready, 1)
            V.tensor_scalar(wo[:, :, :], wo[:, :, :], onw[:, 0:1], None, ALU.mult).then_inc(wo_ready, 1)

            def residual(b):
                rows, w = (P, TT) if b < B else (B, 1)
                dve.wait_ge(p_ready, b + 1)
                acc = ps[:, b % 2, :].rearrange("p (t c) -> p t c", t=TT)
                st.link(V.tensor_tensor(h[0:rows, 2 * b:2 * b + w, :], h[0:rows, 2 * b:2 * b + w, :],
                                        acc[0:rows, 0:w, :], ALU.add))
                variance(lambda t: h[0:rows, 2 * b + t, :], w, rows, b % 2)

            def norm(b):
                rows, w = (P, TT) if b < B else (B, 1)
                normed(2 * B + 1 + b, lambda t: x2[0:rows, 2 * b + t, 0:C], lambda t: h[0:rows, 2 * b + t, :], w, rows,
                       b % 2).then_inc(x2_ready, 1)

            def best(b):
                rows, w = (P, TT) if b < B else (B, 1)
                tiles = slice(2 * b, 2 * b + w)
                dve.wait_ge(sc_ready, b + 1)
                V.tensor_copy(scores[0:rows, tiles, :],
                              ps[0:rows, 4 + b % 2, 0:w * E].rearrange("p (t e) -> p t e", t=w)).then_inc(sc_taken, 1)
                dve.wait_ge(sc_taken, b + 1)
                for n in range(2 * b, 2 * b + w):
                    last = st.mark(V.max(top[0:rows, n, :], scores[0:rows, n, :]))
                dve.wait_ge(dve_step, last)
                for n in range(2 * b, 2 * b + w):
                    last = st.mark(V.max_index(topi[0:rows, n, :], top[0:rows, n, :], scores[0:rows, n, :]))
                dve.wait_ge(dve_step, last)
                st.link(V.tensor_copy(topf[0:rows, tiles, :], topi[0:rows, tiles, 0:TOPK]))
                for k in range(TOPK):
                    last = st.mark(V.tensor_tensor(hot[0:rows, k, tiles, :],
                                                   topf[0:rows, tiles, k:k + 1].to_broadcast([rows, w, E]),
                                                   iota_e[0:rows, :].unsqueeze(1).to_broadcast([rows, w, E]),
                                                   ALU.is_equal))
                st.mark(V.tensor_copy(x2[0:rows, tiles, C + 1], topf[0:rows, tiles, 0]))
                if b == B:
                    last = st.mark(V.memset(hots[:, b % 2, 0:w, :], 0.0))
                dve.wait_ge(dve_step, last)
                V.tensor_tensor(hots[0:rows, b % 2, 0:w, :], hot[0:rows, 0, tiles, :], hot[0:rows, 1, tiles, :],
                                ALU.add).then_inc(hot_ready, 1)

            def slots(b):
                rows, w = (P, TT) if b < B else (B, 1)
                tiles = slice(2 * b, 2 * b + w)
                bank = ps[:, 6 + b % 2, 0:(TT + 1) * E].rearrange("p (t e) -> p t e", e=E)
                dve.wait_ge(rank_ready, b + 1)
                V.tensor_tensor(place[:, 0:w, :], bank[:, 0:w, :],
                                tot[:, b, :].unsqueeze(1).to_broadcast([P, w, E]), ALU.add).then_inc(place_ready, 1)
                V.tensor_tensor(tot[:, b + 1, :], tot[:, b, :], bank[:, TT, :], ALU.add).then_inc(place_ready, 1)
                dve.wait_ge(place_ready, 2 * b + 2)
                last = st.mark(V.tensor_tensor(pick[0:rows, :, 0:w, :], hot[0:rows, :, tiles, :],
                                               place[0:rows, 0:w, :].unsqueeze(1).to_broadcast([rows, TOPK, w, E]),
                                               ALU.mult))
                dve.wait_ge(dve_step, last)
                st.link(V.tensor_reduce(slotf[0:rows, :, 0:w], pick[0:rows, :, 0:w, :], AX, ALU.add))
                V.tensor_copy(slot[0:rows, :, tiles], slotf[0:rows, :, 0:w]).then_inc(slot_ready, 1)

            V.memset(top[:, NTILE - 1, :], 0.0)
            dve.wait_ge(pool_const, 9)
            st.link(V.tensor_copy(tot[:, 0, :], region[:, :]))
            dve.wait_ge(o_ready, 1)
            for b in range(B + 4):
                if b <= B:
                    residual(b)
                if 1 <= b <= B + 1:
                    norm(b - 1)
                if 2 <= b <= B + 2:
                    best(b - 2)
                if b >= 3:
                    slots(b - 3)
            last_tot = tot[:, B + 1, :]
            V.tensor_copy(zslot[:, :], last_tot).then_inc(zslot_ready, 1)
            st.link(V.tensor_tensor(count[:, :], last_tot, region[:, :], ALU.subtract))
            st.link(V.tensor_scalar(ntile_f[:, :], count[:, :], 1.0 / P, None, ALU.mult))
            st.link(V.tensor_tensor(full[:, :, :], ntile_f[:, :].unsqueeze(2).to_broadcast([P, E, NT]),
                                    iota_t[:, :].unsqueeze(1).to_broadcast([P, E, NT]), ALU.is_gt))
            st.link(V.tensor_reduce(ntile_f[:, :], full[:, :, :], AX, ALU.add))
            st.link(V.memset(start[:, 0:1], 0.0))
            for e in range(E):
                st.link(V.tensor_tensor(start[:, e + 1:e + 2], start[:, e:e + 1], ntile_f[:, e:e + 1], ALU.add))
            def by_tile(v):
                return v.unsqueeze(1).to_broadcast([P, NT, E])

            tiles = iota_t[:, :].unsqueeze(2).to_broadcast([P, NT, E])
            step = st.mark(V.tensor_tensor(cmp[:, :, :], tiles, by_tile(start[:, 0:E]), ALU.is_ge))
            st.mark(V.tensor_tensor(tile_row[:, :, :], tiles, by_tile(start[:, 0:E]), ALU.subtract))
            dve.wait_ge(dve_step, step)
            st.mark(V.tensor_reduce(etab_f[:, :], cmp[:, :, :], AX, ALU.add))
            st.mark(V.tensor_tensor(sel[:, :, 0:E - 1], cmp[:, :, 0:E - 1], cmp[:, :, 1:E], ALU.subtract))
            st.link(V.tensor_copy(sel[:, :, E - 1], cmp[:, :, E - 1]))
            st.link(V.scalar_tensor_tensor(out=tile_row[:, :, :], in0=tile_row[:, :, :], scalar=float(P),
                                           in1=by_tile(count[:, :]), op0=ALU.mult, op1=ALU.min))
            st.link(V.tensor_tensor(tile_row[:, :, :], tile_row[:, :, :], by_tile(region[:, :]), ALU.add))
            st.link(V.tensor_tensor(tile_row[:, :, :], tile_row[:, :, :], sel[:, :, :], ALU.mult))
            st.mark(V.tensor_reduce(row_f[:, :], tile_row[:, :, :], AX, ALU.add))
            st.link(V.tensor_scalar(etab_f[:, :], etab_f[:, :], -1.0, None, ALU.add))
            st.mark(V.tensor_copy(row_i[:, :], row_f[:, :]))
            V.tensor_copy(etab[:, :], etab_f[:, :]).then_inc(etab_ready, 1)
            V.tensor_tensor(gexp[:, :], top[:, :, 1], top[:, :, 0], ALU.subtract).then_inc(gd_ready, 1)
            dve.wait_ge(ge_ready, 1)
            st.link(V.tensor_scalar(gate[:, 0, :], gexp[:, :], 1.0, None, ALU.add))
            st.link(V.reciprocal(gate[:, 0, :], gate[:, 0, :]))
            st.link(V.tensor_tensor(gate[:, 1, :], gexp[:, :], gate[:, 0, :], ALU.mult))

            def pairs_of(j):
                dve.wait_ge(xs_loaded[j.slot], 16 * j.half + 16)
                V.tensor_tensor(other[:, j.slot:j.slot + 1], xs[:, j.slot, C + 1:C + 2], etab_f[:, ds(j.n, 1)],
                                ALU.not_equal).then_inc(other_ready, 1)
                dve.wait_ge(other_ready, j.n + 1)
                ge(dve, ys_stored[j.slot], 16 * j.half)
                V.tensor_tensor(pair_id[:, j.slot:j.slot + 1], other[:, j.slot:j.slot + 1],
                                xs[:, j.slot, C:C + 1], ALU.add).then_inc(pair_ready, 1)

            def gated(j):
                pairs_of(j)
                dve.wait_ge(sil_ready, j.n + 1)
                dve.wait_ge(gt_ready, j.n + 1)
                ge(dve, ht_ready, j.n - 1)
                V.tensor_tensor(hid[:, j.slot, :], sil, ps[:, 2 + j.slot, :], ALU.mult).then_inc(hid_ready, 1)

            gated(fixed(0))
            gated(fixed(1))
            with dve.Fori(0, (NT - 2) // 2) as i:
                for j in pair(i)[:2]:
                    gated(j)
            for b in range(B + 1):
                rows, w = (P, TT) if b < B else (B, 1)
                dve.wait_ge(got_loaded[b], 16)
                for n in range(2 * b, 2 * b + w):
                    last = st.mark(V.scalar_tensor_tensor(out=h[0:rows, n, :], in0=got[0:rows, n, 0, :],
                                                          scalar=gate[0:rows, 0, n:n + 1], in1=h[0:rows, n, :],
                                                          op0=ALU.mult, op1=ALU.add))
                dve.wait_ge(dve_step, last)
                for n in range(2 * b, 2 * b + w):
                    last = V.scalar_tensor_tensor(out=h[0:rows, n, :], in0=got[0:rows, n, 1, :],
                                                  scalar=gate[0:rows, 1, n:n + 1], in1=h[0:rows, n, :],
                                                  op0=ALU.mult, op1=ALU.add)
                    if n < 2 * b + w - 1:
                        st.mark(last)
                last.then_inc(fin_ready, 1)

        @block.tensor
        def _(pe):
            mm = nc.tensor.matmul
            pe.wait_ge(pool_const, 9)
            pe.wait_ge(c_ready, 1)
            for j in range(CJ):
                last = nc.tensor.transpose(clp[:, j, :], x1c[0:B, j * P:(j + 1) * P], ident[0:B, 0:B])
            last.then_inc(c_ready, 1)
            pe.wait_ge(ld_small, N_SMALL)

            def front(b):
                pe.wait_ge(x_loaded[b.slot], 32 * b.half + 32)
                for lt in range(2):
                    ge(pe, kvb_ready, 2 * b.n + (lt - 1))
                    for j in range(CJ):
                        last = mm(kvp[lt][:, j, :], xT[:, b.slot, j, lt * P:(lt + 1) * P],
                                  bdkv[:, :, :].rearrange("p w c -> p (w c)"), start=True, stop=True)
                    last.then_inc(kv_ready, 1)
                ge(pe, eq_ready, b.n)
                for j in range(CJ):
                    last = mm(qp[:, j, :], bdq[:, :], xT[:, b.slot, j, :], start=True, stop=True)
                last.then_inc(q_ready, 1)

            def sums(b):
                pe.wait_ge(ekv_ready, 2 * b.n + 2)
                ge(pe, y_ready, b.n)
                for j in range(CJ):
                    for w in range(2):
                        for s in range(2):
                            last = mm(ndp[j][:, w, :], ekv[:, b.slot, s, w, j * P:(j + 1) * P], ew[:, s, :],
                                      start=(s == 0), stop=(s == 1))
                    last.then_inc(nd_ready, 1)

            def project(b):
                pe.wait_ge(y_ready, b.n + 1)
                ge(pe, x1T_ready, b.n + 1)
                for t in range(TT):
                    for j in range(CJ):
                        last = mm(outp[:, t, :], yT[:, b.slot, j, t * P:(t + 1) * P], outw[:, j, :],
                                  start=(j == 0), stop=(j == CJ - 1))
                last.then_inc(h_ready, 1)

            def turn_x1(b):
                pe.wait_ge(x1_ready, b.n + 1)
                for t in range(TT):
                    for j in range(CJ):
                        last = nc.tensor.transpose(trp[:, j, t * P:(t + 1) * P], x1[:, b.slot, t, j * P:(j + 1) * P],
                                                   ident[:, :])
                last.then_inc(tr_ready, 1)

            def proj(b, units):
                rhs = [x1T[:, j, ds(b.n, 1), :].rearrange("p o t -> p (o t)") for j in range(CJ)]
                for n in units:
                    w, m = n // 2, n % 2
                    rows = P if n < 6 else NH
                    wait = ge if n < 6 or isinstance(b.n, int) else apart
                    wait(pe, taken, 7 * b.n + (n - 1))
                    for j in range(CJ):
                        lhsT = wqkv[:, w, j, m * P:(m + 1) * P] if n < 6 else wb[:, j, :]
                        last = mm(ps[0:rows, 6 + (b.slot + n) % 2, 0:T], lhsT, rhs[j],
                                  start=(j == 0), stop=(j == CJ - 1))
                    last.then_inc(qkv_ready, 1)

            def turn(b, prev, old, coming):
                if old is not None:
                    pe.wait_ge(x1T_ready, old.n + 2)
                    proj(old, range(0, 3))
                if prev is not None:
                    project(prev)
                if b is not None:
                    if isinstance(b.n, int) and b.n == 0:
                        pe.wait_ge(ew_ready, 1)
                    sums(b)
                if old is not None:
                    proj(old, range(3, 7))
                if coming is not None:
                    front(coming)
                if prev is not None:
                    turn_x1(prev)

            front(fixed(0))
            turn(fixed(0), None, None, fixed(1))
            turn(fixed(1), fixed(0), None, fixed(2))
            pe.wait_ge(ld_attn, N_ATTN)
            for n in range(2, PEEL):
                turn(fixed(n), fixed(n - 1), fixed(n - 2), fixed(n + 1) if n < PEEL - 1 else None)
            with pe.Fori(0, (B - PEEL) // 2) as i:
                older, prev, one, two = around(i)
                front(one)
                turn(one, prev, older, two)
                turn(two, one, prev, None)
            turn(None, fixed(B - 1), fixed(B - 2), None)
            turn(None, None, fixed(B - 1), None)

            def attn_out(b):
                if b < B:
                    pe.wait_ge(oT_loaded[b % 2], 32 * (b // 2 + 1))
                else:
                    pe.wait_ge(oc_ready, B)
                ge(pe, x2_ready, b - 1)
                rows, w = (P, TT) if b < B else (B, 1)
                for t in range(w):
                    for m in range(CJ):
                        lhsT = oT[:, b % 2, m, 1 + t * P:1 + (t + 1) * P] if b < B else oTc[:, m, :]
                        last = mm(ps[0:rows, b % 2, t * C:(t + 1) * C], lhsT, wo[:, m, :],
                                  start=(m == 0), stop=(m == CJ - 1))
                last.then_inc(p_ready, 1)

            def score(b):
                rows, w = (P, TT) if b < B else (B, 1)
                pe.wait_ge(x2_ready, b + 1)
                ge(pe, x2T_ready, b - 1)
                for t in range(w):
                    for j in range(CJ):
                        last = nc.tensor.transpose(
                            ps[:, 2 + b % 2, :].rearrange("p (j t r) -> p j t r", j=CJ, t=TT)[:, j, t, 0:rows],
                            x2[0:rows, 2 * b + t, j * P:(j + 1) * P], ident[0:rows, 0:rows])
                last.then_inc(t2_ready, 1)
                pe.wait_ge(x2T_ready, b + 1)
                ge(pe, sc_taken, b - 1)
                for t in range(w):
                    for j in range(CJ):
                        last = mm(ps[0:rows, 4 + b % 2, t * E:(t + 1) * E], x2T[:, j, t, 0:rows], wg[:, j, :],
                                  start=(j == 0), stop=(j == CJ - 1))
                last.then_inc(sc_ready, 1)

            def ranks(b):
                w = TT if b < B else 1
                pe.wait_ge(hot_ready, b + 1)
                ge(pe, place_ready, 2 * b - 2)
                bank = ps[:, 6 + b % 2, 0:(TT + 1) * E].rearrange("p (t e) -> p t e", e=E)
                for t in range(w):
                    for m in range(t):
                        mm(bank[:, t, :], ones16[:, :], hots[:, b % 2, m, :], start=(m == 0), stop=False)
                    mm(bank[:, t, :], before16[:, :], hots[:, b % 2, t, :], start=(t == 0), stop=True)
                for t in range(w):
                    last = mm(bank[:, TT, :], ones16[:, :], hots[:, b % 2, t, :], start=(t == 0), stop=(t == w - 1))
                last.then_inc(rank_ready, 1)

            pe.wait_ge(wo_ready, 1)
            attn_out(0)
            for b in range(B + 3):
                if b < B:
                    attn_out(b + 1)
                if 1 <= b <= B + 1:
                    score(b - 1)
                if b >= 2:
                    ranks(b - 2)

            pe.wait_ge(etab_ready, 1)
            pe.wait_ge(ld_ffn, N_FFN)
            pe.wait_ge(ld_down, 16 * E)

            def expert(n):
                return pe.value_load(etab[0:1, ds(n, 1)], min_val=0, max_val=E - 1)

            def rows_in(j):
                pe.wait_ge(xs_loaded[j.slot], 16 * j.half + 16)
                ge(pe, xsT_ready, j.n)
                for c in range(CJ):
                    last = nc.tensor.transpose(ps[:, 4, c * P:(c + 1) * P], xs[:, j.slot, c * P:(c + 1) * P], ident[:, :])
                last.then_inc(xst_ready, 1)

            def up(j, e, w, bank, s, taken):
                ge(pe, taken, j.n - 1)
                for c in range(CJ):
                    last = mm(ps[:, bank + j.slot, :], xsT[:, j.slot, c * P:(c + 1) * P],
                              w[:, ds(e, 1), c, :].rearrange("p o f -> p (o f)"), start=(c == 0), stop=(c == CJ - 1))
                last.then_inc(s, 1)

            def turn_hidden(j):
                pe.wait_ge(hid_ready, j.n + 1)
                ge(pe, hidT_ready, j.n)
                for f in range(FJ):
                    last = nc.tensor.transpose(ps[:, 5, f * P:(f + 1) * P], hid[:, j.slot, f * P:(f + 1) * P], ident[:, :])
                last.then_inc(ht_ready, 1)

            def down(j, e):
                pe.wait_ge(hidT_ready, j.n + 1)
                ge(pe, ys_ready, j.n)
                for f in range(FJ):
                    last = mm(ps[:, 6, 0:C], hidT[:, j.slot, f * P:(f + 1) * P],
                              w3[:, ds(e, 1), f, :].rearrange("p o c -> p (o c)"), start=(f == 0), stop=(f == FJ - 1))
                last.then_inc(y2_ready, 1)

            def ffn(j, e, prev, e_prev, coming):
                pe.wait_ge(xsT_ready, j.n + 1)
                up(j, e, w1, 0, up_ready, sil_ready)
                if prev is not None:
                    if e_prev is None:
                        e_prev = expert(prev.n)
                    turn_hidden(prev)
                up(j, e, w2, 2, gt_ready, hid_ready)
                if coming is not None:
                    rows_in(coming)
                if prev is not None:
                    down(prev, e_prev)

            rows_in(fixed(0))
            e_prev = expert(0)
            ffn(fixed(0), e_prev, None, None, fixed(1))
            for n in range(1, 4):
                e = expert(n)
                ffn(fixed(n), e, fixed(n - 1), e_prev, fixed(n + 1))
                e_prev = e
            with pe.Fori(0, (NT - 8) // 4) as i:
                tiles = six(i)
                e_prev = None
                for k in range(1, 5):
                    e = expert(tiles[k].n)
                    ffn(tiles[k], e, tiles[k - 1], e_prev, tiles[k + 1])
                    e_prev = e
            e_prev = None
            for n in range(NT - 4, NT):
                e = expert(n)
                ffn(fixed(n), e, fixed(n - 1), e_prev, fixed(n + 1) if n < NT - 1 else None)
                e_prev = e
            turn_hidden(fixed(NT - 1))
            down(fixed(NT - 1), e_prev)


def kernel(**inputs):
    import numpy as np
    import concourse.bacc as bacc
    from concourse.bass_utils import run_bass_kernel_spmd

    g = {k: np.asarray(v) for k, v in inputs.items()}
    x = g["x"]
    arrays = [
        ("x_ch", x.transpose(0, 3, 1, 2).reshape(B, C, L)),
        ("x_tok", x.transpose(0, 2, 3, 1).reshape(B, L, C)),
        ("cls_tok", g["cls_tok"].reshape(C)),
        ("tWq", g["L0_tok_Wq_w"].T), ("tWk", g["L0_tok_Wk_w"].T), ("tWv", g["L0_tok_Wv_w"].T),
        ("tbq", g["L0_tok_Wq_b"].reshape(D, 1)), ("tbk", g["L0_tok_Wk_b"]), ("tbv", g["L0_tok_Wv_b"]),
        ("w_bias", g["L0_tok_w_bias"].T), ("mask", g["L0_tok_local_mask"].T),
        ("out_w", g["L0_tok_out_w"]), ("out_b", g["L0_tok_out_b"]),
        ("ln_g", g["L0_tok_ln_g"]), ("ln_b", g["L0_tok_ln_b"]),
        ("aWq", g["L0_attn_Wq"].T), ("aWk", g["L0_attn_Wk"].T), ("aWv", g["L0_attn_Wv"].T),
        ("aWb", g["L0_attn_Wb"].T), ("aWo", g["L0_attn_Wo"].T),
        ("conv_q", g["L0_attn_conv_q"]), ("conv_k", g["L0_attn_conv_k"]), ("conv_v", g["L0_attn_conv_v"]),
        ("o_norm", g["L0_attn_o_norm_w"].reshape(HD, 1)), ("Wg", g["L0_ffn_Wg"].T),
        ("W1", g["L0_ffn_W1"].transpose(0, 2, 1)), ("W2", g["L0_ffn_W2"].transpose(0, 2, 1)),
        ("W3", g["L0_ffn_W3"].transpose(0, 2, 1)),
    ]
    nc = bacc.Bacc("TRN2", target_bir_lowering=False, num_devices=1)
    feed, args = {}, []
    for name, a in arrays:
        a = np.ascontiguousarray(a)
        feed["in_" + name] = a
        args.append(nc.dram_tensor("in_" + name, a.shape, mybir.dt.from_np(a.dtype), kind="ExternalInput").ap())
    out = nc.dram_tensor("out", [B, T, C], F32, kind="ExternalOutput").ap()
    vit_block(nc, *args, out)
    return run_bass_kernel_spmd(nc, [feed], core_ids=[0]).results[0]["out"]
```

```python
from contextlib import ExitStack

import concourse.bass as bass
from concourse import mybir

F32 = mybir.dt.float32
I32 = mybir.dt.int32
U32 = mybir.dt.uint32
BF16 = mybir.dt.bfloat16
U8 = mybir.dt.uint8
ALU = mybir.AluOpType
ACT = mybir.ActivationFunctionType
AX = mybir.AxisListType.X
ds = bass.ds

P = 128
B, F, L, H, D = 8, 64, 256, 4, 64
C = H * F
T = L + 1
NH, HD = 16, C // 16
TAPS = 4
RING = 16
PART = RING // 2
E, FF, TOPK = 8, 512, 2
CJ = C // P
FJ = FF // P
TT = L // P
NTILE = B * TT + 1
PAIRS = B * T * TOPK
NT = (PAIRS + E * (P - 1)) // P
WORK = 5360 + HD * T
ROW = C + 2
REGION = B * T + P
EPS_LN = 1e-5
EPS = 1e-6
SEED = 0x5F3759DF
PEEL = 4
MID = T // 2
REST = 175


class Steps:

    def __init__(self, eng, sem):
        self.eng, self.sem, self.base, self.n = eng, sem, 0, 0

    def mark(self, ins):
        ins.then_inc(self.sem, 1)
        self.n += 1
        return self.base + self.n

    def link(self, ins):
        self.eng.wait_ge(self.sem, self.mark(ins))

    def turn(self, base, i, per):
        self.base, self.n = base + i * per, 0


class Batch:

    def __init__(self, n, half, slot):
        self.n, self.half, self.slot = n, half, slot


def pair(i):
    return Batch(2 * i + 2, i + 1, 0), Batch(2 * i + 3, i + 1, 1), Batch(2 * i + 1, i, 1)


def around(i):
    return [Batch(2 * i + k, i + k // 2, k % 2) for k in range(2, 6)]


def six(i):
    return [Batch(4 * i + k, 2 * i + k // 2, k % 2) for k in range(3, 9)]


def fixed(n):
    return Batch(n, n // 2, n % 2)


def vit_block(nc, x_ch, x_tok, cls_tok, tWq, tWk, tWv, tbq, tbk, tbv, w_bias, mask, out_w, out_b, ln_g, ln_b,
              aWq, aWk, aWv, aWb, aWo, conv_q, conv_k, conv_v, o_norm, Wg, W1, W2, W3, out):
    with ExitStack() as ctx:
        def sb(name, shape, dt=F32):
            return ctx.enter_context(nc.sbuf_tensor(name, shape, dt))

        def sem(name):
            return ctx.enter_context(nc.semaphore(name))

        expert_in = nc.dram_tensor("expert_in", [E * REGION, ROW], F32).ap()
        pair_out = nc.dram_tensor("pair_out", [TOPK * (NTILE * P + 1), C], F32).ap()

        ident = sb("ident", [P, P])
        ones = sb("ones", [P, P])
        before = sb("before", [P, P])
        bdq = sb("bdq", [P, P])
        bdkv = sb("bdkv", [P, 2, P])
        neg_bq = sb("neg_bq", [P, 1])
        kv_bias = sb("kv_bias", [P, 2, 2, D])
        ew = sb("ew", [P, 2, L])
        wmask8 = sb("wmask8", [P, 2, L], U8)
        wmask = sb("wmask", [P, 2, L])
        outw = sb("outw", [P, CJ, C])
        outb = sb("outb", [P, C])
        lng = sb("lng", [P, C])
        lnb = sb("lnb", [P, C])
        wqkv = sb("wqkv", [P, 3, CJ, C])
        wb = sb("wb", [P, CJ, NH])
        wo = sb("wo", [P, CJ, C])
        taps = sb("taps", [P, 3, CJ, TAPS])
        onw = sb("onw", [P, 1])
        wg = sb("wg", [P, CJ, E])
        w1 = sb("w1", [P, E, CJ, FF])
        w2 = sb("w2", [P, E, CJ, FF])
        h = sb("h", [P, NTILE, C])
        big = sb("big", [P, NTILE * ROW])
        x1T = big[:, 0:CJ * B * T].rearrange("p (j b t) -> p j b t", j=CJ, b=B)
        squares = big[:, 0:HD * T].rearrange("p (d t) -> p d t", d=HD)
        nbk = squares
        x2 = big[:, :].rearrange("p (n c) -> p n c", c=ROW)
        kq = sb("kq", [P, 2, HD, T])
        w3 = kq[:, :, :, :].rearrange("p w d t -> p (w d t)")[:, 0:E * FJ * C].rearrange(
            "p (e j c) -> p e j c", e=E, j=FJ)
        betaL = sb("betaL", [P, T])
        nbeta = sb("nbeta", [P, T])
        eps_q = sb("eps_q", [P, T])
        sumsq = sb("sumsq", [P, T])
        root = sb("root", [P, T])
        roott = sb("roott", [P, T])
        work = sb("work", [P, WORK])

        def cut(at, shape):
            n = 1
            for s in shape:
                n *= s
            names = "abcd"[:len(shape)]
            v = work[:, at:at + n]
            if len(shape) == 1:
                return v
            return v.rearrange("p (%s) -> p %s" % (" ".join(names), " ".join(names)),
                               **{k: s for k, s in zip(names, shape)})

        spare = w2[:, :, :, :].rearrange("p e c f -> p (e c f)")

        def lent(at, shape):
            n = 1
            for s in shape:
                n *= s
            names = "abcd"[:len(shape)]
            return spare[:, at:at + n].rearrange("p (%s) -> p %s" % (" ".join(names), " ".join(names)),
                                                 **{k: s for k, s in zip(names, shape)})

        xtok = lent(0, [2, TT, C])
        kvb = lent(1024, [2, CJ, L])
        ekv = lent(2048, [2, 2, 2, C])
        eq = lent(4096, [CJ, L])
        yT = lent(4608, [2, CJ, L])
        den1 = lent(5632, [CJ, L])
        hs = lent(6144, [TT, C])
        x1 = lent(6656, [2, TT, C])
        x1c = lent(7680, [C])
        pre = cut(0, [6, T + TAPS - 1])
        conv = cut(1560, [6, T])
        act_ = [sumsq, eps_q] + [cut(3102 + n * T, [T]) for n in range(4)]
        bet = [root, roott]
        xT = cut(4130, [2, CJ, L])
        squares_q = cut(0, [HD, T])
        vL = cut(WORK - HD * T, [HD, T])
        qS = cut(0, [RING, HD, HD])
        prod = cut(4096, [2, HD, HD + 1])
        outer = cut(4640, [HD, HD])
        S = cut(4896, [HD, HD])
        u = cut(5152, [HD])
        pairs = wqkv[:, 0:2, :, :].rearrange("p w j (m d) -> p (w j m d)", d=HD)[:, 0:PART * HD * 8].rearrange(
            "p (t m d) -> p t m d", t=PART, m=HD)
        fours = wqkv[:, 2, :, :].rearrange("p j c -> p (j c)").rearrange("p (t m d) -> p t m d", t=PART, m=HD)
        eights = outw[:, 0, :].rearrange("p (t m d) -> p t m d", t=PART, m=HD)
        oT = cut(0, [2, CJ, T])
        oTc = cut(1100, [CJ, B])
        x2T = cut(2048, [CJ, TT, P])
        zero_rows = outw[:, :, :].rearrange("p j c -> p (j c)")[:, 0:ROW]
        xs = cut(4096, [2, ROW])
        xsT = cut(4612, [2, C])
        hid = cut(5124, [2, FF])
        sil = cut(6148, [FF])
        hidT = cut(6660, [2, FF])
        ys = cut(7684, [2, C])
        got = cut(0, [NTILE, TOPK, C])
        stats = sb("stats", [P, 2, 2, 6])
        mv = sb("mv", [P, 2, TT, 2])
        rstd = sb("rstd", [P, 2, TT])
        newv = sb("newv", [P, TT])
        newt = sb("newt", [P, TT])
        var_eps = sb("var_eps", [P, 2, TT])
        refined = sb("refined", [P, 2, TT])
        eps_ln = sb("eps_ln", [P, 1])
        cst = sb("cst", [P, 10])
        top = sb("top", [P, NTILE, 8])
        topi = sb("topi", [P, NTILE, 8], U32)
        topf = sb("topf", [P, NTILE, TOPK])
        iota_e = sb("iota_e", [P, E])
        iota_t = sb("iota_t", [P, NT])
        hot = sb("hot", [P, TOPK, NTILE, E])
        hots = sb("hots", [P, 2, TT, E], BF16)
        before16 = sb("before16", [P, P], BF16)
        ones16 = sb("ones16", [P, P], BF16)
        region = sb("region", [P, E])
        token2 = sb("token2", [P, NTILE])
        tot = sb("tot", [P, B + 2, E])
        count = sb("count", [P, E])
        ntile_f = sb("ntile_f", [P, E])
        start = sb("start", [P, E + 1])
        place = sb("place", [P, TT, E])
        pick = sb("pick", [P, TOPK, TT, E])
        slotf = sb("slotf", [P, TOPK, TT])
        slot = sb("slot", [P, TOPK, NTILE], U32)
        zslot = sb("zslot", [P, E], I32)
        gate = sb("gate", [P, TOPK, NTILE])
        gexp = sb("gexp", [P, NTILE])
        cmp = sb("cmp", [P, NT, E])
        full = sb("full", [P, E, NT])
        tile_row = sb("tile_row", [P, NT, E])
        sel = sb("sel", [P, NT, E])
        row_f = sb("row_f", [P, NT])
        row_i = sb("row_i", [P, NT], I32)
        other = sb("other", [P, 2])
        pair_id = sb("pair_id", [P, 2], U32)
        etab_f = sb("etab_f", [P, NT])
        etab = sb("etab", [P, NT], I32)

        ps = ctx.enter_context(nc.psum_tensor("ps", [P, 8, 512], F32))
        kvp = [ps[:, n, :].rearrange("p (j c) -> p j c", j=CJ) for n in range(2)]
        qp = ps[:, 2, :].rearrange("p (j l) -> p j l", j=CJ)
        ndp = [ps[:, 3 + n, :].rearrange("p (w l) -> p w l", w=2) for n in range(2)]
        outp = ps[:, 5, :].rearrange("p (t c) -> p t c", t=TT)
        trp = ps[:, 5, :].rearrange("p (j t) -> p j t", j=CJ)
        clp = ps[:, 7, 0:CJ * B].rearrange("p (j b) -> p j b", j=CJ)

        ld_first = sem("ld_first")
        ld_small = sem("ld_small")
        ld_attn = sem("ld_attn")
        ld_ffn = sem("ld_ffn")
        ld_down = sem("ld_down")
        zslot_ready = sem("zslot_ready")
        zeroed = sem("zeroed")
        near_step = sem("near_step")
        near_ready = sem("near_ready")
        place_ready = sem("place_ready")
        other_ready = sem("other_ready")
        pair_ready = sem("pair_ready")
        x_loaded = [sem(f"x_loaded{s}") for s in range(2)]
        pool_const = sem("pool_const")
        blocks0 = sem("blocks0")
        ew_ready = sem("ew_ready")
        wm_ready = sem("wm_ready")
        xb_ready = sem("xb_ready")
        kv_ready = sem("kv_ready")
        q_ready = sem("q_ready")
        kvb_ready = sem("kvb_ready")
        ek_ready = sem("ek_ready")
        ekv_ready = sem("ekv_ready")
        eq_ready = sem("eq_ready")
        nd_ready = sem("nd_ready")
        y_ready = sem("y_ready")
        h_ready = sem("h_ready")
        h_taken = sem("h_taken")
        x1_ready = sem("x1_ready")
        tr_ready = sem("tr_ready")
        x1T_ready = sem("x1T_ready")
        c_ready = sem("c_ready")
        qkv_ready = sem("qkv_ready")
        taken = sem("taken")
        pad_ready = sem("pad_ready")
        conv_ready = sem("conv_ready")
        act_ready = sem("act_ready")
        relay = [sem(f"relay{n}") for n in range(6)]
        brelay = [sem(f"brelay{s}") for s in range(2)]
        sq_ready = sem("sq_ready")
        norm_step = sem("norm_step")
        sum_ready = sem("sum_ready")
        root_near = sem("root_near")
        root_ready = sem("root_ready")
        var_ready = sem("var_ready")
        rstd_ready = sem("rstd_ready")
        beta_exp = sem("beta_exp")
        beta_ready = sem("beta_ready")
        nbeta_ready = sem("nbeta_ready")
        rest_ready = sem("rest_ready")
        scan_ready = sem("scan_ready")
        scan_step = sem("scan_step")
        bv_put = sem("bv_put")
        q_read = sem("q_read")
        summed = sem("summed")
        o_sq = sem("o_sq")
        o_done = sem("o_done")
        o_ready = sem("o_ready")
        wo_ready = sem("wo_ready")
        oT_loaded = [sem(f"oT_loaded{s}") for s in range(2)]
        oc_ready = sem("oc_ready")
        p_ready = sem("p_ready")
        x2_ready = sem("x2_ready")
        t2_ready = sem("t2_ready")
        x2T_ready = sem("x2T_ready")
        sc_ready = sem("sc_ready")
        sc_taken = sem("sc_taken")
        hot_ready = sem("hot_ready")
        rank_ready = sem("rank_ready")
        gd_ready = sem("gd_ready")
        ge_ready = sem("ge_ready")
        slot_ready = sem("slot_ready")
        etab_ready = sem("etab_ready")
        scattered = sem("scattered")
        xs_loaded = [sem(f"xs_loaded{s}") for s in range(2)]
        xst_ready = sem("xst_ready")
        xsT_ready = sem("xsT_ready")
        up_ready = sem("up_ready")
        gt_ready = sem("gt_ready")
        sil_ready = sem("sil_ready")
        hid_ready = sem("hid_ready")
        ht_ready = sem("ht_ready")
        hidT_ready = sem("hidT_ready")
        y2_ready = sem("y2_ready")
        ys_ready = sem("ys_ready")
        ys_stored = [sem(f"ys_stored{s}") for s in range(2)]
        got_loaded = [sem(f"got_loaded{n}") for n in range(B + 1)]
        share_ready = sem("share_ready")
        half_ready = sem("half_ready")
        fin_ready = [sem(f"fin_ready{s}") for s in range(2)]
        stored = sem("stored")
        dve_step = sem("dve_step")
        act_step = sem("act_step")
        pool_step = sem("pool_step")

        small_loads = [
            (bdq[0:F, 0:D], tWq), (bdq[F:P, D:P], tWq),
            (bdkv[0:F, 0, 0:D], tWk), (bdkv[F:P, 0, D:P], tWk),
            (bdkv[0:F, 1, 0:D], tWv), (bdkv[F:P, 1, D:P], tWv)]
        first_loads = small_loads + [
            (neg_bq[0:D, :], tbq), (neg_bq[D:P, :], tbq),
            (h[0:B, NTILE - 1, :], cls_tok.partition_broadcast(B))]
        for r in range(2):
            first_loads += [(kv_bias[:, 0, r, :], tbk.partition_broadcast(P)),
                            (kv_bias[:, 1, r, :], tbv.partition_broadcast(P))]
        plain_loads = [
            (ew[:, :, :], w_bias.rearrange("(a p) t -> p a t", p=P)),
            (wmask8[:, :, :], mask.rearrange("(a p) t -> p a t", p=P)),
            (outw[:, :, :], out_w.rearrange("(a p) t -> p a t", p=P)),
            (outb[:, :], out_b.partition_broadcast(P)), (lng[:, :], ln_g.partition_broadcast(P)),
            (lnb[:, :], ln_b.partition_broadcast(P))]
        attn_loads = [(wb[:, :, :], aWb.rearrange("(a p) t -> p a t", p=P)),
                      (wo[:, :, :], aWo.rearrange("(a p) t -> p a t", p=P)),
                      (wg[:, :, :], Wg.rearrange("(a p) t -> p a t", p=P))]
        for n, (w, c) in enumerate(((aWk, conv_k), (aWq, conv_q), (aWv, conv_v))):
            attn_loads += [(wqkv[:, n, :, :], w.rearrange("(a p) t -> p a t", p=P)),
                           (taps[:, n, :, :], c.rearrange("(a p) t -> p a t", p=P))]
        for r in range(P // HD):
            attn_loads.append((onw[r * HD:(r + 1) * HD, :], o_norm))
        N_FIRST, N_SMALL, N_ATTN = 16 * len(first_loads), 16 * len(plain_loads), 16 * len(attn_loads)
        ffn_loads = []
        for e in range(E):
            ffn_loads += [(w1[:, e, :, :], W1[e].rearrange("(a p) f -> p a f", p=P)),
                          (w2[:, e, :, :], W2[e].rearrange("(a p) f -> p a f", p=P))]
        N_FFN = 16 * len(ffn_loads)

        def ge(eng, s, v):
            if not (isinstance(v, int) and v <= 0):
                eng.wait_ge(s, v)

        def apart(eng, s, v):
            if not isinstance(v, int):
                v = eng.to_reg(v)
                eng.wait_ge(ld_small, N_SMALL)
            eng.wait_ge(s, v)

        block = ctx.enter_context(nc.Block())

        @block.sync
        def _(sp):
            def load_x(b):
                sp.dma_start(xT[:, b.slot, :, :], x_ch[ds(b.n, 1), :, :].rearrange("o (a p) l -> p (o a) l", p=P)
                             ).then_inc(x_loaded[b.slot], 16)
                sp.dma_start(xtok[:, b.slot, :, :], x_tok[ds(b.n, 1), :, :].rearrange("o (a p) c -> p (o a) c", p=P)
                             ).then_inc(x_loaded[b.slot], 16)

            load_x(fixed(0))
            sp.wait_ge(blocks0, 2)
            for dst, src in first_loads:
                sp.dma_start(dst, src).then_inc(ld_first, 16)
            for dst, src in plain_loads:
                sp.dma_start(dst, src).then_inc(ld_small, 16)
            load_x(fixed(1))
            for dst, src in attn_loads:
                sp.dma_start(dst, src).then_inc(ld_attn, 16)
            def reload_x(b):
                ge(sp, q_ready, b.n - 1)
                ge(sp, h_taken, b.n - 1)
                load_x(b)

            reload_x(fixed(2))
            for b in range(B):
                if b + 3 < B:
                    reload_x(fixed(b + 3))
                for n in range(6):
                    if n == 3:
                        sp.wait_ge(taken, 7 * b + 7)
                        sp.dma_start(betaL[b * NH:(b + 1) * NH, :], bet[b % 2][0:NH, :]).then_inc(brelay[b % 2], 16)
                    w, m = n // 2, n % 2
                    at = b * NH + m * (P // HD)
                    dst = vL[at:at + P // HD, :, :] if w == 2 else kq[at:at + P // HD, w, :, :]
                    sp.wait_ge(act_ready, 6 * b + n + 1)
                    sp.dma_start(dst, act_[n][:, :]).then_inc(relay[n], 16)
            for dst, src in ffn_loads:
                sp.dma_start(dst, src).then_inc(ld_ffn, 16)
            for b in range(B):
                if b == 0:
                    sp.wait_ge(o_ready, 2)
                if b >= 2:
                    sp.wait_ge(p_ready, b - 1)
                    sp.wait_ge(oc_ready, b - 1)
                for m in range(CJ):
                    at = b * NH + m * (P // HD)
                    sp.dma_start(oT[:, b % 2, m, :], kq[at:at + P // HD, 1, :, :]).then_inc(oT_loaded[b % 2], 16)
            for s in range(2):
                sp.wait_ge(oT_loaded[s], 32 * (B // 2))
            for e in range(E):
                sp.dma_start(w3[:, e, :, :], W3[e].rearrange("(a p) c -> p a c", p=P)).then_inc(ld_down, 16)
            sp.wait_ge(pool_const, 10)
            sp.wait_ge(zslot_ready, 1)
            for e in range(E):
                row = sp.value_load(zslot[0:1, e:e + 1], min_val=0, max_val=E * REGION - P)
                sp.dma_start(expert_in[ds(row, P), :], zero_rows).then_inc(zeroed, 16)
            sp.wait_ge(etab_ready, 1)
            sp.wait_ge(zeroed, 16 * E)
            sp.wait_ge(scattered, 16 * TOPK * NTILE)

            def load_tile(j):
                row = sp.value_load(row_i[0:1, ds(j.n, 1)], min_val=0, max_val=E * REGION - P)
                sp.dma_start(xs[:, j.slot, :], expert_in[ds(row, P), :]).then_inc(xs_loaded[j.slot], 16)

            load_tile(fixed(0))
            load_tile(fixed(1))
            with sp.Fori(0, (NT - 2) // 2) as i:
                for j in pair(i)[:2]:
                    sp.wait_ge(xst_ready, j.n - 1)
                    sp.wait_ge(pair_ready, j.n - 1)
                    load_tile(j)
            for s in range(2):
                sp.wait_ge(ys_stored[s], 16 * (NT // 2))
            flat = pair_out[:, :].rearrange("(t k) c -> t (k c)", k=TOPK)
            for b in range(B):
                at = 1 + TT * P * b
                sp.dma_start(got[:, TT * b:TT * (b + 1), :, :].rearrange("p n k c -> p n (k c)"),
                             flat[at:at + TT * P, :].rearrange("(n p) c -> p n c", p=P)).then_inc(got_loaded[b], 16)
            sp.dma_start(got[0:B, NTILE - 1, :, :].rearrange("p k c -> p (k c)"),
                         flat[1 + TT * P * B:1 + TT * P * B + B, :]).then_inc(got_loaded[B], 16)
            for b in range(B + 1):
                sp.wait_ge(fin_ready[b % 2], b // 2 + 1)
                if b < B:
                    sp.dma_start(out[b, 1:T, :].rearrange("(n p) c -> p n c", p=P),
                                 h[:, TT * b:TT * (b + 1), :]).then_inc(stored, 16)
                else:
                    sp.dma_start(out[:, 0, :], h[0:B, NTILE - 1, :]).then_inc(stored, 16)
            sp.wait_ge(stored, 16 * (B + 1))

        @block.gpsimd
        def _(pool):
            st = Steps(pool, pool_step)
            nc.gpsimd.memset(bdq[:, :], 0.0).then_inc(blocks0, 1)
            nc.gpsimd.memset(bdkv[:, :, :], 0.0).then_inc(blocks0, 1)
            nc.gpsimd.memset(eps_ln[:, :], EPS_LN).then_inc(pool_const, 1)
            nc.gpsimd.memset(ones[:, :], 1.0).then_inc(pool_const, 1)
            st.link(nc.gpsimd.memset(ident[:, :], 0.0))
            nc.gpsimd.affine_select(out=ident[:, :], in_=ident[:, :], compare_op=ALU.not_equal, fill=1.0,
                                    base=0, pattern=[[-1, P]], channel_multiplier=1).then_inc(pool_const, 1)
            st.link(nc.gpsimd.memset(before[:, :], 1.0))
            nc.gpsimd.affine_select(out=before[:, :], in_=before[:, :], compare_op=ALU.is_gt, fill=0.0,
                                    base=0, pattern=[[1, P]], channel_multiplier=-1).then_inc(pool_const, 1)
            nc.gpsimd.iota(iota_e[:, :], pattern=[[1, E]], base=0, channel_multiplier=0,
                           allow_small_or_imprecise_dtypes=True).then_inc(pool_const, 1)
            nc.gpsimd.iota(iota_t[:, :], pattern=[[1, NT]], base=0, channel_multiplier=0,
                           allow_small_or_imprecise_dtypes=True).then_inc(pool_const, 1)
            nc.gpsimd.iota(region[:, :], pattern=[[REGION, E]], base=0, channel_multiplier=0,
                           allow_small_or_imprecise_dtypes=True).then_inc(pool_const, 1)
            st.link(nc.gpsimd.iota(token2[:, :], pattern=[[TOPK * P, NTILE]], base=TOPK, channel_multiplier=TOPK,
                                   allow_small_or_imprecise_dtypes=True))
            pool.wait_ge(pool_const, 4)
            nc.gpsimd.tensor_copy(before16[:, :], before[:, :]).then_inc(pool_const, 1)
            nc.gpsimd.tensor_copy(ones16[:, :], ones[:, :]).then_inc(pool_const, 1)
            def newton(y, v, t, ready):
                st.link(nc.gpsimd.tensor_tensor(t, y, y, ALU.mult))
                step = st.mark(nc.gpsimd.tensor_tensor(t, v, t, ALU.mult))
                apart(pool, pool_step, step)
                st.link(nc.gpsimd.tensor_scalar(t, t, -0.5, 1.5, ALU.mult, ALU.add))
                nc.gpsimd.tensor_tensor(y, y, t, ALU.mult).then_inc(ready, 1)

            def rsqrt(number, n=TT, rows=P):
                v, y, t = newv[0:rows, 0:n], rstd[0:rows, 0, 0:n], newt[0:rows, 0:n]
                apart(pool, var_ready, number + 1)
                step = st.mark(nc.gpsimd.tensor_scalar(v, mv[0:rows, 0, 0:n, 1], EPS_LN, None, ALU.add))
                apart(pool, pool_step, step)
                st.link(nc.gpsimd.tensor_scalar(y.bitcast(I32), v.bitcast(I32), -0.5, float(SEED), ALU.mult, ALU.add))
                for k in range(3):
                    st.link(nc.gpsimd.tensor_tensor(t, y, y, ALU.mult))
                    step = st.mark(nc.gpsimd.tensor_tensor(t, v, t, ALU.mult))
                    apart(pool, pool_step, step)
                    st.link(nc.gpsimd.tensor_scalar(t, t, -0.5, 1.5, ALU.mult, ALU.add))
                    last = nc.gpsimd.tensor_tensor(y, y, t, ALU.mult)
                    if k < 2:
                        st.link(last)
                last.then_inc(rstd_ready, 1)

            def mix(b):
                pool.wait_ge(x_loaded[b.slot], 32 * b.half + 32)
                nc.gpsimd.tensor_tensor(xtok[:, b.slot, :, :], xtok[:, b.slot, :, :],
                                        outb[:, :].unsqueeze(1).to_broadcast([P, TT, C]),
                                        ALU.add).then_inc(xb_ready, 1)
                for lt in range(2):
                    pool.wait_ge(ek_ready, 2 * b.n + (lt + 1))
                    nc.gpsimd.tensor_tensor(
                        ekv[:, b.slot, lt, 0, :].rearrange("p (j c) -> p j c", j=CJ),
                        ekv[:, b.slot, lt, 1, :].rearrange("p (j c) -> p j c", j=CJ),
                        kvb[:, lt, :, P:2 * P], ALU.mult).then_inc(ekv_ready, 1)

            def turn(b, prev):
                if b is not None:
                    mix(b)
                if prev is not None:
                    rsqrt(2 * prev.n + 1)
                    rsqrt(2 * prev.n + 2)

            rsqrt(0, 1, B)
            pool.wait_ge(ld_small, N_SMALL)
            turn(fixed(0), None)
            for n in range(1, PEEL):
                start_of = st.n
                turn(fixed(n), fixed(n - 1))
            base, per = st.n, st.n - start_of
            with pool.Fori(0, (B - PEEL) // 2) as i:
                st.turn(base, i, 2 * per)
                _, prev, one, two = around(i)
                turn(one, prev)
                turn(two, one)
            st.base, st.n = base + per * (B - PEEL), 0
            turn(None, fixed(B - 1))
            pool.wait_ge(root_near, 1)
            newton(root[:, :], sumsq[:, :], roott[:, :], root_ready)
            wide = [P, HD, T - REST]
            k_rest = kq[:, 0, :, REST:]
            pool.wait_ge(nbeta_ready, 1)
            nc.gpsimd.tensor_tensor(nbk[:, :, REST:], k_rest, nbeta[:, REST:].unsqueeze(1).to_broadcast(wide),
                                    ALU.mult).then_inc(rest_ready, 1)
            pool.wait_ge(rest_ready, 1)
            nc.gpsimd.tensor_tensor(k_rest, k_rest, root[:, REST:].unsqueeze(1).to_broadcast(wide),
                                    ALU.mult).then_inc(rest_ready, 1)

            G = nc.gpsimd.tensor_tensor

            def read_S(t, n):
                apart(pool, scan_step, 8 * t + 8)
                q_t = kq[:, 1, :, ds(t, 1)].rearrange("p d o -> p (o d)")
                G(qS[:, n % RING, :, :], S, q_t.unsqueeze(1).to_broadcast([P, HD, HD]), ALU.mult).then_inc(q_read, 1)

            def sum_piece(t, n):
                at = (n + PART) % RING // PART * PART
                k = n % PART
                if k == 0:
                    pool.wait_ge(q_read, t)
                elif k < PART - 1:
                    pool.wait_ge(summed, t - PART)
                else:
                    apart(pool, summed, t - PART)
                if k < 4:
                    x, y = slice(at + 2 * k, at + 2 * k + 2), slice(2 * k, 2 * k + 2)
                    last = G(pairs[:, y], qS[:, x, :, 0:8], qS[:, x, :, 8:16], ALU.add)
                elif k < 6:
                    y = slice(4 * k - 16, 4 * k - 12)
                    last = G(fours[:, y], pairs[:, y, :, 0:4], pairs[:, y, :, 4:8], ALU.add)
                elif k == 6:
                    last = G(eights, fours[:, :, :, 0:2], fours[:, :, :, 2:4], ALU.add)
                else:
                    o = kq[:, 1, :, ds(t - (2 * PART - 1), PART)].rearrange("p m t -> p t m")
                    last = G(o, eights[:, :, :, 0], eights[:, :, :, 1], ALU.add)
                last.then_inc(summed, 1)

            assert T % RING == 1
            for t in range(RING):
                read_S(t, t)
                if t >= PART:
                    sum_piece(t, t)
            with pool.Fori(0, T // RING - 1) as i:
                for n in range(RING):
                    read_S(i * RING + (n + RING), n)
                    sum_piece(i * RING + (n + RING), n)
            read_S(T - 1, 0)
            pool.wait_ge(root_near, 2)
            newton(root[:, :], sumsq[:, :], roott[:, :], root_ready)
            pool.wait_ge(root_ready, 2)
            o_rest = kq[:, 1, :, REST:]
            nc.gpsimd.tensor_tensor(o_rest, o_rest, root[:, REST:].unsqueeze(1).to_broadcast(wide),
                                    ALU.mult).then_inc(o_ready, 1)
            st.link(nc.gpsimd.tensor_copy(x2[:, :, C], token2[:, :]))
            nc.gpsimd.memset(zero_rows, 0.0).then_inc(pool_const, 1)

            for b in range(B + 4):
                if b < B:
                    pool.wait_ge(oT_loaded[b % 2], 32 * (b // 2 + 1))
                    nc.gpsimd.tensor_copy(oTc[:, :, b], oT[:, b % 2, :, 0]).then_inc(oc_ready, 1)
                if b >= 3:
                    pool.wait_ge(slot_ready, b - 2)
                    for n in range(TT * (b - 3), min(TT * (b - 2), NTILE)):
                        rows = P if n < NTILE - 1 else B
                        for k in range(TOPK):
                            nc.gpsimd.indirect_dma_start(
                                out=expert_in, out_offset=bass.IndirectOffsetOnAxis(ap=slot[0:rows, k, n:n + 1], axis=0),
                                in_=x2[0:rows, n, :], in_offset=None).then_inc(scattered, 16)
            def results_out(j):
                ge(pool, ys_stored[1 - j.slot], 16 * (j.half + j.slot))
                apart(pool, ys_ready, j.n + 1)
                nc.gpsimd.indirect_dma_start(
                    out=pair_out, out_offset=bass.IndirectOffsetOnAxis(ap=pair_id[:, j.slot:j.slot + 1], axis=0),
                    in_=ys[:, j.slot, :], in_offset=None).then_inc(ys_stored[j.slot], 16)

            results_out(fixed(0))
            results_out(fixed(1))
            with pool.Fori(0, (NT - 2) // 2) as i:
                for j in pair(i)[:2]:
                    results_out(j)

            for b in range(1, B, 2):
                pool.wait_ge(share_ready, b + 1)
                pool.wait_ge(half_ready, 2 * b + 2)
                nc.gpsimd.tensor_tensor(h[:, 2 * b:2 * b + 2, :], h[:, 2 * b:2 * b + 2, :],
                                        got[:, 2 * b:2 * b + 2, 1, :], ALU.add).then_inc(fin_ready[1], 1)

        @block.scalar
        def _(act):
            def near_root(n):
                act.wait_ge(norm_step, n + 1)
                nc.scalar.activation(root[:, :], sumsq[:, :], ACT.Ln).then_inc(act_step, 1)
                act.wait_ge(act_step, n + 2)
                nc.scalar.activation(root[:, :], root[:, :], ACT.Exp, scale=-0.5).then_inc(root_near, 1)

            act.wait_ge(ld_first, N_FIRST)
            nc.scalar.mul(neg_bq[:, :], neg_bq[:, :], -1.0).then_inc(act_step, 1)
            act.wait_ge(act_step, 1)

            def mix_front(b):
                for lt in range(2):
                    act.wait_ge(kvb_ready, 2 * b.n + (lt + 1))
                    ge(act, nd_ready, 2 * b.n - 2)
                    nc.scalar.activation(ekv[:, b.slot, lt, 1, :].rearrange("p (j c) -> p j c", j=CJ),
                                         kvb[:, lt, :, 0:P], ACT.Exp).then_inc(ek_ready, 1)
                act.wait_ge(q_ready, b.n + 1)
                ge(act, y_ready, b.n)
                nc.scalar.activation(eq[:, :, :], qp, ACT.Exp, bias=neg_bq[:, 0:1], scale=-1.0).then_inc(eq_ready, 1)

            def mix_back(b):
                act.wait_ge(tr_ready, b.n + 1)
                nc.scalar.copy(x1T[:, :, ds(b.n, 1), 1:T].rearrange("p j o t -> p j (o t)"), trp
                               ).then_inc(x1T_ready, 1)

            def unit_in(b, n):
                w, m = n // 2, n % 2
                act.wait_ge(qkv_ready, 7 * b.n + (n + 1))
                ge(act, conv_ready, 6 * b.n + (n - 5))
                bank = ps[:, 6 + (b.slot + n) % 2, 0:T]
                nc.scalar.copy(pre[:, n, TAPS - 1:], bank)
                ge(act, act_ready, 6 * b.n + (n - 5))
                nc.scalar.mul(conv[:, n, :], bank, taps[:, w, m, 3:4]).then_inc(taken, 1)

            def unit_out(b, n):
                act.wait_ge(conv_ready, 6 * b.n + (n + 1))
                ge(act, relay[n], 16 * b.n)
                nc.scalar.activation(act_[n][:, :], conv[:, n, :], ACT.Silu).then_inc(act_ready, 1)

            def beta_out(b):
                act.wait_ge(qkv_ready, 7 * b.n + 7)
                ge(act, brelay[b.slot], 16 * b.half)
                nc.scalar.copy(bet[b.slot][0:NH, :], ps[0:NH, 6 + b.slot, 0:T]).then_inc(taken, 1)

            def turn(b, prev, old):
                if old is not None:
                    for n in range(3):
                        unit_in(old, n)
                if b is not None:
                    mix_front(b)
                if old is not None:
                    for n in range(3, 6):
                        unit_in(old, n)
                    beta_out(old)
                    for n in range(6):
                        unit_out(old, n)
                if prev is not None:
                    mix_back(prev)

            act.wait_ge(pad_ready, 1)
            turn(fixed(0), None, None)
            act.wait_ge(wm_ready, 1)
            nc.scalar.activation(ew[:, :, :], ew[:, :, :], ACT.Exp).then_inc(ew_ready, 1)
            act.wait_ge(c_ready, 2)
            nc.scalar.copy(x1T[:, :, :, 0], clp).then_inc(x1T_ready, 1)
            turn(fixed(1), fixed(0), None)
            for n in range(2, PEEL):
                turn(fixed(n), fixed(n - 1), fixed(n - 2))
            with act.Fori(0, (B - PEEL) // 2) as i:
                older, prev, one, two = around(i)
                turn(one, prev, older)
                turn(two, one, prev)
            turn(None, fixed(B - 1), fixed(B - 2))
            turn(None, None, fixed(B - 1))
            for n in range(2):
                act.wait_ge(relay[n], 16 * B)
            nc.scalar.activation(squares[:, :, 0:MID], kq[:, 0, :, 0:MID], ACT.Square).then_inc(sq_ready, 1)
            for s in range(2):
                act.wait_ge(brelay[s], 16 * (B // 2))
            nc.scalar.activation(betaL[:, :], betaL[:, :], ACT.Exp, scale=-1.0).then_inc(beta_exp, 1)
            for n in range(2, 6):
                act.wait_ge(relay[n], 16 * B)
            nc.scalar.activation(squares_q, kq[:, 1, :, :], ACT.Square).then_inc(sq_ready, 1)
            near_root(0)
            act.wait_ge(beta_ready, 1)

            def put_v(t, n):
                ge(act, scan_step, 8 * t - 12 if n >= 2 else 0)
                nc.scalar.activation(prod[:, n % 2, :, HD:HD + 1], vL[:, :, ds(t, 1)], ACT.Copy,
                                     scale=betaL[:, ds(t, 1)]).then_inc(bv_put, 1)

            put_v(0, 0)
            put_v(1, 1)
            with act.Fori(0, (T - 2) // 2) as i:
                for n in (2, 3):
                    put_v(i * 2 + n, n)
            put_v(T - 1, 2)
            early = T - 1 - 2 * PART
            act.wait_ge(summed, early)
            nc.scalar.activation(squares[:, :, 0:early], kq[:, 1, :, 0:early], ACT.Square).then_inc(o_sq, 1)
            act.wait_ge(o_done, 2)
            act.wait_ge(summed, T - 1 - PART)
            nc.scalar.activation(squares[:, :, early:], kq[:, 1, :, early:], ACT.Square).then_inc(o_sq, 1)
            near_root(1)
            def near_rsqrt(b):
                rows, w = (P, TT) if b < B else (B, 1)
                act.wait_ge(var_ready, 2 * B + 2 + b)
                y = rstd[0:rows, b % 2, 0:w]
                nc.scalar.activation(y, mv[0:rows, b % 2, 0:w, 1], ACT.Ln, bias=eps_ln[0:rows, 0:1]
                                     ).then_inc(near_step, 1)
                act.wait_ge(near_step, b + 1)
                nc.scalar.activation(y, y, ACT.Exp, scale=-0.5).then_inc(near_ready, 1)

            near_rsqrt(0)
            for n in range(B + 1):
                if n < B:
                    near_rsqrt(n + 1)
                act.wait_ge(t2_ready, n + 1)
                ge(act, sc_ready, n)
                rows = P if n < B else B
                w = TT if n < B else 1
                nc.scalar.copy(x2T[:, :, 0:w, 0:rows],
                               ps[:, 2 + n % 2, :].rearrange("p (j t r) -> p j t r", j=CJ, t=TT)[:, :, 0:w, 0:rows]
                               ).then_inc(x2T_ready, 1)
            act.wait_ge(gd_ready, 1)
            nc.scalar.activation(gexp[:, :], gexp[:, :], ACT.Exp).then_inc(ge_ready, 1)

            def transposed_in(j):
                act.wait_ge(xst_ready, j.n + 1)
                ge(act, gt_ready, j.n - 1)
                nc.scalar.copy(xsT[:, j.slot, :], ps[:, 4, 0:C]).then_inc(xsT_ready, 1)

            def silu(j):
                act.wait_ge(up_ready, j.n + 1)
                ge(act, hid_ready, j.n)
                nc.scalar.activation(sil, ps[:, j.slot, :], ACT.Silu).then_inc(sil_ready, 1)

            def transposed_hidden(j):
                act.wait_ge(ht_ready, j.n + 1)
                ge(act, y2_ready, j.n - 1)
                nc.scalar.copy(hidT[:, j.slot, :], ps[:, 5, :]).then_inc(hidT_ready, 1)

            def result(j):
                act.wait_ge(y2_ready, j.n + 1)
                ge(act, ys_stored[j.slot], 16 * j.half)
                nc.scalar.copy(ys[:, j.slot, :], ps[:, 6, 0:C]).then_inc(ys_ready, 1)

            def turn(j, last, coming):
                silu(j)
                if last is not None:
                    transposed_hidden(last)
                if coming is not None:
                    transposed_in(coming)
                if last is not None:
                    result(last)

            transposed_in(fixed(0))
            turn(fixed(0), None, fixed(1))
            for n in range(1, 4):
                turn(fixed(n), fixed(n - 1), fixed(n + 1))
            with act.Fori(0, (NT - 8) // 4) as i:
                tiles = six(i)
                for k in range(1, 5):
                    turn(tiles[k], tiles[k - 1], tiles[k + 1])
            for n in range(NT - 4, NT):
                turn(fixed(n), fixed(n - 1), fixed(n + 1) if n < NT - 1 else None)
            transposed_hidden(fixed(NT - 1))
            result(fixed(NT - 1))
            for b in range(B + 1):
                rows, w = (P, TT) if b < B else (B, 1)
                act.wait_ge(got_loaded[b], 16)
                for n in range(2 * b, 2 * b + w):
                    last = nc.scalar.mul(got[0:rows, n, 1, :], got[0:rows, n, 1, :], gate[0:rows, 1, n:n + 1])
                last.then_inc(share_ready, 1)

        @block.vector
        def _(dve):
            st = Steps(dve, dve_step)
            V = nc.vector

            def variance(src, n, rows=P, s=0):
                for t in range(n):
                    last = st.mark(V.bn_stats(stats[0:rows, 0, t, :], src(t)))
                apart(dve, dve_step, last)
                for t in range(n):
                    last = V.bn_aggr(mv[0:rows, s, t, :], stats[0:rows, 0, t, :])
                    if t < n - 1:
                        st.mark(last)
                last.then_inc(var_ready, 1)

            def normed(number, dst, src, n, rows=P, s=0):
                if number is not None:
                    dve.wait_ge(rstd_ready, number + 1)
                for t in range(n):
                    last = V.tensor_scalar(dst(t), src(t), mv[0:rows, s, t, 0:1], rstd[0:rows, s, t:t + 1],
                                           ALU.subtract, ALU.mult)
                return last

            V.memset(pre[:, :, 0:TAPS - 1], 0.0).then_inc(pad_ready, 1)
            dve.wait_ge(ld_first, N_FIRST)
            variance(lambda t: h[0:B, NTILE - 1, :], 1, B)

            def keys_values(b):
                for lt in range(2):
                    dve.wait_ge(kv_ready, 2 * b.n + (lt + 1))
                    ge(dve, ekv_ready, 2 * b.n + (lt - 1))
                    V.tensor_tensor(kvb[:, lt, :, :], kvp[lt],
                                    kv_bias[:, :, :, :].rearrange("p w r d -> p (w r d)").unsqueeze(1)
                                    .to_broadcast([P, CJ, 2 * P]), ALU.add).then_inc(kvb_ready, 1)

            def mixed(b):
                dve.wait_ge(eq_ready, b.n + 1)
                ge(dve, h_ready, b.n - 1)
                for j in range(CJ):
                    dve.wait_ge(nd_ready, 2 * b.n + (j + 1))
                    last = st.mark(V.scalar_tensor_tensor(out=den1[:, j, :], in0=eq[:, j, :], scalar=1.0,
                                                          in1=ndp[j][:, 1, :], op0=ALU.add, op1=ALU.mult))
                dve.wait_ge(dve_step, last)
                st.link(V.reciprocal(den1[:, :, :], den1[:, :, :]))
                for j in range(CJ):
                    last = V.tensor_tensor(yT[:, b.slot, j, :], ndp[j][:, 0, :], den1[:, j, :], ALU.mult)
                    if j == 0:
                        st.mark(last)
                last.then_inc(y_ready, 1)

            def first_variance(b):
                dve.wait_ge(h_ready, b.n + 1)
                dve.wait_ge(xb_ready, b.n + 1)
                V.tensor_tensor(hs[:, :, :], outp, xtok[:, b.slot, :, :], ALU.add).then_inc(h_taken, 1)
                dve.wait_ge(h_taken, b.n + 1)
                variance(lambda t: hs[:, t, :], TT)
                dve.wait_ge(var_ready, 2 * b.n + 2)
                for t in range(TT):
                    st.mark(V.scalar_tensor_tensor(out=hs[:, t, :], in0=hs[:, t, :], scalar=mv[:, 0, t, 0:1],
                                                   in1=lng[:, :], op0=ALU.subtract, op1=ALU.mult))

            def h_tile(b, t):
                return h[:, ds(2 * b.n + t, 1), :].rearrange("p o c -> p (o c)")

            def first_norm(b):
                scaled = st.base + st.n
                dve.wait_ge(dve_step, scaled)
                dve.wait_ge(rstd_ready, 2 * b.n + 2)
                for t in range(TT):
                    step = st.mark(V.scalar_tensor_tensor(out=h_tile(b, t), in0=hs[:, t, :],
                                                          scalar=rstd[:, 0, t:t + 1], in1=lnb[:, :],
                                                          op0=ALU.mult, op1=ALU.add))
                apart(dve, dve_step, step)
                variance(lambda t: h_tile(b, t), TT)

            def second_norm(b):
                ge(dve, tr_ready, b.n - 1)
                normed(2 * b.n + 2, lambda t: x1[:, b.slot, t, :], lambda t: h_tile(b, t), TT).then_inc(x1_ready, 1)

            def convolve(b, half):
                units = range(3 * half, 3 * half + 3)
                steps = {}
                for k in (2, 1, 0):
                    for n in units:
                        if k == 2:
                            dve.wait_ge(taken, 7 * b.n + (n + 1))
                        else:
                            dve.wait_ge(dve_step, steps[n])
                        c = conv[:, n, :]
                        last = V.scalar_tensor_tensor(out=c, in0=pre[:, n, k:T + k],
                                                      scalar=taps[:, n // 2, n % 2, k:k + 1],
                                                      in1=c, op0=ALU.mult, op1=ALU.add)
                        if k:
                            steps[n] = st.mark(last)
                        else:
                            last.then_inc(conv_ready, 1)

            def turn(b, prev, old):
                if prev is not None:
                    mixed(prev)
                if b is not None:
                    keys_values(b)
                if prev is not None:
                    first_variance(prev)
                if old is not None:
                    convolve(old, 0)
                if prev is not None:
                    first_norm(prev)
                if old is not None:
                    convolve(old, 1)
                if prev is not None:
                    second_norm(prev)

            turn(fixed(0), None, None)
            normed(0, lambda t: x1c[0:B, :], lambda t: h[0:B, NTILE - 1, :], 1, B).then_inc(c_ready, 1)
            dve.wait_ge(ld_small, N_SMALL)
            st.link(V.tensor_copy(wmask[:, :, :], wmask8[:, :, :]))
            V.tensor_tensor(ew[:, :, :], ew[:, :, :], wmask[:, :, :], ALU.mult).then_inc(wm_ready, 1)
            turn(fixed(1), fixed(0), None)
            dve.wait_ge(ld_attn, N_ATTN)
            for n in range(2, PEEL):
                start_of = st.n
                turn(fixed(n), fixed(n - 1), fixed(n - 2))
            base, per = st.n, st.n - start_of
            with dve.Fori(0, (B - PEEL) // 2) as i:
                st.turn(base, i, 2 * per)
                older, prev, one, two = around(i)
                turn(one, prev, older)
                turn(two, one, prev)
            st.base, st.n = base + per * (B - PEEL), 0
            turn(None, fixed(B - 1), fixed(B - 2))
            turn(None, None, fixed(B - 1))

            for n in range(2):
                dve.wait_ge(relay[n], 16 * B)
            st.link(V.tensor_tensor(squares[:, :, MID:], kq[:, 0, :, MID:], kq[:, 0, :, MID:], ALU.mult))
            dve.wait_ge(sq_ready, 1)
            V.tensor_reduce(sumsq[:, :], squares.rearrange("p d t -> p t d"), AX, ALU.add).then_inc(sum_ready, 1)
            dve.wait_ge(sum_ready, 1)
            V.tensor_scalar(sumsq[:, :], sumsq[:, :], EPS * EPS, None, ALU.max).then_inc(norm_step, 1)
            dve.wait_ge(beta_exp, 1)
            st.link(V.tensor_scalar(betaL[:, :], betaL[:, :], 1.0, None, ALU.add))
            V.reciprocal(betaL[:, :], betaL[:, :]).then_inc(beta_ready, 1)
            dve.wait_ge(beta_ready, 1)
            st.link(V.tensor_scalar(nbeta[:, :], betaL[:, :], -1.0, None, ALU.mult))
            dve.wait_ge(sq_ready, 2)
            st.link(V.tensor_reduce(eps_q[:, :], squares_q.rearrange("p d t -> p t d"), AX, ALU.add))
            st.link(V.tensor_scalar(eps_q[:, :], eps_q[:, :], EPS * EPS, EPS * HD, ALU.max, ALU.mult))
            dve.wait_ge(root_ready, 1)
            V.tensor_tensor(nbeta[:, :], nbeta[:, :], root[:, :], ALU.mult).then_inc(nbeta_ready, 1)
            dve.wait_ge(nbeta_ready, 1)
            k_first, wide = kq[:, 0, :, 0:REST], [P, HD, REST]
            st.link(V.tensor_tensor(nbk[:, :, 0:REST], k_first, nbeta[:, 0:REST].unsqueeze(1).to_broadcast(wide),
                                    ALU.mult))
            st.link(V.tensor_tensor(k_first, k_first, root[:, 0:REST].unsqueeze(1).to_broadcast(wide), ALU.mult))
            dve.wait_ge(rest_ready, 2)
            V.memset(S, 0.0).then_inc(scan_ready, 1)
            dve.wait_ge(scan_ready, 1)

            CUT = HD // 2 - 1
            halves = [slice(0, CUT), slice(CUT, HD)]
            wide = [[P, CUT, HD], [P, HD - CUT, HD]]

            def step(t, n, first=False):
                bk_t = nbk[:, :, ds(t, 1)].rearrange("p d o -> p (o d)")
                k_t = kq[:, 0, :, ds(t, 1)].rearrange("p d o -> p (o d)")
                for i, m in enumerate(halves):
                    if not first:
                        dve.wait_ge(scan_step, 8 * t + (i - 1))
                    V.tensor_tensor(prod[:, n, m, 0:HD], S[:, m, :], bk_t.unsqueeze(1).to_broadcast(wide[i]),
                                    ALU.mult).then_inc(scan_step, 1)
                dve.wait_ge(bv_put, t + 1)
                for i, m in enumerate(halves):
                    dve.wait_ge(scan_step, 8 * t + (i + 1))
                    V.tensor_reduce(u[:, m], prod[:, n, m, :], AX, ALU.add).then_inc(scan_step, 1)
                for i, m in enumerate(halves):
                    dve.wait_ge(scan_step, 8 * t + (i + 3))
                    V.tensor_tensor(outer[:, m, :], u[:, m].unsqueeze(2).to_broadcast(wide[i]),
                                    k_t.unsqueeze(1).to_broadcast(wide[i]), ALU.mult).then_inc(scan_step, 1)
                if not first:
                    dve.wait_ge(q_read, t)
                for i, m in enumerate(halves):
                    dve.wait_ge(scan_step, 8 * t + (i + 5))
                    V.tensor_tensor(S[:, m, :], S[:, m, :], outer[:, m, :], ALU.add).then_inc(scan_step, 1)

            step(0, 0, True)
            with dve.Fori(0, (T - 1) // RING) as i:
                for k in range(RING):
                    step(i * RING + (k + 1), (k + 1) % 2)

            for t, n in ((T - 1 - PART, PART), (T - 1, 1)):
                dve.wait_ge(q_read, t + n)
                last = V.tensor_reduce(kq[:, 1, :, t:t + n].rearrange("p m t -> p t m"),
                                       qS[:, t % RING:t % RING + n, :, :], AX, ALU.add).then_inc(o_done, 1)
            dve.wait_ge(o_sq, 2)
            st.link(V.tensor_reduce(sumsq[:, :], squares.rearrange("p d t -> p t d"), AX, ALU.add))
            V.scalar_tensor_tensor(out=sumsq[:, :], in0=sumsq[:, :], scalar=1.0 / HD, in1=eps_q[:, :],
                                   op0=ALU.mult, op1=ALU.add).then_inc(norm_step, 1)
            dve.wait_ge(root_ready, 2)
            V.tensor_tensor(kq[:, 1, :, 0:REST], kq[:, 1, :, 0:REST],
                            root[:, 0:REST].unsqueeze(1).to_broadcast([P, HD, REST]), ALU.mult).then_inc(o_ready, 1)
            V.tensor_scalar(wo[:, :, :], wo[:, :, :], onw[:, 0:1], None, ALU.mult).then_inc(wo_ready, 1)

            def stage(b):
                def of(n):
                    return (P if n < B else B, TT if n < B else 1) if 0 <= n <= B else (0, 0)

                (rows, w), (rows1, w1), (rows2, w2), (rows3, w3) = of(b), of(b - 1), of(b - 2), of(b - 3)
                tiles2, tiles3 = slice(2 * b - 4, 2 * b - 4 + w2), slice(2 * b - 6, 2 * b - 6 + w3)
                if w:
                    dve.wait_ge(p_ready, b + 1)
                    acc = ps[:, b % 2, :].rearrange("p (t c) -> p t c", t=TT)
                    added = st.mark(V.tensor_tensor(h[0:rows, 2 * b:2 * b + w, :], h[0:rows, 2 * b:2 * b + w, :],
                                                    acc[0:rows, 0:w, :], ALU.add))
                if w1:
                    y, v, t2 = (a[0:rows1, (b - 1) % 2, 0:w1] for a in (rstd, var_eps, refined))
                    dve.wait_ge(near_ready, b)
                    step = st.mark(V.tensor_tensor(t2, y, y, ALU.mult))
                if w1:
                    dve.wait_ge(dve_step, step)
                    step = st.mark(V.scalar_tensor_tensor(out=t2, in0=t2, scalar=-0.5, in1=v, op0=ALU.mult,
                                                          op1=ALU.mult))
                if w:
                    dve.wait_ge(dve_step, added)
                    for t in range(w):
                        counted = st.mark(V.bn_stats(stats[0:rows, 0, t, :], h[0:rows, 2 * b + t, :]))
                if w1:
                    dve.wait_ge(dve_step, step)
                    step = st.mark(V.scalar_tensor_tensor(out=y, in0=t2, scalar=1.5, in1=y, op0=ALU.add, op1=ALU.mult))
                if w:
                    dve.wait_ge(dve_step, counted)
                    for t in range(w):
                        last = V.bn_aggr(mv[0:rows, b % 2, t, :], stats[0:rows, 0, t, :])
                        if t < w - 1:
                            st.mark(last)
                    last.then_inc(var_ready, 1)
                if w1:
                    dve.wait_ge(dve_step, step)
                    normed(None, lambda t: x2[0:rows1, 2 * b - 2 + t, 0:C], lambda t: h[0:rows1, 2 * b - 2 + t, :], w1,
                           rows1, (b - 1) % 2).then_inc(x2_ready, 1)
                if w:
                    dve.wait_ge(var_ready, 2 * B + 2 + b)
                    st.mark(V.tensor_scalar(var_eps[0:rows, b % 2, 0:w], mv[0:rows, b % 2, 0:w, 1], EPS_LN, None,
                                            ALU.add))
                if w2:
                    dve.wait_ge(sc_ready, b - 1)
                    score = ps[0:rows2, 4 + b % 2, 0:w2 * E].rearrange("p (t e) -> p t e", t=w2)
                    for t in range(w2):
                        maxed = st.mark(V.max(top[0:rows2, 2 * b - 4 + t, :], score[:, t, :]))
                if w3:
                    bank = ps[:, 6 + (b - 3) % 2, 0:(TT + 1) * E].rearrange("p (t e) -> p t e", e=E)
                    dve.wait_ge(rank_ready, b - 2)
                    V.tensor_tensor(place[:, 0:w3, :], bank[:, 0:w3, :],
                                    tot[:, b - 3, :].unsqueeze(1).to_broadcast([P, w3, E]), ALU.add
                                    ).then_inc(place_ready, 1)
                    V.tensor_tensor(tot[:, b - 2, :], tot[:, b - 3, :], bank[:, TT, :], ALU.add
                                    ).then_inc(place_ready, 1)
                if w2:
                    dve.wait_ge(dve_step, maxed)
                    for t in range(w2):
                        last = V.max_index(topi[0:rows2, 2 * b - 4 + t, :], top[0:rows2, 2 * b - 4 + t, :],
                                           score[:, t, :])
                        if t < w2 - 1:
                            st.mark(last)
                    last.then_inc(sc_taken, 1)
                if w3:
                    dve.wait_ge(place_ready, 2 * b - 4)
                    picked = st.mark(V.tensor_tensor(
                        pick[0:rows3, :, 0:w3, :], hot[0:rows3, :, tiles3, :],
                        place[0:rows3, 0:w3, :].unsqueeze(1).to_broadcast([rows3, TOPK, w3, E]), ALU.mult))
                if w2:
                    dve.wait_ge(sc_taken, b - 1)
                    found = st.mark(V.tensor_copy(topf[0:rows2, tiles2, :], topi[0:rows2, tiles2, 0:TOPK]))
                if w3:
                    dve.wait_ge(dve_step, picked)
                    summed3 = st.mark(V.tensor_reduce(slotf[0:rows3, :, 0:w3], pick[0:rows3, :, 0:w3, :], AX, ALU.add))
                if w2:
                    dve.wait_ge(dve_step, found)
                    for k in range(TOPK):
                        marked = st.mark(V.tensor_tensor(hot[0:rows2, k, tiles2, :],
                                                         topf[0:rows2, tiles2, k:k + 1].to_broadcast([rows2, w2, E]),
                                                         iota_e[0:rows2, :].unsqueeze(1).to_broadcast([rows2, w2, E]),
                                                         ALU.is_equal))
                if w3:
                    dve.wait_ge(dve_step, summed3)
                    V.tensor_copy(slot[0:rows3, :, tiles3], slotf[0:rows3, :, 0:w3]).then_inc(slot_ready, 1)
                if w2:
                    if b - 2 == B:
                        marked = st.mark(V.memset(hots[:, b % 2, 0:w2, :], 0.0))
                    st.mark(V.tensor_copy(x2[0:rows2, tiles2, C + 1], topf[0:rows2, tiles2, 0]))
                    dve.wait_ge(dve_step, marked)
                    V.tensor_tensor(hots[0:rows2, b % 2, 0:w2, :], hot[0:rows2, 0, tiles2, :],
                                    hot[0:rows2, 1, tiles2, :], ALU.add).then_inc(hot_ready, 1)

            V.memset(top[:, NTILE - 1, :], 0.0)
            dve.wait_ge(pool_const, 9)
            st.link(V.tensor_copy(tot[:, 0, :], region[:, :]))
            dve.wait_ge(o_ready, 2)
            for b in range(B + 4):
                stage(b)
            dve.wait_ge(place_ready, 2 * B + 2)
            last_tot = tot[:, B + 1, :]
            V.tensor_copy(zslot[:, :], last_tot).then_inc(zslot_ready, 1)
            st.link(V.tensor_tensor(count[:, :], last_tot, region[:, :], ALU.subtract))
            st.link(V.tensor_scalar(ntile_f[:, :], count[:, :], 1.0 / P, None, ALU.mult))
            st.link(V.tensor_tensor(full[:, :, :], ntile_f[:, :].unsqueeze(2).to_broadcast([P, E, NT]),
                                    iota_t[:, :].unsqueeze(1).to_broadcast([P, E, NT]), ALU.is_gt))
            st.link(V.tensor_reduce(ntile_f[:, :], full[:, :, :], AX, ALU.add))
            st.link(V.memset(start[:, 0:1], 0.0))
            for e in range(E):
                st.link(V.tensor_tensor(start[:, e + 1:e + 2], start[:, e:e + 1], ntile_f[:, e:e + 1], ALU.add))
            def by_tile(v):
                return v.unsqueeze(1).to_broadcast([P, NT, E])

            tiles = iota_t[:, :].unsqueeze(2).to_broadcast([P, NT, E])
            step = st.mark(V.tensor_tensor(cmp[:, :, :], tiles, by_tile(start[:, 0:E]), ALU.is_ge))
            st.mark(V.tensor_tensor(tile_row[:, :, :], tiles, by_tile(start[:, 0:E]), ALU.subtract))
            dve.wait_ge(dve_step, step)
            st.mark(V.tensor_reduce(etab_f[:, :], cmp[:, :, :], AX, ALU.add))
            st.mark(V.tensor_tensor(sel[:, :, 0:E - 1], cmp[:, :, 0:E - 1], cmp[:, :, 1:E], ALU.subtract))
            st.link(V.tensor_copy(sel[:, :, E - 1], cmp[:, :, E - 1]))
            st.link(V.scalar_tensor_tensor(out=tile_row[:, :, :], in0=tile_row[:, :, :], scalar=float(P),
                                           in1=by_tile(count[:, :]), op0=ALU.mult, op1=ALU.min))
            st.link(V.tensor_tensor(tile_row[:, :, :], tile_row[:, :, :], by_tile(region[:, :]), ALU.add))
            st.link(V.tensor_tensor(tile_row[:, :, :], tile_row[:, :, :], sel[:, :, :], ALU.mult))
            st.mark(V.tensor_reduce(row_f[:, :], tile_row[:, :, :], AX, ALU.add))
            st.link(V.tensor_scalar(etab_f[:, :], etab_f[:, :], -1.0, None, ALU.add))
            st.mark(V.tensor_copy(row_i[:, :], row_f[:, :]))
            V.tensor_copy(etab[:, :], etab_f[:, :]).then_inc(etab_ready, 1)
            V.tensor_tensor(gexp[:, :], top[:, :, 1], top[:, :, 0], ALU.subtract).then_inc(gd_ready, 1)
            dve.wait_ge(ge_ready, 1)
            st.link(V.tensor_scalar(gate[:, 0, :], gexp[:, :], 1.0, None, ALU.add))
            st.link(V.reciprocal(gate[:, 0, :], gate[:, 0, :]))
            st.link(V.tensor_tensor(gate[:, 1, :], gexp[:, :], gate[:, 0, :], ALU.mult))

            def pairs_of(j):
                dve.wait_ge(xs_loaded[j.slot], 16 * j.half + 16)
                V.tensor_tensor(other[:, j.slot:j.slot + 1], xs[:, j.slot, C + 1:C + 2], etab_f[:, ds(j.n, 1)],
                                ALU.not_equal).then_inc(other_ready, 1)
                dve.wait_ge(other_ready, j.n + 1)
                ge(dve, ys_stored[j.slot], 16 * j.half)
                V.tensor_tensor(pair_id[:, j.slot:j.slot + 1], other[:, j.slot:j.slot + 1],
                                xs[:, j.slot, C:C + 1], ALU.add).then_inc(pair_ready, 1)

            def gated(j):
                pairs_of(j)
                dve.wait_ge(sil_ready, j.n + 1)
                dve.wait_ge(gt_ready, j.n + 1)
                ge(dve, ht_ready, j.n - 1)
                V.tensor_tensor(hid[:, j.slot, :], sil, ps[:, 2 + j.slot, :], ALU.mult).then_inc(hid_ready, 1)

            gated(fixed(0))
            gated(fixed(1))
            with dve.Fori(0, (NT - 2) // 2) as i:
                for j in pair(i)[:2]:
                    gated(j)
            for b in range(B + 1):
                rows, w = (P, TT) if b < B else (B, 1)
                dve.wait_ge(got_loaded[b], 16)
                for n in range(2 * b, 2 * b + w):
                    last = V.scalar_tensor_tensor(out=h[0:rows, n, :], in0=got[0:rows, n, 0, :],
                                                  scalar=gate[0:rows, 0, n:n + 1], in1=h[0:rows, n, :],
                                                  op0=ALU.mult, op1=ALU.add).then_inc(half_ready, 1)
                if b % 2 == 0:
                    dve.wait_ge(share_ready, b + 1)
                    dve.wait_ge(half_ready, 2 * b + w)
                    V.tensor_tensor(h[0:rows, 2 * b:2 * b + w, :], h[0:rows, 2 * b:2 * b + w, :],
                                    got[0:rows, 2 * b:2 * b + w, 1, :], ALU.add).then_inc(fin_ready[0], 1)

        @block.tensor
        def _(pe):
            mm = nc.tensor.matmul
            pe.wait_ge(pool_const, 9)
            def front(b):
                pe.wait_ge(x_loaded[b.slot], 32 * b.half + 32)
                for lt in range(2):
                    ge(pe, kvb_ready, 2 * b.n + (lt - 1))
                    for j in range(CJ):
                        last = mm(kvp[lt][:, j, :], xT[:, b.slot, j, lt * P:(lt + 1) * P],
                                  bdkv[:, :, :].rearrange("p w c -> p (w c)"), start=True, stop=True)
                    last.then_inc(kv_ready, 1)
                ge(pe, eq_ready, b.n)
                for j in range(CJ):
                    last = mm(qp[:, j, :], bdq[:, :], xT[:, b.slot, j, :], start=True, stop=True)
                last.then_inc(q_ready, 1)

            def sums(b):
                pe.wait_ge(ekv_ready, 2 * b.n + 2)
                ge(pe, y_ready, b.n)
                for j in range(CJ):
                    for w in range(2):
                        for s in range(2):
                            last = mm(ndp[j][:, w, :], ekv[:, b.slot, s, w, j * P:(j + 1) * P], ew[:, s, :],
                                      start=(s == 0), stop=(s == 1))
                    last.then_inc(nd_ready, 1)

            def project(b):
                pe.wait_ge(y_ready, b.n + 1)
                ge(pe, x1T_ready, b.n + 1)
                for t in range(TT):
                    for j in range(CJ):
                        last = mm(outp[:, t, :], yT[:, b.slot, j, t * P:(t + 1) * P], outw[:, j, :],
                                  start=(j == 0), stop=(j == CJ - 1))
                last.then_inc(h_ready, 1)

            def turn_x1(b):
                pe.wait_ge(x1_ready, b.n + 1)
                for t in range(TT):
                    for j in range(CJ):
                        last = nc.tensor.transpose(trp[:, j, t * P:(t + 1) * P], x1[:, b.slot, t, j * P:(j + 1) * P],
                                                   ident[:, :])
                last.then_inc(tr_ready, 1)

            def proj(b, units):
                rhs = [x1T[:, j, ds(b.n, 1), :].rearrange("p o t -> p (o t)") for j in range(CJ)]
                for n in units:
                    w, m = n // 2, n % 2
                    rows = P if n < 6 else NH
                    wait = ge if n < 6 or isinstance(b.n, int) else apart
                    wait(pe, taken, 7 * b.n + (n - 1))
                    for j in range(CJ):
                        lhsT = wqkv[:, w, j, m * P:(m + 1) * P] if n < 6 else wb[:, j, :]
                        last = mm(ps[0:rows, 6 + (b.slot + n) % 2, 0:T], lhsT, rhs[j],
                                  start=(j == 0), stop=(j == CJ - 1))
                    last.then_inc(qkv_ready, 1)

            def turn(b, prev, old, coming):
                if old is not None:
                    pe.wait_ge(x1T_ready, old.n + 2)
                    proj(old, range(0, 3))
                if prev is not None:
                    project(prev)
                if b is not None:
                    if isinstance(b.n, int) and b.n == 0:
                        pe.wait_ge(ew_ready, 1)
                    sums(b)
                if old is not None:
                    proj(old, range(3, 7))
                if coming is not None:
                    front(coming)
                if prev is not None:
                    turn_x1(prev)

            pe.wait_ge(ld_first, N_FIRST)
            front(fixed(0))
            pe.wait_ge(c_ready, 1)
            for j in range(CJ):
                last = nc.tensor.transpose(clp[:, j, :], x1c[0:B, j * P:(j + 1) * P], ident[0:B, 0:B])
            last.then_inc(c_ready, 1)
            turn(fixed(0), None, None, fixed(1))
            pe.wait_ge(ld_small, N_SMALL)
            turn(fixed(1), fixed(0), None, fixed(2))
            pe.wait_ge(ld_attn, N_ATTN)
            for n in range(2, PEEL):
                turn(fixed(n), fixed(n - 1), fixed(n - 2), fixed(n + 1) if n < PEEL - 1 else None)
            with pe.Fori(0, (B - PEEL) // 2) as i:
                older, prev, one, two = around(i)
                front(one)
                turn(one, prev, older, two)
                turn(two, one, prev, None)
            turn(None, fixed(B - 1), fixed(B - 2), None)
            turn(None, None, fixed(B - 1), None)

            def attn_out(b):
                if b < B:
                    pe.wait_ge(oT_loaded[b % 2], 32 * (b // 2 + 1))
                else:
                    pe.wait_ge(oc_ready, B)
                ge(pe, x2_ready, b - 1)
                rows, w = (P, TT) if b < B else (B, 1)
                for t in range(w):
                    for m in range(CJ):
                        lhsT = oT[:, b % 2, m, 1 + t * P:1 + (t + 1) * P] if b < B else oTc[:, m, :]
                        last = mm(ps[0:rows, b % 2, t * C:(t + 1) * C], lhsT, wo[:, m, :],
                                  start=(m == 0), stop=(m == CJ - 1))
                last.then_inc(p_ready, 1)

            def score(b):
                rows, w = (P, TT) if b < B else (B, 1)
                pe.wait_ge(x2_ready, b + 1)
                ge(pe, x2T_ready, b - 1)
                for t in range(w):
                    for j in range(CJ):
                        last = nc.tensor.transpose(
                            ps[:, 2 + b % 2, :].rearrange("p (j t r) -> p j t r", j=CJ, t=TT)[:, j, t, 0:rows],
                            x2[0:rows, 2 * b + t, j * P:(j + 1) * P], ident[0:rows, 0:rows])
                last.then_inc(t2_ready, 1)
                pe.wait_ge(x2T_ready, b + 1)
                ge(pe, sc_taken, b - 1)
                for t in range(w):
                    for j in range(CJ):
                        last = mm(ps[0:rows, 4 + b % 2, t * E:(t + 1) * E], x2T[:, j, t, 0:rows], wg[:, j, :],
                                  start=(j == 0), stop=(j == CJ - 1))
                last.then_inc(sc_ready, 1)

            def ranks(b):
                w = TT if b < B else 1
                pe.wait_ge(hot_ready, b + 1)
                ge(pe, place_ready, 2 * b - 2)
                bank = ps[:, 6 + b % 2, 0:(TT + 1) * E].rearrange("p (t e) -> p t e", e=E)
                for t in range(w):
                    for m in range(t):
                        mm(bank[:, t, :], ones16[:, :], hots[:, b % 2, m, :], start=(m == 0), stop=False)
                    mm(bank[:, t, :], before16[:, :], hots[:, b % 2, t, :], start=(t == 0), stop=True)
                for t in range(w):
                    last = mm(bank[:, TT, :], ones16[:, :], hots[:, b % 2, t, :], start=(t == 0), stop=(t == w - 1))
                last.then_inc(rank_ready, 1)

            pe.wait_ge(wo_ready, 1)
            attn_out(0)
            for b in range(B + 3):
                if b < B:
                    attn_out(b + 1)
                if 1 <= b <= B + 1:
                    score(b - 1)
                if b >= 2:
                    ranks(b - 2)

            pe.wait_ge(etab_ready, 1)
            pe.wait_ge(ld_ffn, N_FFN)
            pe.wait_ge(ld_down, 16 * E)

            def expert(n):
                return pe.value_load(etab[0:1, ds(n, 1)], min_val=0, max_val=E - 1)

            def rows_in(j):
                pe.wait_ge(xs_loaded[j.slot], 16 * j.half + 16)
                ge(pe, xsT_ready, j.n)
                for c in range(CJ):
                    last = nc.tensor.transpose(ps[:, 4, c * P:(c + 1) * P], xs[:, j.slot, c * P:(c + 1) * P], ident[:, :])
                last.then_inc(xst_ready, 1)

            def up(j, e, w, bank, s, taken):
                ge(pe, taken, j.n - 1)
                for c in range(CJ):
                    last = mm(ps[:, bank + j.slot, :], xsT[:, j.slot, c * P:(c + 1) * P],
                              w[:, ds(e, 1), c, :].rearrange("p o f -> p (o f)"), start=(c == 0), stop=(c == CJ - 1))
                last.then_inc(s, 1)

            def turn_hidden(j):
                pe.wait_ge(hid_ready, j.n + 1)
                ge(pe, hidT_ready, j.n)
                for f in range(FJ):
                    last = nc.tensor.transpose(ps[:, 5, f * P:(f + 1) * P], hid[:, j.slot, f * P:(f + 1) * P], ident[:, :])
                last.then_inc(ht_ready, 1)

            def down(j, e):
                pe.wait_ge(hidT_ready, j.n + 1)
                ge(pe, ys_ready, j.n)
                for f in range(FJ):
                    last = mm(ps[:, 6, 0:C], hidT[:, j.slot, f * P:(f + 1) * P],
                              w3[:, ds(e, 1), f, :].rearrange("p o c -> p (o c)"), start=(f == 0), stop=(f == FJ - 1))
                last.then_inc(y2_ready, 1)

            def ffn(j, e, prev, e_prev, coming):
                pe.wait_ge(xsT_ready, j.n + 1)
                up(j, e, w1, 0, up_ready, sil_ready)
                if prev is not None:
                    if e_prev is None:
                        e_prev = expert(prev.n)
                    turn_hidden(prev)
                up(j, e, w2, 2, gt_ready, hid_ready)
                if coming is not None:
                    rows_in(coming)
                if prev is not None:
                    down(prev, e_prev)

            rows_in(fixed(0))
            e_prev = expert(0)
            ffn(fixed(0), e_prev, None, None, fixed(1))
            for n in range(1, 4):
                e = expert(n)
                ffn(fixed(n), e, fixed(n - 1), e_prev, fixed(n + 1))
                e_prev = e
            with pe.Fori(0, (NT - 8) // 4) as i:
                tiles = six(i)
                e_prev = None
                for k in range(1, 5):
                    e = expert(tiles[k].n)
                    ffn(tiles[k], e, tiles[k - 1], e_prev, tiles[k + 1])
                    e_prev = e
            e_prev = None
            for n in range(NT - 4, NT):
                e = expert(n)
                ffn(fixed(n), e, fixed(n - 1), e_prev, fixed(n + 1) if n < NT - 1 else None)
                e_prev = e
            turn_hidden(fixed(NT - 1))
            down(fixed(NT - 1), e_prev)


def kernel(**inputs):
    import numpy as np
    import concourse.bacc as bacc
    from concourse.bass_utils import run_bass_kernel_spmd

    g = {k: np.asarray(v) for k, v in inputs.items()}
    x = g["x"]
    arrays = [
        ("x_ch", x.transpose(0, 3, 1, 2).reshape(B, C, L)),
        ("x_tok", x.transpose(0, 2, 3, 1).reshape(B, L, C)),
        ("cls_tok", g["cls_tok"].reshape(C)),
        ("tWq", g["L0_tok_Wq_w"].T), ("tWk", g["L0_tok_Wk_w"].T), ("tWv", g["L0_tok_Wv_w"].T),
        ("tbq", g["L0_tok_Wq_b"].reshape(D, 1)), ("tbk", g["L0_tok_Wk_b"]), ("tbv", g["L0_tok_Wv_b"]),
        ("w_bias", g["L0_tok_w_bias"].T), ("mask", g["L0_tok_local_mask"].T),
        ("out_w", g["L0_tok_out_w"]), ("out_b", g["L0_tok_out_b"]),
        ("ln_g", g["L0_tok_ln_g"]), ("ln_b", g["L0_tok_ln_b"]),
        ("aWq", g["L0_attn_Wq"].T), ("aWk", g["L0_attn_Wk"].T), ("aWv", g["L0_attn_Wv"].T),
        ("aWb", g["L0_attn_Wb"].T), ("aWo", g["L0_attn_Wo"].T),
        ("conv_q", g["L0_attn_conv_q"]), ("conv_k", g["L0_attn_conv_k"]), ("conv_v", g["L0_attn_conv_v"]),
        ("o_norm", g["L0_attn_o_norm_w"].reshape(HD, 1)), ("Wg", g["L0_ffn_Wg"].T),
        ("W1", g["L0_ffn_W1"].transpose(0, 2, 1)), ("W2", g["L0_ffn_W2"].transpose(0, 2, 1)),
        ("W3", g["L0_ffn_W3"].transpose(0, 2, 1)),
    ]
    nc = bacc.Bacc("TRN2", target_bir_lowering=False, num_devices=1)
    feed, args = {}, []
    for name, a in arrays:
        a = np.ascontiguousarray(a)
        feed["in_" + name] = a
        args.append(nc.dram_tensor("in_" + name, a.shape, mybir.dt.from_np(a.dtype), kind="ExternalInput").ap())
    out = nc.dram_tensor("out", [B, T, C], F32, kind="ExternalOutput").ap()
    vit_block(nc, *args, out)
    return run_bass_kernel_spmd(nc, [feed], core_ids=[0]).results[0]["out"]
```
